# Optimizing a Trainium2 kernel written in Bass

```python
import numpy as np
import jax
import jax.numpy as jnp

def _softmax(x, axis=-1):
    return jax.nn.softmax(x, axis=axis)

def _gelu(x):
    return jax.nn.gelu(x, approximate=True)

def _silu(x):
    return jax.nn.silu(x)

def _sigmoid(x):
    return jax.nn.sigmoid(x)

def _layernorm(x, axis=-1, eps=1e-05):
    m = jnp.mean(x, axis=axis, keepdims=True)
    v = jnp.var(x, axis=axis, keepdims=True)
    return (x - m) / jnp.sqrt(v + eps)

def _scatter_add(tgt, idx, src, axis=0):
    return tgt.at[idx].add(src)

def _segment_sum(src, seg, n):
    return jax.ops.segment_sum(src, seg, n)
kernel_name = 'mk_adaln_d2_jaxref_r4_690ad0'

def setup_inputs(seed: int=0):
    np.random.seed(seed)
    _w = jnp.asarray

    def _L0_attn_setup():
        import jax, jax.numpy as jnp
        import numpy as np
        D_MODEL = 256
        NHEAD = 16
        D_K = D_MODEL // NHEAD
        MAX_REL = 256
        key = jax.random.key(seed)
        ks = jax.random.split(key, 6)
        B, S = (4, 512)
        s = 1.0 / np.sqrt(D_MODEL)
        x = jax.random.normal(ks[0], (B, S, D_MODEL), dtype=jnp.float32)
        W_qkv = jax.random.normal(ks[1], (D_MODEL, 3 * D_MODEL), dtype=jnp.float32) * s
        b_qkv = jnp.zeros((3 * D_MODEL,), dtype=jnp.float32)
        W_out = jax.random.normal(ks[2], (D_MODEL, D_MODEL), dtype=jnp.float32) * s
        b_out = jnp.zeros((D_MODEL,), dtype=jnp.float32)
        rel_bias = jax.random.normal(ks[3], (2 * MAX_REL + 1, NHEAD), dtype=jnp.float32) * 0.02
        return {'x': x, 'W_qkv': W_qkv, 'b_qkv': b_qkv, 'W_out': W_out, 'b_out': b_out, 'rel_bias': rel_bias}
    _L0_attn_in = _L0_attn_setup()

    def _L0_ffn_setup():
        import jax, jax.numpy as jnp
        import numpy as np
        S, B, H = (512, 4, 256)
        E = 64
        K = 4
        I = 128
        CAP = 256
        key = jax.random.key(seed)
        k1, k2, k3, k4 = jax.random.split(key, 4)
        return {'hidden_states': jax.random.normal(k1, (S, B, H), dtype=jnp.float32), 'router_w': jax.random.normal(k2, (H, E), dtype=jnp.float32) * 0.02, 'w1': jax.random.normal(k3, (E, H, 2 * I), dtype=jnp.float32) * 0.02, 'w2': jax.random.normal(k4, (E, I, H), dtype=jnp.float32) * 0.02}
    _L0_ffn_in = _L0_ffn_setup()
    _L0_c = _w((lambda *s: np.random.randn(*s).astype(np.float32) * 0.05)(2, 256))
    _L0_wmod = _w((lambda *s: np.random.randn(*s).astype(np.float32) * 0.05)(256, 6 * 256) * 256 ** (-0.5))

    def _L1_attn_setup():
        import jax, jax.numpy as jnp
        import numpy as np
        import math
        HEADS = 16
        SEG = 64
        DIL = 4
        BLOCK_M = 64

        def _hilbert_points(level, x=0, y=0, xi=1, xj=0, yi=0, yj=1):
            if level <= 0:
                yield (x, y)
            else:
                for pt in _hilbert_points(level - 1, x, y, yi // 2, yj // 2, xi // 2, xj // 2):
                    yield pt
                for pt in _hilbert_points(level - 1, x + xi // 2, y + xj // 2, xi // 2, xj // 2, yi // 2, yj // 2):
                    yield pt
                for pt in _hilbert_points(level - 1, x + xi // 2 + yi // 2, y + xj // 2 + yj // 2, xi // 2, xj // 2, yi // 2, yj // 2):
                    yield pt
                for pt in _hilbert_points(level - 1, x + xi // 2 + yi, y + xj // 2 + yj, -yi // 2, -yj // 2, -xi // 2, -xj // 2):
                    yield pt

        def create_hilbert_mapping(seq_len):
            grid = 2 ** int(math.ceil(math.log2(math.sqrt(seq_len))))
            pts = list(_hilbert_points(int(math.log2(grid)), 0, 0, grid, 0, 0, grid))
            m = np.zeros(seq_len, dtype=np.int32)
            for hidx, (x, y) in enumerate(pts[:seq_len]):
                lin = y * grid + x
                if lin < seq_len:
                    m[lin] = hidx
            return jnp.asarray(m)

        def _hilbert_attention(x, Wqkv, bqkv, Wproj, bproj, mapping):
            B, M, dim = x.shape
            H = HEADS
            D = dim // H
            scale = D ** (-0.5)
            qkv = (x @ Wqkv + bqkv).reshape(B, M, 3, H, D)
            qkv = jnp.transpose(qkv, (2, 0, 3, 1, 4))
            q, k, v = (qkv[0], qkv[1], qkv[2])
            nb = M // BLOCK_M
            rm = jnp.arange(M).reshape(nb, BLOCK_M)
            mrm = mapping[rm].astype(jnp.int32)
            seg_idx = mrm // SEG
            offs = jnp.arange(0, SEG, DIL)
            key_pos = seg_idx[:, :, None] * SEG + offs[None, None, :]
            mask_k = key_pos < M
            kp0 = key_pos[:, 0, :]
            mask0 = mask_k[:, 0, :]
            idx0 = jnp.where(mask0, mapping[jnp.clip(kp0, 0, M - 1)], 0)
            Ksel = k[:, :, idx0, :] * mask0[None, None, :, :, None]
            Vsel = v[:, :, idx0, :] * mask0[None, None, :, :, None]
            qm = q[:, :, mrm, :] * scale
            scores = jnp.einsum('bhnmd,bhnsd->bhnms', qm, Ksel)
            scores = jnp.where(mask_k[None, None], scores, -1000000000.0)
            sexp = jnp.exp(scores - jnp.max(scores, axis=3, keepdims=True))
            acc = jnp.einsum('bhnms,bhnsd->bhnmd', sexp, Vsel)
            lsum = 1e-06 + jnp.sum(sexp, axis=-1)
            out = acc / lsum[..., None]
            out = out.reshape(B, H, M, D).transpose(0, 2, 1, 3).reshape(B, M, dim)
            return out @ Wproj + bproj
        key = jax.random.key(seed)
        ks = jax.random.split(key, 5)
        B, M, dim = (2, 1024, 256)
        s = 1.0 / math.sqrt(dim)
        return {'x': jax.random.normal(ks[0], (B, M, dim), jnp.float32), 'Wqkv': jax.random.normal(ks[1], (dim, 3 * dim), jnp.float32) * s, 'bqkv': jax.random.normal(ks[2], (3 * dim,), jnp.float32) * 0.01, 'Wproj': jax.random.normal(ks[3], (dim, dim), jnp.float32) * s, 'bproj': jax.random.normal(ks[4], (dim,), jnp.float32) * 0.01, 'mapping': create_hilbert_mapping(M)}
    _L1_attn_in = _L1_attn_setup()

    def _L1_ffn_setup():
        import jax, jax.numpy as jnp
        import numpy as np
        D = 256
        H = 256
        E = 8
        K = 2
        I = 2 * 256
        ROUTE_SCALE = 1.0
        key = jax.random.key(seed)
        ks = jax.random.split(key, 12)
        s = lambda *sh: 1.0 / np.sqrt(sh[-1])
        return {'x': jax.random.normal(ks[0], (1, 512, D), jnp.float32), 'gate_w': jax.random.normal(ks[1], (E, D), jnp.float32) * s(E, D), 'w1': jax.random.normal(ks[2], (E, H, D), jnp.float32) * s(H, D), 'b1': jax.random.normal(ks[3], (E, H), jnp.float32) * 0.01, 'w2': jax.random.normal(ks[4], (E, D, H), jnp.float32) * s(D, H), 'b2': jax.random.normal(ks[5], (E, D), jnp.float32) * 0.01, 'w3': jax.random.normal(ks[6], (E, H, D), jnp.float32) * s(H, D), 'b3': jax.random.normal(ks[7], (E, H), jnp.float32) * 0.01, 'sw1': jax.random.normal(ks[8], (I, D), jnp.float32) * s(I, D), 'sw2': jax.random.normal(ks[9], (I, D), jnp.float32) * s(I, D), 'sw3': jax.random.normal(ks[10], (D, I), jnp.float32) * s(D, I)}
    _L1_ffn_in = _L1_ffn_setup()
    _L1_c = _w((lambda *s: np.random.randn(*s).astype(np.float32) * 0.05)(2, 256))
    _L1_wmod = _w((lambda *s: np.random.randn(*s).astype(np.float32) * 0.05)(256, 6 * 256) * 256 ** (-0.5))
    _d = {'L0_attn_x': _L0_attn_in['x'], 'L0_attn_W_qkv': _L0_attn_in['W_qkv'], 'L0_attn_b_qkv': _L0_attn_in['b_qkv'], 'L0_attn_W_out': _L0_attn_in['W_out'], 'L0_attn_b_out': _L0_attn_in['b_out'], 'L0_attn_rel_bias': _L0_attn_in['rel_bias'], 'L0_ffn_router_w': _L0_ffn_in['router_w'], 'L0_ffn_w1': _L0_ffn_in['w1'], 'L0_ffn_w2': _L0_ffn_in['w2'], 'L0_c': _L0_c, 'L0_wmod': _L0_wmod, 'L1_attn_Wqkv': _L1_attn_in['Wqkv'], 'L1_attn_bqkv': _L1_attn_in['bqkv'], 'L1_attn_Wproj': _L1_attn_in['Wproj'], 'L1_attn_bproj': _L1_attn_in['bproj'], 'L1_attn_mapping': _L1_attn_in['mapping'], 'L1_ffn_gate_w': _L1_ffn_in['gate_w'], 'L1_ffn_w1': _L1_ffn_in['w1'], 'L1_ffn_b1': _L1_ffn_in['b1'], 'L1_ffn_w2': _L1_ffn_in['w2'], 'L1_ffn_b2': _L1_ffn_in['b2'], 'L1_ffn_w3': _L1_ffn_in['w3'], 'L1_ffn_b3': _L1_ffn_in['b3'], 'L1_ffn_sw1': _L1_ffn_in['sw1'], 'L1_ffn_sw2': _L1_ffn_in['sw2'], 'L1_ffn_sw3': _L1_ffn_in['sw3'], 'L1_c': _L1_c, 'L1_wmod': _L1_wmod}
    _x0 = _d['L0_attn_x']
    _d['L0_attn_x'] = jax.random.normal(jax.random.fold_in(jax.random.key(seed), 1), (2, 2048, 256), dtype=_x0.dtype)
    del _x0
    return _d

def reference(L0_attn_x, L0_attn_W_qkv, L0_attn_b_qkv, L0_attn_W_out, L0_attn_b_out, L0_attn_rel_bias, L0_ffn_router_w, L0_ffn_w1, L0_ffn_w2, L0_c, L0_wmod, L1_attn_Wqkv, L1_attn_bqkv, L1_attn_Wproj, L1_attn_bproj, L1_attn_mapping, L1_ffn_gate_w, L1_ffn_w1, L1_ffn_b1, L1_ffn_w2, L1_ffn_b2, L1_ffn_w3, L1_ffn_b3, L1_ffn_sw1, L1_ffn_sw2, L1_ffn_sw3, L1_c, L1_wmod):

    def _L0_attn_ref(x, W_qkv, b_qkv, W_out, b_out, rel_bias):
        import jax, jax.numpy as jnp
        import numpy as np
        D_MODEL = 256
        NHEAD = 16
        D_K = D_MODEL // NHEAD
        MAX_REL = 256
        B, S, D = x.shape
        qkv = x @ W_qkv + b_qkv
        qkv = qkv.reshape(B, S, 3, NHEAD, D_K)
        q, k, v = (qkv[:, :, 0], qkv[:, :, 1], qkv[:, :, 2])
        scores = jnp.einsum('bihd,bjhd->bhij', q, k) / jnp.sqrt(jnp.float32(D_K))
        idxs = jnp.arange(S)
        rel = jnp.clip(idxs[:, None] - idxs[None, :] + MAX_REL, 0, 2 * MAX_REL)
        bias = rel_bias[rel]
        scores = scores + jnp.transpose(bias, (2, 0, 1))[None]
        attn = jax.nn.softmax(scores, axis=-1)
        out = jnp.einsum('bhij,bjhd->bihd', attn, v).reshape(B, S, D)
        return out @ W_out + b_out

    def _L0_ffn_ref(hidden_states, router_w, w1, w2):
        import jax, jax.numpy as jnp
        import numpy as np
        S, B, H = (512, 4, 256)
        E = 64
        K = 4
        I = 128
        CAP = 256
        s, b, h = hidden_states.shape
        x = hidden_states.reshape(-1, h)
        T = x.shape[0]
        P = T * K
        logits = x @ router_w
        probs_all = jax.nn.softmax(logits, axis=-1)
        top_p, top_i = jax.lax.top_k(probs_all, K)
        rows = jnp.arange(T)[:, None]
        routing_map = jnp.zeros((T, E), dtype=bool).at[rows, top_i].set(True)
        probs = jnp.zeros((T, E), dtype=x.dtype).at[rows, top_i].set(top_p)
        flat = routing_map.T.reshape(-1)
        order = jnp.argsort((~flat).astype(jnp.int32), stable=True)[:P]
        expert_id = order // T
        token_idx = order % T
        group_sizes = routing_map.sum(axis=0)
        starts = jnp.cumsum(group_sizes) - group_sizes
        pos = jnp.arange(P) - starts[expert_id]
        perm_x = x[token_idx]
        buf = jnp.zeros((E, CAP, h), dtype=x.dtype).at[expert_id, pos].set(perm_x)
        h1 = jnp.einsum('ech,ehf->ecf', buf, w1)
        g = jax.nn.silu(h1[..., :I]) * h1[..., I:]
        y = jnp.einsum('eci,eih->ech', g, w2)
        perm_y = y[expert_id, pos]
        perm_probs = probs.T.reshape(-1)[order]
        out = jnp.zeros((T, h), dtype=x.dtype).at[token_idx].add(perm_y * perm_probs[:, None])
        return out.reshape(s, b, h)

    def _L1_attn_ref(x, Wqkv, bqkv, Wproj, bproj, mapping):
        import jax, jax.numpy as jnp
        import numpy as np
        import math
        HEADS = 16
        SEG = 64
        DIL = 4
        BLOCK_M = 64

        def _hilbert_points(level, x=0, y=0, xi=1, xj=0, yi=0, yj=1):
            if level <= 0:
                yield (x, y)
            else:
                for pt in _hilbert_points(level - 1, x, y, yi // 2, yj // 2, xi // 2, xj // 2):
                    yield pt
                for pt in _hilbert_points(level - 1, x + xi // 2, y + xj // 2, xi // 2, xj // 2, yi // 2, yj // 2):
                    yield pt
                for pt in _hilbert_points(level - 1, x + xi // 2 + yi // 2, y + xj // 2 + yj // 2, xi // 2, xj // 2, yi // 2, yj // 2):
                    yield pt
                for pt in _hilbert_points(level - 1, x + xi // 2 + yi, y + xj // 2 + yj, -yi // 2, -yj // 2, -xi // 2, -xj // 2):
                    yield pt

        def create_hilbert_mapping(seq_len):
            grid = 2 ** int(math.ceil(math.log2(math.sqrt(seq_len))))
            pts = list(_hilbert_points(int(math.log2(grid)), 0, 0, grid, 0, 0, grid))
            m = np.zeros(seq_len, dtype=np.int32)
            for hidx, (x, y) in enumerate(pts[:seq_len]):
                lin = y * grid + x
                if lin < seq_len:
                    m[lin] = hidx
            return jnp.asarray(m)

        def _hilbert_attention(x, Wqkv, bqkv, Wproj, bproj, mapping):
            B, M, dim = x.shape
            H = HEADS
            D = dim // H
            scale = D ** (-0.5)
            qkv = (x @ Wqkv + bqkv).reshape(B, M, 3, H, D)
            qkv = jnp.transpose(qkv, (2, 0, 3, 1, 4))
            q, k, v = (qkv[0], qkv[1], qkv[2])
            nb = M // BLOCK_M
            rm = jnp.arange(M).reshape(nb, BLOCK_M)
            mrm = mapping[rm].astype(jnp.int32)
            seg_idx = mrm // SEG
            offs = jnp.arange(0, SEG, DIL)
            key_pos = seg_idx[:, :, None] * SEG + offs[None, None, :]
            mask_k = key_pos < M
            kp0 = key_pos[:, 0, :]
            mask0 = mask_k[:, 0, :]
            idx0 = jnp.where(mask0, mapping[jnp.clip(kp0, 0, M - 1)], 0)
            Ksel = k[:, :, idx0, :] * mask0[None, None, :, :, None]
            Vsel = v[:, :, idx0, :] * mask0[None, None, :, :, None]
            qm = q[:, :, mrm, :] * scale
            scores = jnp.einsum('bhnmd,bhnsd->bhnms', qm, Ksel)
            scores = jnp.where(mask_k[None, None], scores, -1000000000.0)
            sexp = jnp.exp(scores - jnp.max(scores, axis=3, keepdims=True))
            acc = jnp.einsum('bhnms,bhnsd->bhnmd', sexp, Vsel)
            lsum = 1e-06 + jnp.sum(sexp, axis=-1)
            out = acc / lsum[..., None]
            out = out.reshape(B, H, M, D).transpose(0, 2, 1, 3).reshape(B, M, dim)
            return out @ Wproj + bproj
        return _hilbert_attention(x, Wqkv, bqkv, Wproj, bproj, mapping)

    def _L1_ffn_ref(x, gate_w, w1, b1, w2, b2, w3, b3, sw1, sw2, sw3):
        import jax, jax.numpy as jnp
        import numpy as np
        D = 256
        H = 256
        E = 8
        K = 2
        I = 2 * 256
        ROUTE_SCALE = 1.0
        B, S, _ = x.shape
        xt = x.reshape(-1, D)
        logits = xt @ gate_w.T
        scores = jax.nn.softmax(logits.astype(jnp.float32), axis=-1)
        top_vals, idx = jax.lax.top_k(scores, K)
        weights = jnp.take_along_axis(scores, idx, axis=1).astype(x.dtype) * ROUTE_SCALE
        xs = xt[:, None, :] * weights[:, :, None]
        y = jnp.zeros_like(xt)
        for e in range(E):
            mask = (idx == e).astype(x.dtype)
            h = jax.nn.silu(jnp.einsum('tkd,hd->tkh', xs, w1[e]) + b1[e])
            x2 = jnp.einsum('tkh,dh->tkd', h, w2[e]) + b2[e]
            x3 = jnp.einsum('tkd,hd->tkh', xs, w3[e]) + b3[e]
            y = y + jnp.sum(x2 * x3 * mask[:, :, None], axis=1)
        z = jax.nn.silu(xt @ sw1.T) * (xt @ sw2.T) @ sw3.T
        return (y + z).reshape(B, S, D)
    x = L0_attn_x
    mod = (_silu(L0_c) @ L0_wmod).reshape(L0_c.shape[0], 6, 1, -1)
    sa, ca, ga, sb, cb, gb = (mod[:, 0], mod[:, 1], mod[:, 2], mod[:, 3], mod[:, 4], mod[:, 5])
    ga = (2 * (ga >= 0) - 1) * jnp.maximum(jnp.abs(ga), 0.25)
    gb = (2 * (gb >= 0) - 1) * jnp.maximum(jnp.abs(gb), 0.25)
    h = _layernorm(x, axis=-1) * (1 + ca) + sa
    x = x + ga * _L0_attn_ref(h, L0_attn_W_qkv, L0_attn_b_qkv, L0_attn_W_out, L0_attn_b_out, L0_attn_rel_bias)
    h = _layernorm(x, axis=-1) * (1 + cb) + sb
    x = x + gb * _L0_ffn_ref(h, L0_ffn_router_w, L0_ffn_w1, L0_ffn_w2)
    mod = (_silu(L1_c) @ L1_wmod).reshape(L1_c.shape[0], 6, 1, -1)
    sa, ca, ga, sb, cb, gb = (mod[:, 0], mod[:, 1], mod[:, 2], mod[:, 3], mod[:, 4], mod[:, 5])
    ga = (2 * (ga >= 0) - 1) * jnp.maximum(jnp.abs(ga), 0.25)
    gb = (2 * (gb >= 0) - 1) * jnp.maximum(jnp.abs(gb), 0.25)
    h = _layernorm(x, axis=-1) * (1 + ca) + sa
    x = x + ga * _L1_attn_ref(h, L1_attn_Wqkv, L1_attn_bqkv, L1_attn_Wproj, L1_attn_bproj, L1_attn_mapping)
    h = _layernorm(x, axis=-1) * (1 + cb) + sb
    x = x + gb * _L1_ffn_ref(h, L1_ffn_gate_w, L1_ffn_w1, L1_ffn_b1, L1_ffn_w2, L1_ffn_b2, L1_ffn_w3, L1_ffn_b3, L1_ffn_sw1, L1_ffn_sw2, L1_ffn_sw3)
    return x

_drawn_inputs = setup_inputs


def setup_inputs(seed=0):
    import zlib

    import numpy as np

    out = dict(_drawn_inputs(seed))
    spreads = {'L0_attn_b_qkv': (0.0, 0.319), 'L0_attn_b_out': (0.0, 0.329)}
    factors = {'L0_attn_W_qkv': 3.02,
     'L0_attn_rel_bias': 8.0,
     'L0_ffn_router_w': 8.0,
     'L0_ffn_w1': 8.0,
     'L0_ffn_w2': 8.0,
     'L1_attn_bqkv': 29.365,
     'L1_attn_bproj': 35.885,
     'L1_ffn_b1': 64.0,
     'L1_ffn_b2': 64.0,
     'L1_ffn_b3': 64.0,
     'L1_ffn_gate_w': 3.275,
     'L1_ffn_w1': 3.298,
     'L1_ffn_w2': 3.167,
     'L1_ffn_w3': 3.068}
    for name, (base, spread) in spreads.items():
        noise = np.random.default_rng([zlib.crc32(name.encode()), seed]).standard_normal(out[name].shape)
        drawn = base * np.exp(spread * noise) if base else spread * noise
        out[name] = jnp.asarray(drawn.astype(out[name].dtype))
    for name, factor in factors.items():
        out[name] = (out[name] * factor).astype(out[name].dtype)
    return out
```

```python
import numpy as np
import concourse.bass as bass
from concourse import mybir
from contextlib import ExitStack

F32 = mybir.dt.float32
BF16 = mybir.dt.bfloat16
I32 = mybir.dt.int32
U32 = mybir.dt.uint32
ALU = mybir.AluOpType
ACT = mybir.ActivationFunctionType
AX = mybir.AxisListType.X

P = 128
B, S, D = 2, 2048, 256
NT = B * S // P
TB = S // P
KD = D // P
CH = 512
NC = B * S // CH
CT = CH // P
H, DH = 16, 16
NH = B * H
REL = 256
EPS = 1e-5
SA, CA, GA, SB_, CB, GB = range(6)
ONE = 1


class World:
    pass


def sbuf(nc, ctx, name, shape, dt=F32):
    return ctx.enter_context(nc.sbuf_tensor(name, shape, dt))


def psum(nc, ctx, name, shape, dt=F32):
    return ctx.enter_context(nc.psum_tensor(name, shape, dt))


def semaphore(nc, ctx, name):
    s = ctx.enter_context(nc.semaphore(name))
    nc.gpsimd.sem_inc(s, ONE)
    return s


def gpsimd_dma_semaphore(nc, ctx, name):
    return ctx.enter_context(nc.semaphore(name))


def start(nc, ctx):
    nc.all_engine_barrier()
    return ctx.enter_context(nc.Block())


def linker(engine, sem, first=0):
    count = [first]

    def link(instruction):
        count[0] += 1
        instruction.then_inc(sem, 1)
        engine.wait_ge(sem, ONE + count[0])

    return link


def wait_alone(w, engine, sem, value):
    engine.wait_ge(sem, value)
    engine.sem_inc(w.passed, 1)


def stage_constants(nc, w):
    with ExitStack() as ctx:
        sem = lambda name: semaphore(nc, ctx, name)
        loaded = sem("a_loaded")
        filled = sem("a_filled")
        act_step = sem("a_act_step")
        dve_step = sem("a_dve_step")
        silu_ready = sem("a_silu_ready")
        mod_ready = [sem(f"a_mod_ready{i}") for i in range(2)]
        mod_used = [sem(f"a_mod_used{i}") for i in range(2)]
        col_ready = sem("a_col_ready")
        bias_exp_in = sem("a_bias_exp_in")
        bias_exp = sem("a_bias_exp")
        bias_rows_ready = sem("a_bias_rows_ready")
        bias_stored = sem("a_bias_stored")
        far_loaded = sem("a_far_loaded")
        pool_step = sem("a_pool_step")
        map_ready = sem("a_map_ready")
        map_loaded = sem("a_map_loaded")

        cT = sbuf(nc, ctx, "cT", [P, 2, KD, B])
        ce = sbuf(nc, ctx, "ce", [P, 2, KD, B])
        sc = sbuf(nc, ctx, "sc", [P, 2, KD, B])
        wm = sbuf(nc, ctx, "wm", [P, 2, KD, 6 * D])
        rb = sbuf(nc, ctx, "rb", [H, 2 * REL + 1])
        rbm = sbuf(nc, ctx, "rbm", [H, 1])
        rbd = sbuf(nc, ctx, "rbd", [H, 2 * REL + 1])
        ext = sbuf(nc, ctx, "ext", [H, w.EXT])
        row = sbuf(nc, ctx, "row", [P, D * 2])
        kp = sbuf(nc, ctx, "kp", [P, 6], I32)
        m0 = sbuf(nc, ctx, "m0", [P, 3], I32)
        ps = [psum(nc, ctx, f"a_ps{i}", [P, CH]) for i in range(2)]
        pc = psum(nc, ctx, "a_pc", [P, 2, 12, B])
        block = start(nc, ctx)

        small = [(cT[:, l, :, :], w.c[l].rearrange("(k p) b -> p k b", p=P)) for l in range(2)]
        wmods = [(wm[:, l, :, :], w.wmod[l].rearrange("(k p) n -> p k n", p=P)) for l in range(2)]
        big = wmods + [(rb[:, :], w.rel_biasT)]
        weights = [
            (w.Wqkv0[:, :, :], w.W_qkv0.rearrange("(k p) n -> p k n", p=P)),
            (w.Wout0[:, :, :], w.W_out0.rearrange("(k p) n -> p k n", p=P)),
            (w.Wr0[:, :, :], w.router_w.rearrange("(k p) n -> p k n", p=P)),
            (w.Wg1[:, :, :], w.a['L1_ffn_gate_w'].rearrange("(k p) n -> p k n", p=P)),
            (w.bqk[:, :], w.b_qkv0[0:2 * D].rearrange("(c p) -> p c", p=P)),
            (w.bv0[:, :], w.b_qkv0[2 * D:3 * D].rearrange("(o n) -> o n", o=1).broadcast_to([P, D])),
            (w.bo0[:, :], w.b_out0.rearrange("(o n) -> o n", o=1).broadcast_to([P, D])),
        ]
        MAPS = 6

        @block.sync
        def _(sp):
            for dst, src in small + big + weights:
                sp.dma_start(dst, src, allow_slow_non_contiguous=True).then_inc(loaded, 16)
            sp.wait_ge(bias_rows_ready, ONE + 1)
            for b in range(B):
                sp.dma_start(w.ext_dram[b * H:(b + 1) * H, :], ext[:, :]).then_inc(bias_stored, 16)
            sp.dma_start(w.far_dram[:, 0:1], rbd[:, 0:1], allow_slow_non_contiguous=True).then_inc(bias_stored, 16)
            sp.dma_start(w.far_dram[:, 1:2], rbd[:, 2 * REL:2 * REL + 1], allow_slow_non_contiguous=True).then_inc(bias_stored, 16)
            sp.wait_ge(bias_stored, ONE + 64)
            for b in range(B):
                sp.dma_start(w.far[:, b * H:(b + 1) * H, :], w.far_dram.rearrange("h (o t) -> o h t", o=1).broadcast_to([P, H, 2])).then_inc(far_loaded, 16)
            sp.wait_ge(far_loaded, ONE + 32)

        @block.scalar
        def _(act):
            act.wait_ge(loaded, ONE + 16 * len(small + big + weights))
            act.activation(ce[:, :, :, :], cT[:, :, :, :], ACT.Exp, scale=-1.0).then_inc(act_step, 1)
            act.wait_ge(bias_exp_in, ONE + 1)
            act.activation(ext[:, P - 1:P + 2 * REL], rbd[:, :], ACT.Exp).then_inc(bias_exp, 1)

        @block.tensor
        def _(pe):
            pe.wait_ge(silu_ready, ONE + 1)
            n = 0
            for l in range(2):
                for b in range(B):
                    for j in range(3):
                        if n >= 2:
                            pe.wait_ge(mod_used[n % 2], ONE + n // 2)
                        for k in range(KD):
                            last = pe.matmul(ps[n % 2][:, :], sc[:, l, k, b:b + 1].broadcast_to([P, P]),
                                             wm[:, l, k, j * CH:(j + 1) * CH], start=k == 0, stop=k == KD - 1)
                        last.then_inc(mod_ready[n % 2], 1)
                        n += 1
            for l in range(2):
                for j in range(12):
                    for k in range(KD):
                        last = pe.matmul(pc[:, l, j, :], wm[:, l, k, j * P:(j + 1) * P], sc[:, l, k, :],
                                         start=k == 0, stop=k == KD - 1)
            last.then_inc(col_ready, 1)

        @block.vector
        def _(dve):
            link = linker(dve, dve_step)
            dve.wait_ge(act_step, ONE + 1)
            link(dve.tensor_scalar_add(ce[:, :, :, :], ce[:, :, :, :], 1.0))
            link(dve.reciprocal(ce[:, :, :, :], ce[:, :, :, :]))
            dve.tensor_tensor(sc[:, :, :, :], cT[:, :, :, :], ce[:, :, :, :], ALU.mult).then_inc(silu_ready, 1)
            link(dve.reduce_max(rbm[:, :], rb[:, :], AX))
            link(dve.tensor_scalar(rbd[:, :], rb[:, :], rbm[:, 0:1], None, ALU.subtract))
            dve.sem_inc(bias_exp_in, 1)
            dve.wait_ge(bias_exp, ONE + 1)
            dve.tensor_copy(ext[:, 0:P - 1], ext[:, P - 1:P].broadcast_to([H, P - 1]))
            link(dve.tensor_copy(ext[:, P + 2 * REL:w.EXT], ext[:, P + 2 * REL - 1:P + 2 * REL].broadcast_to([H, P - 1])))
            dve.sem_inc(bias_rows_ready, 1)
            n = 0
            for l in range(2):
                for b in range(B):
                    for j in range(3):
                        dve.wait_ge(mod_ready[n % 2], ONE + n // 2 + 1)
                        dve.tensor_copy(w.modrow[l][:, b, j * CH:(j + 1) * CH], ps[n % 2][:, :]).then_inc(mod_used[n % 2], 1)
                        n += 1
            dve.wait_ge(mod_used[0], ONE + 6)
            dve.wait_ge(mod_used[1], ONE + 6)
            dve.wait_ge(col_ready, ONE + 1)
            link(dve.tensor_copy(w.modcol[:, :, :, :], pc[:, :, :, :]))
            for l in range(2):
                for part in (CA, CB):
                    link(dve.tensor_scalar_add(w.modcol[:, l, 2 * part:2 * part + 2, :], w.modcol[:, l, 2 * part:2 * part + 2, :], 1.0))
                    r = w.modrow[l][:, :, part * D:(part + 1) * D]
                    link(dve.tensor_scalar_add(r, r, 1.0))
                for part in (GA, GB):
                    g = w.modrow[l][:, :, part * D:(part + 1) * D]
                    t = row[:, :].rearrange("p (b n) -> p b n", b=B)
                    link(dve.scalar_tensor_tensor(t, g, -1.0, g, op0=ALU.mult, op1=ALU.max))
                    link(dve.tensor_scalar(g, g, 0.0, 2.0, ALU.is_ge, ALU.mult))
                    link(dve.tensor_scalar_add(g, g, -1.0))
                    link(dve.tensor_scalar_max(t, t, 0.25))
                    link(dve.tensor_tensor(g, g, t, ALU.mult))
            link(dve.tensor_scalar_mul(w.bqk[:, 0:KD], w.bqk[:, 0:KD], w.SCALE))
            for b in range(B):
                link(dve.tensor_tensor(w.gbo0[:, b, :], w.modrow[0][:, b, GA * D:(GA + 1) * D], w.bo0[:, :], ALU.mult))

        @block.gpsimd
        def _(pool):
            link = linker(pool, pool_step)
            link(pool.memset(w.ident[:, :], 0.0))
            link(pool.affine_select(out=w.ident[:, :], in_=w.ident[:, :], compare_op=ALU.not_equal, fill=1.0,
                                    base=0, pattern=[[-1, P]], channel_multiplier=1))
            link(pool.memset(w.zeros[:, :], 0.0))
            link(pool.memset(w.eps[:, :], EPS))


def stage_qkv(nc, w):
    with ExitStack() as ctx:
        sem = lambda name: semaphore(nc, ctx, name)
        x_loaded = [sem(f"b_x_loaded{c}") for c in range(NC)]
        stat_step = sem("b_stat_step")
        var_ready = sem("b_var_ready")
        std_ready = sem("b_std_ready")
        norm_ready = sem("b_norm_ready")
        norm_used = sem("b_norm_used")
        turned = sem("b_turned")
        hT_ready = sem("b_hT_ready")
        hT_used = sem("b_hT_used")
        qk_ready = sem("b_qk_ready")
        v_ready = sem("b_v_ready")
        v_used = sem("b_v_used")
        whole_ready = sem("b_whole_ready")
        hi_ready = sem("b_hi_ready")
        rest_ready = sem("b_rest_ready")
        mid_ready = sem("b_mid_ready")
        low_ready = sem("b_low_ready")
        vout_ready = sem("b_vout_ready")
        stored = sem("b_stored")
        band_stored = sem("b_band_stored")
        stored_v = sem("b_stored_v")

        st = sbuf(nc, ctx, "b_st", [P, NT, 6])
        std = sbuf(nc, ctx, "b_std", [P, NT])
        mv = sbuf(nc, ctx, "b_mv", [P, NT, 2])
        xn = sbuf(nc, ctx, "b_xn", [P, CT, D])
        hT = sbuf(nc, ctx, "b_hT", [P, KD, CH])
        NB = 4
        whole = sbuf(nc, ctx, "b_whole", [P, NB, CH])
        parts = sbuf(nc, ctx, "b_parts", [P, 3, NB, CH], BF16)
        vout = sbuf(nc, ctx, "b_vout", [P, CT, D])
        pT = psum(nc, ctx, "b_pT", [P, KD, CH])
        pqk = psum(nc, ctx, "b_pqk", [P, NB, CH])
        pv = psum(nc, ctx, "b_pv", [P, CT, D])
        block = start(nc, ctx)

        @block.sync
        def _(sp):
            for c in range(NC):
                sp.dma_start(w.x[:, c * CT:(c + 1) * CT, :],
                             w.x_dram[c * CH:(c + 1) * CH, :].rearrange("(t p) n -> p t n", p=P)).then_inc(x_loaded[c], 16)
            for n in range(NH):
                sp.dma_start(w.skew_dram[n, :].rearrange("(p r) -> p r", r=w.EXT + 1)[:, 0:w.EXT],
                             w.ext_dram[n:n + 1, :].broadcast_to([P, w.EXT])).then_inc(band_stored, 16)
            with sp.Fori(0, B) as b:
                with sp.Fori(0, NC // B) as cb:
                    c = b * (NC // B) + cb
                    sp.wait_ge(vout_ready, ONE + c + 1)
                    for t in range(CT):
                        sp.dma_start(
                            w.v_dram[bass.ds(b * H, H), bass.ds(cb * CH + t * P, P), :].rearrange("h p d -> p h d"),
                            vout[:, t, :].rearrange("p (h d) -> p h d", d=DH)).then_inc(stored_v, 16)
                    sp.wait_ge(low_ready, ONE + NB * c + NB)
                    for part in range(3):
                        for blk in range(NB):
                            sp.dma_start(
                                w.qk_parts[blk // KD][part, bass.ds(b * D + blk % KD * P, P), bass.ds(cb * CH, CH)],
                                parts[:, part, blk, :]).then_inc(stored, 16)
            sp.wait_ge(band_stored, ONE + 16 * NH)
            sp.wait_ge(stored, ONE + 16 * 3 * NB * NC)
            sp.wait_ge(stored_v, ONE + 16 * CT * NC)

        @block.vector
        def _(dve):
            for t in range(NT):
                if t % CT == 0:
                    dve.wait_ge(x_loaded[t // CT], ONE + 16)
                dve.bn_stats(st[:, t, :], w.x[:, t, :]).then_inc(stat_step, 1)
            for t in range(NT):
                dve.wait_ge(stat_step, ONE + t + 1)
                dve.bn_aggr(mv[:, t, :], st[:, t, :]).then_inc(var_ready, 1)
            dve.wait_ge(std_ready, ONE + 1)
            dve.reciprocal(std[:, :], std[:, :]).then_inc(stat_step, 1)
            dve.wait_ge(stat_step, ONE + NT + 1)
            with dve.Fori(0, NC) as c:
                dve.wait_ge(norm_used, ONE + c + 1)
                for t in range(CT):
                    i = c * CT + t
                    last = dve.tensor_scalar(xn[:, t:t + 1, :], w.x[:, bass.ds(i, 1), :], mv[:, bass.ds(i, 1), 0:1].rearrange("p a b -> p (a b)"),
                                             std[:, bass.ds(i, 1)], ALU.subtract, ALU.mult)
                last.then_inc(norm_ready, 1)
                for blk in range(NB):
                    dve.wait_ge(hi_ready, ONE + NB * c + blk + 1)
                    dve.wait_ge(whole_ready, ONE + NB * c + blk + 1)
                    dve.tensor_tensor(whole[:, blk, :], whole[:, blk, :], parts[:, 0, blk, :], ALU.subtract).then_inc(rest_ready, 1)
                dve.wait_ge(v_ready, ONE + c + 1)
                dve.wait_ge(stored_v, ONE + 16 * CT * c)
                dve.tensor_tensor(vout[:, :, :], pv[:, :, :], w.bv0[:, :].rearrange("p (o n) -> p o n", o=1).broadcast_to([P, CT, D]),
                                  ALU.add).then_inc(vout_ready, 1)
                for blk in range(NB):
                    dve.wait_ge(mid_ready, ONE + NB * c + blk + 1)
                    dve.tensor_tensor(parts[:, 2, blk, :], whole[:, blk, :], parts[:, 1, blk, :], ALU.subtract).then_inc(low_ready, 1)

        @block.tensor
        def _(pe):
            pe.sem_inc(norm_used, 1)
            with pe.Fori(0, NC) as c:
                pe.wait_ge(norm_ready, ONE + c + 1)
                for t in range(CT):
                    for k in range(KD):
                        last = pe.transpose(pT[:, k, t * P:(t + 1) * P], xn[:, t, k * P:(k + 1) * P], w.ident[:, :])
                last.then_inc(norm_used, 1)
                pe.wait_ge(hT_ready, ONE + c * KD + KD)
                pe.wait_ge(hi_ready, ONE + NB * c)
                pe.wait_ge(whole_ready, ONE + NB * c)
                for blk in range(NB):
                    for k in range(KD):
                        last = pe.matmul(pqk[:, blk, :], w.Wqkv0[:, k, blk * P:(blk + 1) * P], hT[:, k, :],
                                         start=k == 0, stop=k == KD - 1)
                    last.then_inc(qk_ready, 1)
                pe.wait_ge(vout_ready, ONE + c)
                for t in range(CT):
                    for k in range(KD):
                        last = pe.matmul(pv[:, t, :], hT[:, k, t * P:(t + 1) * P], w.Wqkv0[:, k, 2 * D:3 * D],
                                         start=k == 0, stop=k == KD - 1)
                last.then_inc(v_ready, 1)

        @block.scalar
        def _(act):
            act.wait_ge(var_ready, ONE + NT)
            act.activation(std[:, :], mv[:, :, 1], ACT.Sqrt, bias=w.eps[:, 0:1]).then_inc(std_ready, 1)
            with act.Fori(0, B) as b:
                with act.Fori(0, NC // B) as cb:
                    c = b * (NC // B) + cb
                    wait_alone(w, act, norm_used, ONE + c + 2)
                    act.wait_ge(v_ready, ONE + c)
                    for k in range(KD):
                        act.activation(hT[:, k, :], pT[:, k, :], ACT.Identity,
                                       
                                       scale=w.modcol[:, 0, 2 * CA + k, bass.ds(b, 1)], bias=w.modcol[:, 0, 2 * SA + k, bass.ds(b, 1)]).then_inc(hT_ready, 1)
                    act.wait_ge(low_ready, ONE + NB * c)
                    act.wait_ge(stored, ONE + 16 * 3 * NB * c)
                    for blk in range(NB):
                        s = w.SCALE if blk < KD else 1.0
                        act.wait_ge(qk_ready, ONE + NB * c + blk + 1)
                        act.activation(parts[:, 0, blk, :], pqk[:, blk, :], ACT.Identity, scale=s, bias=w.bqk[:, blk:blk + 1]).then_inc(hi_ready, 1)
                        act.activation(whole[:, blk, :], pqk[:, blk, :], ACT.Identity, scale=s, bias=w.bqk[:, blk:blk + 1]).then_inc(whole_ready, 1)
                    for blk in range(NB):
                        act.wait_ge(rest_ready, ONE + NB * c + blk + 1)
                        act.activation(parts[:, 1, blk, :], whole[:, blk, :], ACT.Copy).then_inc(mid_ready, 1)


def stage_attention(nc, w):
    R6 = 6 * DH
    R8 = R6 + 2
    JT = S // P
    HALF = S // 2
    BANDT = w.BAND // P
    NBUF = 4
    VW = 32
    GROUPS = JT * (S // CH)
    PER_STEP = GROUPS // JT
    SHIFT = 6
    AHEAD = 2

    def band(t):
        return max(0, (t - 2) * P), min(S, (t + BANDT - 2) * P)

    def segments(t, half):
        lo, hi = band(t)
        a, z = half * HALF, (half + 1) * HALF
        cuts = [(a, min(z, lo), "left"), (max(a, lo), min(z, hi), "band"), (max(a, hi), z, "right")]
        return [c for c in cuts if c[0] < c[1]]

    band_parts = [[sum(k == "band" for _, _, k in segments(t, half)) for half in range(2)] for t in range(JT)]
    POOL_STEPS = sum(map(sum, band_parts))
    pool_after = [sum(map(sum, band_parts[:t + 1])) for t in range(JT)]

    with ExitStack() as ctx:
        sem = lambda name: semaphore(nc, ctx, name)
        max_loaded = [sem(f"c_max_loaded{q}") for q in range(2)]
        score_loaded = [sem(f"c_score_loaded{q}") for q in range(2)]
        consts_ready = sem("c_consts_ready")
        value_pad_ready = sem("c_value_pad_ready")
        group_ready = sem("c_group_ready")
        group_done = sem("c_group_done")
        max_ready = sem("c_max_ready")
        maxT_ready = sem("c_maxT_ready")
        max_parts_hi = sem("c_max_parts_hi")
        max_parts_ready = sem("c_max_parts_ready")
        max_rows_loaded = sem("c_max_rows_loaded")
        scores_ready = sem("c_scores_ready")
        probs_ready = sem("c_probs_ready")
        band_ready = sem("c_band_ready")
        summed = sem("c_summed")
        out_taken = sem("c_out_taken")
        out_stored = sem("c_out_stored")
        max_step = sem("c_max_step")
        zeroed = sem("c_zeroed")

        QM = [sbuf(nc, ctx, f"QM{q}", [R6, S], BF16) for q in range(2)]
        KM = [sbuf(nc, ctx, f"KM{q}", [R6, S], BF16) for q in range(2)]
        QS = [sbuf(nc, ctx, f"QS{q}", [R8, S], BF16) for q in range(2)]
        KS = [sbuf(nc, ctx, f"KS{q}", [R8, S], BF16) for q in range(2)]
        V = [sbuf(nc, ctx, f"V{q}", [P, JT, VW]) for q in range(2)]
        EB = [sbuf(nc, ctx, f"EB{q}", [P, BANDT * P]) for q in range(2)]
        probs = [sbuf(nc, ctx, f"probs{i}", [P, S]) for i in range(NBUF)]
        gmax = sbuf(nc, ctx, "gmax", [P, JT, S // CH])
        qmax = sbuf(nc, ctx, "qmax", [P, JT])
        mhi = sbuf(nc, ctx, "mhi", [JT, P], BF16)
        mlo = sbuf(nc, ctx, "mlo", [JT, P], BF16)
        osb = sbuf(nc, ctx, "osb", [P, CH])
        pg = [psum(nc, ctx, f"pg{i}", [P, CH]) for i in range(2)]
        psc = [psum(nc, ctx, f"psc{i}", [P, HALF]) for i in range(2)]
        po = psum(nc, ctx, "po", [P, CH])
        pm = psum(nc, ctx, "pm", [P, P])
        block = start(nc, ctx)

        @block.sync
        def _(sp):
            def load_parts(dst, order, src, n, loaded):
                at = 0
                for part, times in order:
                    for _ in range(times):
                        sp.dma_start(dst[at:at + DH, :], src[part, bass.ds(n * DH, DH), :]).then_inc(loaded, 16)
                        at += DH

            Q_ORDER = [(0, 3), (1, 2), (2, 1)]
            K_ORDER = [(0, 1), (1, 1), (2, 1), (0, 1), (1, 1), (0, 1)]

            def load_max(n, q):
                load_parts(QM[q], Q_ORDER, w.qk_parts[0], n, max_loaded[q])
                load_parts(KM[q], K_ORDER, w.qk_parts[1], n, max_loaded[q])

            def load_scores(n, q):
                load_parts(QS[q], Q_ORDER, w.qk_parts[0], n, score_loaded[q])
                load_parts(KS[q], K_ORDER, w.qk_parts[1], n, score_loaded[q])
                sp.dma_start(V[q][:, :, 0:DH], w.v_dram[bass.ds(n, 1), :, :].rearrange("o (t p) d -> p (o t) d", p=P)).then_inc(score_loaded[q], 16)
                sp.dma_start(EB[q][:, :], 
                             w.skew_dram[bass.ds(n, 1), P - 1:P - 1 + P * w.EXT].rearrange("o (p r) -> p (o r)", r=w.EXT)[:, 0:BANDT * P]).then_inc(score_loaded[q], 16)

            def move_max(n, q):
                sp.wait_ge(max_parts_ready, ONE + n + 1)
                sp.dma_start(QS[q][R6:R6 + 1, :], mhi[:, :]).then_inc(max_rows_loaded, 16)
                sp.dma_start(QS[q][R6 + 1:R8, :], mlo[:, :]).then_inc(max_rows_loaded, 16)

            def store_out(n):
                sp.wait_ge(out_taken, ONE + n + 1)
                for c in range(S // CH):
                    sp.dma_start(w.attT_dram[bass.ds(n, 1), :, c * CH:(c + 1) * CH].rearrange("o r t -> (o r) t"),
                                 osb[VW * c:VW * c + DH + 1, :]).then_inc(out_stored, 16)

            load_max(0, 0)
            rows = w.xe_dram.rearrange("(n p k) d -> n p (k d)", p=P, k=w.zeros.shape[1] // D)
            for i in range(rows.shape[0]):
                sp.dma_start(rows[i], w.zeros[:, :]).then_inc(zeroed, 16)
            sp.wait_ge(value_pad_ready, ONE + 1)
            load_scores(0, 0)
            load_max(1, 1)
            load_scores(1, 1)
            move_max(0, 0)

            def pair(g, last):
                for q in range(2):
                    n = g * 2 + q
                    if not last:
                        sp.wait_ge(group_ready, ONE + GROUPS * n + GROUPS)
                        load_max(n + 2, q)
                    if not last or q == 0:
                        move_max(n + 1, 1 - q)
                    if not last:
                        sp.wait_ge(summed, ONE + JT * n + JT + NBUF - 1)
                        sp.wait_ge(band_ready, ONE + POOL_STEPS * n + POOL_STEPS)
                        load_scores(n + 2, q)
                    store_out(n)

            with sp.Fori(0, NH // 2 - 1) as g:
                pair(g, False)
            pair(NH // 2 - 1, True)
            sp.wait_ge(out_stored, ONE + 16 * (S // CH) * NH)
            sp.wait_ge(zeroed, ONE + 16 * rows.shape[0])

        @block.tensor
        def _(pe):
            def group(n, q, k):
                tile, c = divmod(k, S // CH)
                pe.wait_ge(group_done, ONE + GROUPS * n + k)
                pe.matmul(pg[k % 2][:, :], QM[q][:, tile * P:(tile + 1) * P], KM[q][:, c * CH:(c + 1) * CH],
                          start=True, stop=True).then_inc(group_ready, 1)

            def turn_max(n):
                pe.wait_ge(max_ready, ONE + n + 1)
                pe.transpose(pm[0:JT, :], qmax[:, :], w.ident[:, :]).then_inc(maxT_ready, 1)

            def scores(n, q, t, half):
                pe.wait_ge(probs_ready, ONE + 2 * JT * n + 2 * t + half)
                for c in range(HALF // CH):
                    at = half * HALF + c * CH
                    last = pe.matmul(psc[half][:, c * CH:(c + 1) * CH], KS[q][:, t * P:(t + 1) * P], QS[q][:, at:at + CH],
                                     start=True, stop=True)
                last.then_inc(scores_ready, 1)

            def sums(n, q, t):
                pe.wait_ge(probs_ready, ONE + 2 * JT * n + 2 * t + 3)
                pe.wait_ge(band_ready, ONE + POOL_STEPS * n + pool_after[t])
                if t == 0:
                    pe.wait_ge(out_taken, ONE + n)
                for c in range(S // CH):
                    last = pe.matmul(po[VW * c:VW * (c + 1), :], V[q][:, t, :], probs[t % NBUF][:, c * CH:(c + 1) * CH],
                                     start=t == 0, stop=t == JT - 1)
                last.then_inc(summed, 1)

            pe.sem_inc(summed, NBUF - 1)
            pe.wait_ge(consts_ready, ONE + 1)
            pe.wait_ge(max_loaded[0], ONE + 192)
            for k in range(GROUPS):
                group(0, 0, k)
            turn_max(0)
            pe.wait_ge(max_loaded[1], ONE + 192)
            for k in range(2):
                group(1, 1, k)
            pe.wait_ge(score_loaded[0], ONE + 224)
            pe.wait_ge(max_rows_loaded, ONE + 32)
            for t in range(AHEAD):
                scores(0, 0, t, 0)
                scores(0, 0, t, 1)
                for k in range(SHIFT * PER_STEP // AHEAD):
                    if k + t * (SHIFT * PER_STEP // AHEAD) >= 2:
                        group(1, 1, k + t * (SHIFT * PER_STEP // AHEAD))

            def pair(g, last):
                for q in range(2):
                    n = g * 2 + q
                    more = not last or q == 0
                    for t in range(JT):
                        if t == JT - SHIFT and not last:
                            pe.wait_ge(max_loaded[q], ONE + 192 * g + 384)
                        if t == JT - AHEAD and more:
                            pe.wait_ge(max_rows_loaded, ONE + 32 * n + 64)
                            pe.wait_ge(score_loaded[1 - q], ONE + 224 * g + 224 * (1 + q))

                        def next_group(i):
                            if t < JT - SHIFT and more:
                                group(n + 1, 1 - q, (t + SHIFT) * PER_STEP + i)
                            elif t >= JT - SHIFT and not last:
                                group(n + 2, q, (t + SHIFT - JT) * PER_STEP + i)

                        for half in range(2):
                            if t < JT - AHEAD:
                                scores(n, q, t + AHEAD, half)
                            elif more:
                                scores(n + 1, 1 - q, t + AHEAD - JT, half)
                            next_group(half)
                        if t == JT - SHIFT and more:
                            turn_max(n + 1)
                        sums(n, q, t)
                        for i in range(2, PER_STEP):
                            next_group(i)

            with pe.Fori(0, NH // 2 - 1) as g:
                pair(g, False)
            pair(NH // 2 - 1, True)

        @block.vector
        def _(dve):
            dve.sem_inc(group_done, 1)
            for q in range(2):
                dve.memset(KS[q][R6:R8, :], 1.0)
                dve.memset(V[q][:, :, :], 0.0).then_inc(max_step, 1)
            dve.wait_ge(max_step, ONE + 2)
            for q in range(2):
                last = dve.memset(V[q][:, :, DH:DH + 1], 1.0)
            last.then_inc(value_pad_ready, 1)
            dve.wait_ge(value_pad_ready, ONE + 1)
            dve.sem_inc(consts_ready, 1)

            def head_max(n):
                for k in range(GROUPS):
                    tile, c = divmod(k, S // CH)
                    dve.wait_ge(group_ready, ONE + GROUPS * n + k + 1)
                    dve.reduce_max(gmax[:, tile, c:c + 1], pg[k % 2][:, :], AX).then_inc(group_done, 1)
                dve.wait_ge(group_done, ONE + GROUPS * n + GROUPS + 1)
                dve.reduce_max(qmax[:, :], gmax[:, :, :], AX).then_inc(max_ready, 1)
                dve.wait_ge(maxT_ready, ONE + n + 1)
                dve.wait_ge(max_rows_loaded, ONE + 32 * n)
                dve.tensor_scalar_mul(mhi[:, :], pm[0:JT, :], -1.0).then_inc(max_parts_hi, 1)
                dve.wait_ge(max_parts_hi, ONE + n + 1)
                dve.scalar_tensor_tensor(mlo[:, :], pm[0:JT, :], -1.0, mhi[:, :], op0=ALU.mult, op1=ALU.subtract).then_inc(max_parts_ready, 1)

            head_max(0)
            with dve.Fori(1, NH) as n:
                head_max(n)

        @block.scalar
        def _(act):
            def exps(n, t, half):
                if half == 0:
                    act.wait_ge(summed, ONE + JT * n + t)
                wait_alone(w, act, scores_ready, ONE + 2 * JT * n + 2 * t + half + 1)
                for a, z, kind in segments(t, half):
                    bias = {"left": w.far[:, bass.ds(n, 1), 0:1], "right": w.far[:, bass.ds(n, 1), 1:2], "band": None}[kind]
                    more = {} if bias is None else {"bias": bias.rearrange("p a b -> p (a b)")}
                    last = act.activation(probs[t % NBUF][:, a:z], psc[half][:, a - half * HALF:z - half * HALF], ACT.Exp, **more)
                last.then_inc(probs_ready, 1)

            act.sem_inc(probs_ready, 1)
            for t in range(AHEAD):
                exps(0, t, 0)
                exps(0, t, 1)

            def head(n, last):
                for t in range(AHEAD, JT):
                    exps(n, t, 0)
                    exps(n, t, 1)
                if not last:
                    for t in range(AHEAD):
                        exps(n + 1, t, 0)
                        exps(n + 1, t, 1)
                act.wait_ge(summed, ONE + JT * n + JT + NBUF - 1)
                act.wait_ge(out_stored, ONE + 16 * (S // CH) * n)
                act.activation(osb[:, :], po[:, :], ACT.Copy).then_inc(out_taken, 1)

            with act.Fori(0, NH - 1) as n:
                head(n, False)
            head(NH - 1, True)

        @block.gpsimd
        def _(pool):
            with pool.Fori(0, NH // 2) as g:
                for q in range(2):
                    n = g * 2 + q
                    pool.wait_ge(score_loaded[q], ONE + 224 * g + 224)
                    for t in range(JT):
                        lo = (t - 2) * P
                        for half in range(2):
                            for a, z, kind in segments(t, half):
                                if kind == "band":
                                    pool.wait_ge(probs_ready, ONE + 2 * JT * n + 2 * t + half + 2)
                                    part = probs[t % NBUF][:, a:z]
                                    pool.tensor_tensor(part, part, EB[q][:, a - lo:z - lo], ALU.mult).then_inc(band_ready, 1)


E0, K0, I0, CAP = 64, 4, 128, 256


def stage_project(nc, w):
    with ExitStack() as ctx:
        sem = lambda name: semaphore(nc, ctx, name)
        loaded = sem("d_loaded")
        inverse_ready = sem("d_inverse_ready")
        att_ready = sem("d_att_ready")
        projected = sem("d_projected")
        gated = sem("d_gated")
        added = sem("d_added")
        raw = sbuf(nc, ctx, "d_raw", [P, KD, CH])
        tot = sbuf(nc, ctx, "d_tot", [P, KD, CH])
        att = sbuf(nc, ctx, "d_att", [P, KD, CH])
        gate = sbuf(nc, ctx, "d_gate", [P, CT, D])
        pp = psum(nc, ctx, "d_pp", [P, CT, D])
        block = start(nc, ctx)
        HB = P // DH

        @block.sync
        def _(sp):
            with sp.Fori(0, B) as b:
                with sp.Fori(0, NC // B) as cb:
                    c = b * (NC // B) + cb
                    sp.wait_ge(att_ready, ONE + c)
                    for k in range(KD):
                        heads = bass.ds(b * H + k * HB, HB)
                        sp.dma_start(raw[:, k, :], w.attT_dram[heads, 0:DH, bass.ds(cb * CH, CH)]).then_inc(loaded, 16)
                        sp.dma_start(tot[:, k, :], w.attT_dram[heads, DH:DH + 1, bass.ds(cb * CH, CH)].broadcast_to([HB, DH, CH])).then_inc(loaded, 16)

        @block.vector
        def _(dve):
            with dve.Fori(0, B) as b:
                with dve.Fori(0, NC // B) as cb:
                    c = b * (NC // B) + cb
                    dve.wait_ge(loaded, ONE + 16 * 2 * KD * c + 16 * 2 * KD)
                    dve.reciprocal(tot[:, :, :], tot[:, :, :]).then_inc(inverse_ready, 1)
                    dve.wait_ge(inverse_ready, ONE + c + 1)
                    dve.wait_ge(projected, ONE + c)
                    dve.tensor_tensor(att[:, :, :], raw[:, :, :], tot[:, :, :], ALU.mult).then_inc(att_ready, 1)
                    dve.wait_ge(projected, ONE + c + 1)
                    ga = w.modrow[0][:, bass.ds(b, 1), GA * D:(GA + 1) * D].broadcast_to([P, CT, D])
                    xs = w.x[:, bass.ds(c * CT, CT), :]
                    dve.tensor_tensor(gate[:, :, :], pp[:, :, :], ga, ALU.mult).then_inc(gated, 1)
                    dve.wait_ge(gated, ONE + 2 * c + 1)
                    dve.tensor_tensor(gate[:, :, :], gate[:, :, :], w.gbo0[:, bass.ds(b, 1), :].broadcast_to([P, CT, D]), ALU.add).then_inc(gated, 1)
                    dve.wait_ge(gated, ONE + 2 * c + 2)
                    dve.tensor_tensor(xs, xs, gate[:, :, :], ALU.add).then_inc(added, 1)

        @block.tensor
        def _(pe):
            with pe.Fori(0, NC) as c:
                pe.wait_ge(att_ready, ONE + c + 1)
                pe.wait_ge(gated, ONE + 2 * c)
                for t in range(CT):
                    for k in range(KD):
                        last = pe.matmul(pp[:, t, :], att[:, k, t * P:(t + 1) * P], w.Wout0[:, k, :], start=k == 0, stop=k == KD - 1)
                last.then_inc(projected, 1)


def stage_norm(nc, w, x, tiles, mean_var, rstd, name):
    with ExitStack() as ctx:
        sem = lambda n: semaphore(nc, ctx, f"{name}_{n}")
        stats_ready, var_ready, std_ready = sem("stats_ready"), sem("var_ready"), sem("std_ready")
        st = sbuf(nc, ctx, f"{name}_st", [P, tiles, 6])
        block = start(nc, ctx)

        @block.vector
        def _(dve):
            for t in range(tiles):
                dve.bn_stats(st[:, t, :], x[:, t, :]).then_inc(stats_ready, 1)
            for t in range(tiles):
                dve.wait_ge(stats_ready, ONE + t + 1)
                dve.bn_aggr(mean_var[:, t, :], st[:, t, :]).then_inc(var_ready, 1)
            dve.wait_ge(std_ready, ONE + 1)
            dve.reciprocal(rstd[:, 0:tiles], rstd[:, 0:tiles])

        @block.scalar
        def _(act):
            act.wait_ge(var_ready, ONE + tiles)
            act.activation(rstd[:, 0:tiles], mean_var[:, 0:tiles, 1], ACT.Sqrt, bias=w.eps[:, 0:1]).then_inc(std_ready, 1)


def stage_router(nc, w, x, mean_var, rstd, h, hT_all, layer, Wg, logits, name):
    n_experts = logits.shape[2]
    with ExitStack() as ctx:
        sem = lambda n: semaphore(nc, ctx, f"{name}_{n}")
        norm_ready, norm_turned, hT_ready, logits_ready = sem("norm_ready"), sem("norm_turned"), sem("hT_ready"), sem("logits_ready")
        logits_out, scaled, shifted, hT_kept = sem("logits_out"), sem("scaled"), sem("shifted"), sem("hT_kept")
        xn = sbuf(nc, ctx, f"{name}_xn", [P, CT, D])
        hT = sbuf(nc, ctx, f"{name}_hT", [P, KD, CH])
        tmp = sbuf(nc, ctx, f"{name}_tmp", [P, CT, D])
        pT = psum(nc, ctx, f"{name}_pT", [P, KD, CH])
        pl = psum(nc, ctx, f"{name}_pl", [P, CT, n_experts])
        block = start(nc, ctx)
        natural = h is not None

        @block.vector
        def _(dve):
            with dve.Fori(0, NC) as c:
                dve.wait_ge(norm_turned, ONE + c)
                if natural:
                    dve.wait_ge(scaled, ONE + c)
                for t in range(CT):
                    i = c * CT + t
                    last = dve.tensor_scalar(xn[:, t:t + 1, :], x[:, bass.ds(i, 1), :], mean_var[:, bass.ds(i, 1), 0:1].rearrange("p a b -> p (a b)"),
                                             rstd[:, bass.ds(i, 1)], ALU.subtract, ALU.mult)
                last.then_inc(norm_ready, 1)
                dve.wait_ge(logits_ready, ONE + c + 1)
                dve.tensor_copy(logits[:, bass.ds(c * CT, CT), :], pl[:, :, :]).then_inc(logits_out, 1)

        @block.tensor
        def _(pe):
            with pe.Fori(0, NC) as c:
                pe.wait_ge(norm_ready, ONE + c + 1)
                pe.wait_ge(hT_ready, ONE + KD * c)
                for t in range(CT):
                    for k in range(KD):
                        last = pe.transpose(pT[:, k, t * P:(t + 1) * P], xn[:, t, k * P:(k + 1) * P], w.ident[:, :])
                last.then_inc(norm_turned, 1)
                pe.wait_ge(hT_ready, ONE + KD * c + KD)
                pe.wait_ge(logits_out, ONE + c)
                for t in range(CT):
                    for k in range(KD):
                        last = pe.matmul(pl[:, t, :], hT[:, k, t * P:(t + 1) * P], Wg[:, k, :], start=k == 0, stop=k == KD - 1)
                last.then_inc(logits_ready, 1)

        @block.scalar
        def _(act):
            with act.Fori(0, B) as b:
                with act.Fori(0, NC // B) as cb:
                    c = b * (NC // B) + cb
                    wait_alone(w, act, norm_turned, ONE + c + 1)
                    act.wait_ge(logits_ready, ONE + c)
                    if hT_all is not None:
                        act.wait_ge(hT_kept, ONE + c)
                    for k in range(KD):
                        act.activation(hT[:, k, :], pT[:, k, :], ACT.Identity, scale=w.modcol[:, layer, 2 * CB + k, bass.ds(b, 1)],
                                       bias=w.modcol[:, layer, 2 * SB_ + k, bass.ds(b, 1)]).then_inc(hT_ready, 1)

        @block.gpsimd
        def _(pool):
            with pool.Fori(0, B) as b:
                with pool.Fori(0, NC // B) as cb:
                    c = b * (NC // B) + cb
                    if hT_all is not None:
                        pool.wait_ge(hT_ready, ONE + KD * c + KD)
                        pool.tensor_copy(hT_all[:, :, bass.ds(c * CH, CH)], hT[:, :, :]).then_inc(hT_kept, 1)
                    if natural:
                        pool.wait_ge(norm_ready, ONE + c + 1)
                        pool.wait_ge(shifted, ONE + c)
                        row = lambda part: w.modrow[layer][:, bass.ds(b, 1), part * D:(part + 1) * D].broadcast_to([P, CT, D])
                        pool.tensor_tensor(tmp[:, :, :], xn[:, :, :], row(CB), ALU.mult).then_inc(scaled, 1)
                        pool.wait_ge(scaled, ONE + c + 1)
                        pool.tensor_tensor(h[:, bass.ds(c * CT, CT), :], tmp[:, :, :], row(SB_), ALU.add).then_inc(shifted, 1)


def softmax_rows(dve, link, logits, top, total, exp_request, exp_done):
    tiles, n = logits.shape[1], logits.shape[2]
    over = lambda v: v[:, :].rearrange("p (t o) -> p t o", o=1).broadcast_to([P, tiles, n])
    link(dve.reduce_max(top[:, :], logits[:, :, :], AX))
    dve.tensor_tensor(logits[:, :, :], logits[:, :, :], over(top), ALU.subtract).then_inc(exp_request, 1)
    dve.wait_ge(exp_done, ONE + 1)
    link(dve.reduce_sum(total[:, :], logits[:, :, :], AX))
    link(dve.reciprocal(total[:, :], total[:, :]))
    link(dve.tensor_tensor(logits[:, :, :], logits[:, :, :], over(total), ALU.mult))


def stage_route(nc, w):
    with ExitStack() as ctx:
        sem = lambda name: semaphore(nc, ctx, name)
        step = sem("r_step")
        exp_request, exp_done = sem("r_exp_request"), sem("r_exp_done")
        made = sem("r_made")
        mask_ready, counted, base_step = sem("r_mask_ready"), sem("r_counted"), sem("r_base_step")
        N = NT * K0
        top = sbuf(nc, ctx, "r_top", [P, NT])
        total = sbuf(nc, ctx, "r_total", [P, NT])
        m8 = sbuf(nc, ctx, "r_m8", [P, NT, 8])
        i8 = sbuf(nc, ctx, "r_i8", [P, NT, 8], U32)
        i4 = sbuf(nc, ctx, "r_i4", [P, N])
        col_i = sbuf(nc, ctx, "r_col_i", [P, E0], I32)
        col = sbuf(nc, ctx, "r_col", [P, E0])
        chosen = sbuf(nc, ctx, "r_chosen", [P, N, E0], BF16)
        mask = sbuf(nc, ctx, "r_mask", [P, NT, E0], BF16)
        before = sbuf(nc, ctx, "r_before", [P, P], BF16)
        ones = sbuf(nc, ctx, "r_ones", [P, P], BF16)
        base = sbuf(nc, ctx, "r_base", [P, NT, E0])
        tot = sbuf(nc, ctx, "r_tot", [P, NT, E0])
        prod = sbuf(nc, ctx, "r_prod", [P, N, E0])
        place = sbuf(nc, ctx, "r_place", [P, N])
        over = sbuf(nc, ctx, "r_over", [P, N])
        slot = sbuf(nc, ctx, "r_slot", [P, N])
        G = CH // E0
        pw = psum(nc, ctx, "r_pw", [P, NT, E0])
        pt = psum(nc, ctx, "r_pt", [P, NT, E0])
        block = start(nc, ctx)
        BIG = float(1 << 22)

        @block.gpsimd
        def _(pool):
            pool.iota(col_i[:, :], [[1, E0]], base=0, channel_multiplier=0).then_inc(made, 1)
            pool.memset(ones[:, :], 1.0).then_inc(made, 1)
            pool.wait_ge(made, ONE + 2)
            pool.affine_select(out=before[:, :], in_=ones[:, :], compare_op=ALU.is_gt, fill=0.0, base=0,
                               pattern=[[1, P]], channel_multiplier=-1).then_inc(made, 1)

        @block.scalar
        def _(act):
            act.wait_ge(exp_request, ONE + 1)
            act.activation(w.logits0[:, :, :], w.logits0[:, :, :], ACT.Exp).then_inc(exp_done, 1)

        @block.tensor
        def _(pe):
            pe.wait_ge(made, ONE + 3)
            pe.wait_ge(mask_ready, ONE + 1)
            for g in range(NT // G):
                pe.matmul(pw[:, g * G:(g + 1) * G, :], before[:, :], mask[:, g * G:(g + 1) * G, :], start=True, stop=True)
                last = pe.matmul(pt[:, g * G:(g + 1) * G, :], ones[:, :], mask[:, g * G:(g + 1) * G, :], start=True, stop=True)
            last.then_inc(counted, 1)

        @block.vector
        def _(dve):
            link = linker(dve, step)
            probs = w.logits0
            softmax_rows(dve, link, probs, top, total, exp_request, exp_done)
            for t in range(NT):
                last = dve.max(m8[:, t, :], probs[:, t, :])
            link(last)
            for t in range(NT):
                last = dve.max_index(i8[:, t, :], m8[:, t, :], probs[:, t, :])
            dve.tensor_copy(w.gate4[:, :, :], m8[:, :, 0:K0])
            link(last)
            link(dve.tensor_copy(i4[:, :].rearrange("p (t k) -> p t k", k=K0), i8[:, :, 0:K0]))
            dve.wait_ge(made, ONE + 1)
            link(dve.tensor_copy(col[:, :], col_i[:, :]))
            link(dve.tensor_tensor(chosen[:, :, :], col[:, :].rearrange("p (o e) -> p o e", o=1).broadcast_to([P, N, E0]),
                                   i4[:, :].rearrange("p (n o) -> p n o", o=1).broadcast_to([P, N, E0]), ALU.is_equal))
            by_k = chosen[:, :, :].rearrange("p (t k) e -> p t k e", k=K0)
            link(dve.tensor_tensor(mask[:, :, :], by_k[:, :, 0, :], by_k[:, :, 1, :], ALU.add))
            link(dve.tensor_tensor(mask[:, :, :], mask[:, :, :], by_k[:, :, 2, :], ALU.add))
            dve.tensor_tensor(mask[:, :, :], mask[:, :, :], by_k[:, :, 3, :], ALU.add).then_inc(mask_ready, 1)
            dve.wait_ge(counted, ONE + 1)
            dve.tensor_copy(tot[:, :, :], pt[:, :, :]).then_inc(base_step, 1)
            dve.memset(base[:, 0:1, :], 0.0).then_inc(base_step, 1)
            dve.wait_ge(base_step, ONE + 2)
            with dve.Fori(0, NT - 1) as t:
                dve.wait_ge(base_step, ONE + t + 2)
                dve.tensor_tensor(base[:, bass.ds(t + 1, 1), :], base[:, bass.ds(t, 1), :], tot[:, bass.ds(t, 1), :], ALU.add).then_inc(base_step, 1)
            dve.wait_ge(base_step, ONE + NT + 1)
            link(dve.tensor_tensor(base[:, :, :], pw[:, :, :], base[:, :, :], ALU.add))
            for k in range(K0):
                last = dve.tensor_tensor(prod[:, :, :].rearrange("p (t k) e -> p t k e", k=K0)[:, :, k, :], by_k[:, :, k, :], base[:, :, :], ALU.mult)
            link(last)
            link(dve.reduce_sum(place[:, :], prod[:, :, :], AX))
            link(dve.tensor_scalar(over[:, :], place[:, :], float(CAP), BIG, ALU.is_ge, ALU.mult))
            link(dve.scalar_tensor_tensor(slot[:, :], i4[:, :], float(CAP), place[:, :], op0=ALU.mult, op1=ALU.add))
            link(dve.tensor_tensor(slot[:, :], slot[:, :], over[:, :], ALU.add))
            link(dve.tensor_copy(w.put_at[:, :, :].rearrange("p t k -> p (t k)"), slot[:, :]))
            link(dve.tensor_scalar_min(place[:, :], place[:, :], float(CAP - 1)))
            link(dve.scalar_tensor_tensor(slot[:, :], i4[:, :], float(CAP), place[:, :], op0=ALU.mult, op1=ALU.add))
            dve.memset(w.get_from[:, NT:NT + 2, :], 0)
            link(dve.tensor_copy(w.get_from[:, 0:NT, :].rearrange("p t k -> p (t k)"), slot[:, :]))


def stage_scatter(nc, w):
    with ExitStack() as ctx:
        sem = lambda name: semaphore(nc, ctx, name)
        staged = sem("s_staged")
        sent = [gpsimd_dma_semaphore(nc, ctx, f"s_sent{q}") for q in range(2)]
        rows = [sbuf(nc, ctx, f"s_rows{q}", [P, D]) for q in range(2)]
        at = [sbuf(nc, ctx, f"s_at{q}", [P, K0], I32) for q in range(2)]
        block = start(nc, ctx)

        @block.vector
        def _(dve):
            def stage(t, q):
                dve.tensor_copy(at[q][:, :].rearrange("p (o k) -> p o k", o=1), w.put_at[:, bass.ds(t, 1), :])
                dve.tensor_copy(rows[q][:, :].rearrange("p (o n) -> p o n", o=1), w.h[:, bass.ds(t, 1), :]).then_inc(staged, 1)

            for q in range(2):
                stage(q, q)
            with dve.Fori(1, NT // 2) as g:
                for q in range(2):
                    dve.wait_ge(sent[q], 16 * K0 * g)
                    stage(g * 2 + q, q)

        @block.gpsimd
        def _(pool):
            with pool.Fori(0, NT // 2) as g:
                for q in range(2):
                    wait_alone(w, pool, staged, ONE + g * 2 + q + 1)
                    for k in range(K0):
                        pool.indirect_dma_start(out=w.xe_dram[:, :], out_offset=bass.IndirectOffsetOnAxis(ap=at[q][:, k:k + 1], axis=0),
                                                in_=rows[q][:, :], in_offset=None, bounds_check=E0 * CAP - 1, oob_is_err=False).then_inc(sent[q], 16)
            for q in range(2):
                pool.wait_ge(sent[q], 16 * K0 * (NT // 2))


def stage_experts(nc, w):
    with ExitStack() as ctx:
        sem = lambda name: semaphore(nc, ctx, name)
        loaded = [sem(f"e_loaded{q}") for q in range(2)]
        turned, xT_ready = sem("e_turned"), sem("e_xT_ready")
        up_ready, silu_ready, g_ready, down_ready = sem("e_up_ready"), sem("e_silu_ready"), sem("e_g_ready"), sem("e_down_ready")
        y_ready = sem("e_y_ready")
        stored = [sem(f"e_stored{q}") for q in range(2)]
        SC = CAP // P
        X = [sbuf(nc, ctx, f"e_X{q}", [P, SC, D]) for q in range(2)]
        W1 = [sbuf(nc, ctx, f"e_W1{q}", [P, KD, 2 * I0]) for q in range(2)]
        W2 = [sbuf(nc, ctx, f"e_W2{q}", [P, D]) for q in range(2)]
        XT = [sbuf(nc, ctx, f"e_XT{q}", [P, KD, CAP]) for q in range(2)]
        SG = [sbuf(nc, ctx, f"e_SG{q}", [P, CAP]) for q in range(2)]
        G = [sbuf(nc, ctx, f"e_G{q}", [P, CAP]) for q in range(2)]
        Y = [sbuf(nc, ctx, f"e_Y{q}", [P, SC, D]) for q in range(2)]
        px = [psum(nc, ctx, f"e_px{q}", [P, KD, CAP]) for q in range(2)]
        ph = [psum(nc, ctx, f"e_ph{q}", [P, 2, CAP]) for q in range(2)]
        py = [psum(nc, ctx, f"e_py{q}", [P, SC, D]) for q in range(2)]
        block = start(nc, ctx)

        @block.sync
        def _(sp):
            with sp.Fori(0, E0 // 2) as g:
                for q in range(2):
                    e = g * 2 + q
                    sp.wait_ge(down_ready, ONE + g * 2)
                    sp.dma_start(W1[q][:, :, :], w.w1_0[bass.ds(e, 1), :, :].rearrange("o (k p) n -> p (o k) n", p=P)).then_inc(loaded[q], 16)
                    sp.dma_start(W2[q][:, :], w.w2_0[bass.ds(e, 1), :, :].rearrange("o p n -> p (o n)")).then_inc(loaded[q], 16)
                    sp.dma_start(X[q][:, :, :], w.xe_dram[bass.ds(e * CAP, CAP), :].rearrange("(s p) n -> p s n", p=P)).then_inc(loaded[q], 16)

        @block.tensor
        def _(pe):
            with pe.Fori(0, E0 // 2) as g:
                for q in range(2):
                    pe.wait_ge(loaded[q], ONE + 48 * g + 48)
                    pe.wait_ge(xT_ready, ONE + g * 2)
                    for s in range(SC):
                        for k in range(KD):
                            last = pe.transpose(px[q][:, k, s * P:(s + 1) * P], X[q][:, s, k * P:(k + 1) * P], w.ident[:, :])
                    last.then_inc(turned, 1)
                for q in range(2):
                    pe.wait_ge(xT_ready, ONE + g * 2 + q + 1)
                    pe.wait_ge(g_ready, ONE + g * 2)
                    for f in range(2):
                        for k in range(KD):
                            last = pe.matmul(ph[q][:, f, :], W1[q][:, k, f * I0:(f + 1) * I0], XT[q][:, k, :], start=k == 0, stop=k == KD - 1)
                    last.then_inc(up_ready, 1)
                for q in range(2):
                    pe.wait_ge(g_ready, ONE + g * 2 + q + 1)
                    pe.wait_ge(y_ready, ONE + g * 2)
                    for s in range(SC):
                        last = pe.matmul(py[q][:, s, :], G[q][:, s * P:(s + 1) * P], W2[q][:, :], start=True, stop=True)
                    last.then_inc(down_ready, 1)

        @block.scalar
        def _(act):
            with act.Fori(0, E0 // 2) as g:
                for q in range(2):
                    act.wait_ge(turned, ONE + g * 2 + q + 1)
                    act.wait_ge(up_ready, ONE + g * 2)
                    act.activation(XT[q][:, :, :], px[q][:, :, :], ACT.Copy).then_inc(xT_ready, 1)
                for q in range(2):
                    act.wait_ge(up_ready, ONE + g * 2 + q + 1)
                    act.wait_ge(g_ready, ONE + g * 2)
                    act.activation(SG[q][:, :], ph[q][:, 0, :], ACT.Silu).then_inc(silu_ready, 1)
                for q in range(2):
                    act.wait_ge(y_ready, ONE + g * 2 + q + 1)
                    act.dma_start(w.ye_dram[bass.ds((g * 2 + q) * CAP, CAP), :].rearrange("(s p) n -> p s n", p=P), Y[q][:, :, :]).then_inc(stored[q], 16)
            for q in range(2):
                act.wait_ge(stored[q], ONE + 16 * (E0 // 2))

        @block.vector
        def _(dve):
            with dve.Fori(0, E0 // 2) as g:
                for q in range(2):
                    dve.wait_ge(silu_ready, ONE + g * 2 + q + 1)
                    dve.wait_ge(down_ready, ONE + g * 2)
                    dve.tensor_tensor(G[q][:, :], SG[q][:, :], ph[q][:, 1, :], ALU.mult).then_inc(g_ready, 1)
                for q in range(2):
                    dve.wait_ge(down_ready, ONE + g * 2 + q + 1)
                    dve.wait_ge(stored[q], ONE + 16 * g)
                    dve.tensor_copy(Y[q][:, :, :], py[q][:, :, :]).then_inc(y_ready, 1)


def stage_combine(nc, w):
    with ExitStack() as ctx:
        sem = lambda name: semaphore(nc, ctx, name)
        staged, summed, scaled, added = sem("f_staged"), sem("f_summed"), sem("f_scaled"), sem("f_added")
        got = [gpsimd_dma_semaphore(nc, ctx, f"f_got{q}") for q in range(2)]
        stored = sem("f_stored")
        at = [sbuf(nc, ctx, f"f_at{q}", [P, K0], I32) for q in range(2)]
        y = [sbuf(nc, ctx, f"f_y{q}", [P, K0, D]) for q in range(2)]
        acc = [sbuf(nc, ctx, f"f_acc{q}", [P, 1, D]) for q in range(2)]
        block = start(nc, ctx)

        @block.gpsimd
        def _(pool):
            with pool.Fori(0, NT // 2) as g:
                for q in range(2):
                    wait_alone(w, pool, staged, ONE + g * 2 + q + 1)
                    for k in range(K0):
                        pool.indirect_dma_start(out=y[q][:, k, :], out_offset=None, in_=w.ye_dram[:, :],
                                                in_offset=bass.IndirectOffsetOnAxis(ap=at[q][:, k:k + 1], axis=0)).then_inc(got[q], 16)

        @block.vector
        def _(dve):
            def stage(t, q):
                dve.tensor_copy(at[q][:, :].rearrange("p (o k) -> p o k", o=1), w.get_from[:, bass.ds(t, 1), :]).then_inc(staged, 1)

            for q in range(2):
                stage(q, q)
            with dve.Fori(0, B) as b:
                with dve.Fori(0, TB // 2) as gb:
                    g = b * (TB // 2) + gb
                    for q in range(2):
                        t = g * 2 + q
                        dve.wait_ge(got[q], 16 * K0 * g + 16 * K0)
                        p4 = lambda k: w.gate4[:, bass.ds(t, 1), k:k + 1].rearrange("p a b -> p (a b)")
                        y1 = lambda k: y[q][:, k:k + 1, :]
                        dve.tensor_scalar(acc[q][:, :, :], y1(0), p4(0), None, ALU.mult).then_inc(summed, 1)
                        for k in range(1, K0):
                            dve.wait_ge(summed, ONE + K0 * t + k)
                            dve.scalar_tensor_tensor(acc[q][:, :, :], y1(k), p4(k), acc[q][:, :, :], op0=ALU.mult, op1=ALU.add).then_inc(summed, 1)
                        dve.wait_ge(summed, ONE + K0 * t + K0)
                        stage_t = t + 2
                        dve.tensor_copy(at[q][:, :].rearrange("p (o k) -> p o k", o=1), w.get_from[:, bass.ds(stage_t, 1), :]).then_inc(staged, 1)
                        dve.tensor_tensor(acc[q][:, :, :], acc[q][:, :, :], w.modrow[0][:, bass.ds(b, 1), GB * D:(GB + 1) * D], ALU.mult).then_inc(scaled, 1)
                        dve.wait_ge(scaled, ONE + t + 1)
                        xs = w.x[:, bass.ds(t, 1), :]
                        dve.tensor_tensor(xs, xs, acc[q][:, :, :], ALU.add).then_inc(added, 1)

        @block.sync
        def _(sp):
            with sp.Fori(0, NT // 4) as g:
                sp.wait_ge(added, ONE + g * 4 + 4)
                sp.dma_start(w.x2_dram[bass.ds(g * 4 * P, 4 * P), :].rearrange("(t p) n -> p t n", p=P), w.x[:, bass.ds(g * 4, 4), :]).then_inc(stored, 16)
            sp.wait_ge(stored, ONE + 16 * (NT // 4))


MAP = 1024
BLOCK, SEG, DIL = 64, 64, 4
NK = SEG // DIL
U = MAP // P + 1
UK = 3
TPT = 3


def stage_gather(nc, w):
    with ExitStack() as ctx:
        sem = lambda name: semaphore(nc, ctx, name)
        loaded, step, made = sem("i_loaded"), sem("i_step"), sem("i_made")
        key_at_ready, keys_got, all_ready, got = sem("i_key_at_ready"), gpsimd_dma_semaphore(nc, ctx, "i_keys_got"), sem("i_all_ready"), gpsimd_dma_semaphore(nc, ctx, "i_got")
        first = sbuf(nc, ctx, "i_first", [P, UK], I32)
        offs = sbuf(nc, ctx, "i_offs", [P, 1], I32)
        key_at = sbuf(nc, ctx, "i_key_at", [P, UK], I32)
        keys = sbuf(nc, ctx, "i_keys", [P, UK], I32)
        index = sbuf(nc, ctx, "i_index", [P, B, U + UK], I32)
        block = start(nc, ctx)
        m = w.a['L1_attn_mapping']
        by_block = m.rearrange("(n r) -> n r", r=BLOCK)
        last = m[MAP - 1:MAP].rearrange("(n r) -> n r", r=1)
        NBT = P // NK

        @block.sync
        def _(sp):
            sp.dma_start(index[:, 0, 0:U - 1], m.rearrange("(u p) -> p u", p=P), allow_slow_non_contiguous=True).then_inc(loaded, 16)
            sp.dma_start(index[:, 0, U - 1:U], last.broadcast_to([P, 1])).then_inc(loaded, 16)
            for j in range(UK - 1):
                for i in range(NBT):
                    n = j * NBT + i
                    sp.dma_start(first[i * NK:(i + 1) * NK, j:j + 1], by_block[n:n + 1, 0:1].broadcast_to([NK, 1])).then_inc(loaded, 16)
            sp.dma_start(first[:, UK - 1:UK], last.broadcast_to([P, 1])).then_inc(loaded, 16)

        @block.gpsimd
        def _(pool):
            pool.iota(offs[:, :], [[0, 1]], base=0, channel_multiplier=1).then_inc(made, 1)
            pool.wait_ge(key_at_ready, ONE + 1)
            for j in range(UK):
                pool.indirect_dma_start(out=keys[:, j:j + 1], out_offset=None, in_=m.rearrange("(n o) -> n o", o=1),
                                        in_offset=bass.IndirectOffsetOnAxis(ap=key_at[:, j:j + 1], axis=0)).then_inc(keys_got, 16)
            pool.wait_ge(all_ready, ONE + 1)
            for b in range(B):
                for u in range(U + UK):
                    pool.indirect_dma_start(out=w.xg[:, b * (U + UK) + u, :], out_offset=None, in_=w.x2_dram[:, :],
                                            in_offset=bass.IndirectOffsetOnAxis(ap=index[:, b, u:u + 1], axis=0)).then_inc(got, 16)
            pool.wait_ge(got, 16 * B * (U + UK))

        @block.vector
        def _(dve):
            link = linker(dve, step)
            dve.wait_ge(made, ONE + 1)
            link(dve.tensor_scalar(offs[:, :], offs[:, :], NK - 1, DIL.bit_length() - 1, ALU.bitwise_and, ALU.logical_shift_left))
            dve.wait_ge(loaded, ONE + 16 * (3 + (UK - 1) * NBT))
            link(dve.tensor_scalar(key_at[:, :], first[:, :], -SEG, None, ALU.bitwise_and))
            link(dve.tensor_tensor(key_at[:, :], key_at[:, :], offs[:, :].broadcast_to([P, UK]), ALU.add))
            link(dve.tensor_scalar_min(key_at[:, :], key_at[:, :], float(MAP - 1)))
            dve.sem_inc(key_at_ready, 1)
            dve.wait_ge(keys_got, 16 * UK)
            link(dve.tensor_copy(index[:, 0, U:U + UK], keys[:, :]))
            for b in range(1, B):
                link(dve.tensor_scalar_add(index[:, b, :], index[:, 0, :], float(b * S)))
            dve.sem_inc(all_ready, 1)


def stage_keys(nc, w):
    with ExitStack() as ctx:
        sem = lambda name: semaphore(nc, ctx, name)
        norm_ready, turned, hk_ready, projected, kT_ready, made, step = (
            sem(f"k_{n}") for n in ("norm_ready", "turned", "hk_ready", "projected", "kT_ready", "made", "step"))
        loaded = sem("k_loaded")
        xn = sbuf(nc, ctx, "k_xn", [P, UK, D])
        pT = psum(nc, ctx, "k_pT", [P, KD, CH])
        pk = psum(nc, ctx, "k_pk", [P, KD, CH])
        block = start(nc, ctx)
        R = U * 2 * NK

        @block.sync
        def _(sp):
            sp.dma_start(w.Wqkv1[:, :, :], w.a['L1_attn_Wqkv'].rearrange("(k p) n -> p k n", p=P)).then_inc(loaded, 16)
            sp.dma_start(w.Wproj1[:, :, :], w.a['L1_attn_Wproj'].rearrange("(k p) n -> p k n", p=P)).then_inc(loaded, 16)
            sp.dma_start(w.bqk1[:, :], w.a['L1_attn_bqkv'][0:2 * D].rearrange("(c p) -> p c", p=P), allow_slow_non_contiguous=True).then_inc(loaded, 16)
            sp.dma_start(w.bv1[:, :], w.a['L1_attn_bqkv'][2 * D:3 * D].rearrange("(o n) -> o n", o=1).broadcast_to([P, D])).then_inc(loaded, 16)
            sp.dma_start(w.bo1[:, :], w.a['L1_attn_bproj'].rearrange("(o n) -> o n", o=1).broadcast_to([P, D])).then_inc(loaded, 16)

        @block.gpsimd
        def _(pool):
            pool.memset(w.own[:, :], 1.0).then_inc(made, 1)
            pool.wait_ge(made, ONE + 1)
            pool.affine_select(out=w.own[:, :], in_=w.own[:, :], compare_op=ALU.is_ge, fill=0.0, base=0,
                               pattern=[[-NK, P // NK]], channel_multiplier=1).then_inc(made, 1)
            pool.wait_ge(made, ONE + 2)
            pool.affine_select(out=w.own[:, :], in_=w.own[:, :], compare_op=ALU.is_ge, fill=0.0, base=NK - 1,
                               pattern=[[NK, P // NK]], channel_multiplier=-1).then_inc(made, 1)
            pool.wait_ge(made, ONE + 3)

        @block.vector
        def _(dve):
            link = linker(dve, step)
            for b in range(B):
                if b:
                    dve.wait_ge(turned, ONE + b)
                for j in range(UK):
                    i = b * (U + UK) + U + j
                    last = dve.tensor_scalar(xn[:, j, :], w.xg[:, i, :], w.mean_var[:, i, 0:1], w.rstd[:, i:i + 1], ALU.subtract, ALU.mult)
                last.then_inc(norm_ready, 1)
            dve.wait_ge(loaded, ONE + 80)
            link(dve.tensor_scalar_mul(w.bqk1[:, 0:KD], w.bqk1[:, 0:KD], w.SCALE))
            dve.wait_ge(made, ONE + 3)
            link(dve.tensor_copy(w.own_square[:, :].rearrange("p (h d) -> p h d", d=DH), w.own[:, :].rearrange("p (h o) -> p h o", o=1).broadcast_to([P, P // DH, DH])))
            for b in range(B):
                link(dve.tensor_tensor(w.gbo1[:, b, :], w.modrow[1][:, b, GA * D:(GA + 1) * D], w.bo1[:, :], ALU.mult))

        @block.tensor
        def _(pe):
            for b in range(B):
                pe.wait_ge(norm_ready, ONE + b + 1)
                if b:
                    pe.wait_ge(hk_ready, ONE + KD * b)
                for j in range(UK):
                    for k in range(KD):
                        last = pe.transpose(pT[:, k, j * P:(j + 1) * P], xn[:, j, k * P:(k + 1) * P], w.ident[:, :])
                last.then_inc(turned, 1)
                pe.wait_ge(hk_ready, ONE + KD * b + KD)
                if not b:
                    pe.wait_ge(loaded, ONE + 80)
                else:
                    pe.wait_ge(kT_ready, ONE + KD * b)
                for f in range(KD):
                    for k in range(KD):
                        last = pe.matmul(pk[:, f, 0:R], w.Wqkv1[:, k, D + f * P:D + (f + 1) * P], w.hk[:, k, b, 0:R], start=k == 0, stop=k == KD - 1)
                last.then_inc(projected, 1)

        @block.scalar
        def _(act):
            for b in range(B):
                act.wait_ge(turned, ONE + b + 1)
                for k in range(KD):
                    act.activation(w.hk[:, k, b, :], pT[:, k, 0:UK * P], ACT.Identity, scale=w.modcol[:, 1, 2 * CA + k, b:b + 1],
                                   bias=w.modcol[:, 1, 2 * SA + k, b:b + 1]).then_inc(hk_ready, 1)
                act.wait_ge(projected, ONE + b + 1)
                for f in range(KD):
                    act.activation(w.kT[:, f, b, :], pk[:, f, 0:R], ACT.Identity, bias=w.bqk1[:, KD + f:KD + f + 1]).then_inc(kT_ready, 1)


def stage_blocks(nc, w):
    with ExitStack() as ctx:
        sem = lambda name: semaphore(nc, ctx, name)
        s = World()
        s.norm_ready = sem("l_norm_ready")
        s.turned = sem("l_turned")
        s.hT_ready = sem("l_hT_ready")
        s.projected = sem("l_projected")
        s.q_ready = sem("l_q_ready")
        s.kd_ready = sem("l_kd_ready")
        s.scored = sem("l_scored")
        s.top_ready = sem("l_top_ready")
        s.less_ready = sem("l_less_ready")
        s.exp_ready = sem("l_exp_ready")
        s.eps_ready = sem("l_eps_ready")
        s.inverse_ready = sem("l_inverse_ready")
        s.total_ready = sem("l_total_ready")
        s.rep_ready = sem("l_rep_ready")
        s.v_ready = sem("l_v_ready")
        s.vb_ready = sem("l_vb_ready")
        s.vd_ready = sem("l_vd_ready")
        s.summed = sem("l_summed")
        s.oT_ready = sem("l_oT_ready")
        s.out_ready = sem("l_out_ready")
        s.gated = sem("l_gated")
        s.kept = sem("l_kept")
        GH = P // NK
        xn = sbuf(nc, ctx, "l_xn", [P, TPT, D])
        hT = sbuf(nc, ctx, "l_hT", [P, KD, TPT * P])
        qT = sbuf(nc, ctx, "l_qT", [P, KD, TPT * P])
        kd = sbuf(nc, ctx, "l_kd", [P, KD, TPT * 2, GH, NK])
        hr = sbuf(nc, ctx, "l_hr", [P, KD, TPT * 2, GH, NK])
        sc = sbuf(nc, ctx, "l_sc", [P, KD, TPT * P])
        top = sbuf(nc, ctx, "l_top", [P, KD, TPT * 2])
        tot = sbuf(nc, ctx, "l_tot", [P, KD, TPT * P])
        vb = sbuf(nc, ctx, "l_vb", [P, TPT * 2, D])
        vd = sbuf(nc, ctx, "l_vd", [P, TPT * 2, D])
        oT = sbuf(nc, ctx, "l_oT", [P, KD, TPT * P])
        gate = sbuf(nc, ctx, "l_gate", [P, TPT, D])
        pa = psum(nc, ctx, "l_pa", [P, 2, CH])
        pb = psum(nc, ctx, "l_pb", [P, 2, CH])
        pv = psum(nc, ctx, "l_pv", [P, TPT * 2, D])
        block = start(nc, ctx)
        wide = lambda t: t[:, :, :].rearrange("p a n -> p (a n)")[:, 0:TPT * D]
        TURNS = U // TPT

        @block.vector
        def _(dve):
            with dve.Fori(0, B) as b:
                with dve.Fori(0, TURNS) as j:
                    n = b * TURNS + j
                    dve.wait_ge(s.turned, ONE + n)
                    for u in range(TPT):
                        i = b * (U + UK) + j * TPT + u
                        last = dve.tensor_scalar(xn[:, u:u + 1, :], w.xg[:, bass.ds(i, 1), :], w.mean_var[:, bass.ds(i, 1), 0:1].rearrange("p a b -> p (a b)"),
                                                 w.rstd[:, bass.ds(i, 1)], ALU.subtract, ALU.mult)
                    last.then_inc(s.norm_ready, 1)
                    keys = bass.ds(j * TPT * 2 * NK, TPT * 2 * NK)
                    own = w.own[:, :].rearrange("p (o h q) -> p o h q", o=1, q=1).broadcast_to([P, TPT * 2, GH, NK])
                    for k in range(KD):
                        dve.tensor_tensor(kd[:, k, :, :, :], w.kT[:, k, bass.ds(b, 1), keys].rearrange("p a (n o r) -> p (a n) o r", o=1, r=NK).broadcast_to([P, TPT * 2, GH, NK]),
                                          own, ALU.mult).then_inc(s.kd_ready, 1)
                        dve.tensor_copy(hr[:, k, :, :, :], w.hk[:, k, bass.ds(b, 1), keys].rearrange("p a (n o r) -> p (a n) o r", o=1, r=NK).broadcast_to([P, TPT * 2, GH, NK])).then_inc(s.rep_ready, 1)
                    dve.wait_ge(s.scored, ONE + n + 1)
                    by_block = lambda v: v[:, :, 0:TPT * P].rearrange("p k (m q) -> p k m q", q=BLOCK)
                    over = top[:, :, :].rearrange("p k (m o) -> p k m o", o=1).broadcast_to([P, KD, TPT * 2, BLOCK])
                    dve.reduce_max(top[:, :, :], by_block(pb), AX).then_inc(s.top_ready, 1)
                    dve.wait_ge(s.top_ready, ONE + n + 1)
                    dve.tensor_tensor(by_block(sc), by_block(pb), over, ALU.subtract).then_inc(s.less_ready, 1)
                    dve.wait_ge(s.v_ready, ONE + n + 1)
                    dve.tensor_tensor(vb[:, :, :], pv[:, :, :], w.bv1[:, :].rearrange("p (o n) -> p o n", o=1).broadcast_to([P, TPT * 2, D]), ALU.add).then_inc(s.vb_ready, 1)
                    dve.wait_ge(s.vb_ready, ONE + n + 1)
                    for k in range(KD):
                        cols = lambda v: v[:, :, k * P:(k + 1) * P].rearrange("p m (h d) -> p m h d", d=DH)
                        dve.tensor_tensor(cols(vd), cols(vb), own, ALU.mult).then_inc(s.vd_ready, 1)
                    dve.wait_ge(s.total_ready, ONE + n + 1)
                    dve.tensor_scalar_add(tot[:, :, :], pa[:, :, 0:TPT * P], 1e-6).then_inc(s.eps_ready, 1)
                    dve.wait_ge(s.eps_ready, ONE + n + 1)
                    dve.reciprocal(tot[:, :, :], tot[:, :, :]).then_inc(s.inverse_ready, 1)
                    dve.wait_ge(s.inverse_ready, ONE + n + 1)
                    dve.wait_ge(s.summed, ONE + n + 1)
                    dve.tensor_tensor(oT[:, :, :], pb[:, :, 0:TPT * P], tot[:, :, :], ALU.mult).then_inc(s.oT_ready, 1)
                    dve.wait_ge(s.out_ready, ONE + n + 1)
                    dve.tensor_tensor(gate[:, :, :], wide(pa).rearrange("p (t n) -> p t n", t=TPT),
                                      w.modrow[1][:, bass.ds(b, 1), GA * D:(GA + 1) * D].broadcast_to([P, TPT, D]), ALU.mult).then_inc(s.gated, 1)
                    dve.wait_ge(s.gated, ONE + n + 1)
                    dve.tensor_tensor(w.att1[:, bass.ds(n * TPT, TPT), :], gate[:, :, :], w.gbo1[:, bass.ds(b, 1), :].broadcast_to([P, TPT, D]), ALU.add).then_inc(s.kept, 1)
            for b in range(B):
                if b == 0:
                    dve.wait_ge(s.kept, ONE + B * TURNS)
                t0, a0 = b * TB, b * U
                for x, y in ((w.x[:, t0:t0 + U - 1, :], w.att1[:, a0:a0 + U - 1, :]),
                             (w.x[:, t0 + U - 1:t0 + TB, :], w.att1[:, a0 + U - 1:a0 + U, :].broadcast_to([P, TB - U + 1, D]))):
                    dve.tensor_tensor(x, x, y, ALU.add)

        @block.tensor
        def _(pe):
            with pe.Fori(0, B * TURNS) as n:
                pe.wait_ge(s.norm_ready, ONE + n + 1)
                pe.wait_ge(s.gated, ONE + n)
                for u in range(TPT):
                    for k in range(KD):
                        last = pe.transpose(pa[:, k, u * P:(u + 1) * P], xn[:, u, k * P:(k + 1) * P], w.ident[:, :])
                last.then_inc(s.turned, 1)
                pe.wait_ge(s.rep_ready, ONE + KD * n + KD)
                pe.wait_ge(s.vb_ready, ONE + n)
                for m in range(TPT * 2):
                    for k in range(KD):
                        last = pe.matmul(pv[:, m, :], hr[:, k, m, :, :], w.Wqkv1[:, k, 2 * D:3 * D], start=k == 0, stop=k == KD - 1)
                last.then_inc(s.v_ready, 1)
                pe.wait_ge(s.hT_ready, ONE + KD * n + KD)
                pe.wait_ge(s.oT_ready, ONE + n)
                for f in range(KD):
                    for k in range(KD):
                        last = pe.matmul(pb[:, f, 0:TPT * P], w.Wqkv1[:, k, f * P:(f + 1) * P], hT[:, k, :], start=k == 0, stop=k == KD - 1)
                last.then_inc(s.projected, 1)
                pe.wait_ge(s.q_ready, ONE + KD * n + KD)
                pe.wait_ge(s.kd_ready, ONE + KD * n + KD)
                for k in range(KD):
                    for m in range(TPT * 2):
                        at = slice(m * BLOCK, (m + 1) * BLOCK)
                        last = pe.matmul(pb[:, k, at], kd[:, k, m, :, :], qT[:, k, at], start=True, stop=True)
                last.then_inc(s.scored, 1)
                pe.wait_ge(s.exp_ready, ONE + n + 1)
                for k in range(KD):
                    last = pe.matmul(pa[:, k, 0:TPT * P], w.own_square[:, :], sc[:, k, :], start=True, stop=True)
                last.then_inc(s.total_ready, 1)
                pe.wait_ge(s.vd_ready, ONE + KD * n + KD)
                for k in range(KD):
                    for m in range(TPT * 2):
                        at = slice(m * BLOCK, (m + 1) * BLOCK)
                        last = pe.matmul(pb[:, k, at], vd[:, m, k * P:(k + 1) * P], sc[:, k, at], start=True, stop=True)
                last.then_inc(s.summed, 1)
                pe.wait_ge(s.oT_ready, ONE + n + 1)
                for u in range(TPT):
                    for k in range(KD):
                        last = pe.matmul(wide(pa)[:, u * D:(u + 1) * D], oT[:, k, u * P:(u + 1) * P], w.Wproj1[:, k, :], start=k == 0, stop=k == KD - 1)
                last.then_inc(s.out_ready, 1)

        @block.scalar
        def _(act):
            with act.Fori(0, B) as b:
                with act.Fori(0, TURNS) as j:
                    n = b * TURNS + j
                    wait_alone(w, act, s.turned, ONE + n + 1)
                    for k in range(KD):
                        act.activation(hT[:, k, :], pa[:, k, 0:TPT * P], ACT.Identity, scale=w.modcol[:, 1, 2 * CA + k, bass.ds(b, 1)],
                                       bias=w.modcol[:, 1, 2 * SA + k, bass.ds(b, 1)]).then_inc(s.hT_ready, 1)
                    act.wait_ge(s.projected, ONE + n + 1)
                    for f in range(KD):
                        act.activation(qT[:, f, :], pb[:, f, 0:TPT * P], ACT.Identity, scale=w.SCALE, bias=w.bqk1[:, f:f + 1]).then_inc(s.q_ready, 1)
                    act.wait_ge(s.less_ready, ONE + n + 1)
                    act.activation(sc[:, :, :], sc[:, :, :], ACT.Exp).then_inc(s.exp_ready, 1)


E1, K1, I1 = 8, 2, 512


def stage_gates(nc, w):
    with ExitStack() as ctx:
        sem = lambda name: semaphore(nc, ctx, name)
        step, exp_request, exp_done, made = sem("t_step"), sem("t_exp_request"), sem("t_exp_done"), sem("t_made")
        cols_ready, turned, rows_ready, stored = sem("t_cols_ready"), sem("t_turned"), sem("t_rows_ready"), sem("t_stored")
        N = NT * K1
        top = sbuf(nc, ctx, "t_top", [P, NT])
        total = sbuf(nc, ctx, "t_total", [P, NT])
        m8 = sbuf(nc, ctx, "t_m8", [P, NT, 8])
        i8 = sbuf(nc, ctx, "t_i8", [P, NT, 8], U32)
        i2 = sbuf(nc, ctx, "t_i2", [P, N])
        col_i = sbuf(nc, ctx, "t_col_i", [P, E1], I32)
        col = sbuf(nc, ctx, "t_col", [P, E1])
        chosen = sbuf(nc, ctx, "t_chosen", [P, N, E1])
        both = sbuf(nc, ctx, "t_both", [P, NT, 2 * E1])
        rows = sbuf(nc, ctx, "t_rows", [2 * E1, NT, P])
        pr = psum(nc, ctx, "t_pr", [2 * E1, NT, P])
        block = start(nc, ctx)

        @block.gpsimd
        def _(pool):
            pool.iota(col_i[:, :], [[1, E1]], base=0, channel_multiplier=0).then_inc(made, 1)

        @block.scalar
        def _(act):
            act.wait_ge(exp_request, ONE + 1)
            act.activation(w.logits1[:, :, :], w.logits1[:, :, :], ACT.Exp).then_inc(exp_done, 1)

        @block.vector
        def _(dve):
            link = linker(dve, step)
            probs = w.logits1
            softmax_rows(dve, link, probs, top, total, exp_request, exp_done)
            for t in range(NT):
                last = dve.max(m8[:, t, :], probs[:, t, :])
            link(last)
            for t in range(NT):
                last = dve.max_index(i8[:, t, :], m8[:, t, :], probs[:, t, :])
            link(last)
            link(dve.tensor_copy(i2[:, :].rearrange("p (t k) -> p t k", k=K1), i8[:, :, 0:K1]))
            dve.wait_ge(made, ONE + 1)
            link(dve.tensor_copy(col[:, :], col_i[:, :]))
            link(dve.tensor_tensor(chosen[:, :, :], col[:, :].rearrange("p (o e) -> p o e", o=1).broadcast_to([P, N, E1]),
                                   i2[:, :].rearrange("p (n o) -> p n o", o=1).broadcast_to([P, N, E1]), ALU.is_equal))
            by_k = chosen[:, :, :].rearrange("p (t k) e -> p t k e", k=K1)
            dve.tensor_copy(both[:, :, 0:E1], probs[:, :, :])
            link(dve.tensor_tensor(both[:, :, E1:2 * E1], by_k[:, :, 0, :], by_k[:, :, 1, :], ALU.add))
            dve.sem_inc(cols_ready, 1)
            dve.wait_ge(turned, ONE + 1)
            dve.tensor_copy(rows[:, :, :], pr[:, :, :]).then_inc(rows_ready, 1)

        @block.tensor
        def _(pe):
            pe.wait_ge(cols_ready, ONE + 1)
            for t in range(NT):
                last = pe.transpose(pr[:, t, :], both[:, t, :], w.ident[:, :])
            last.then_inc(turned, 1)

        @block.sync
        def _(sp):
            sp.wait_ge(rows_ready, ONE + 1)
            sp.dma_start(w.gates_dram[:, :], rows[:, :, :].rearrange("e t p -> e (t p)")).then_inc(stored, 16)
            sp.wait_ge(stored, ONE + 16)


def stage_shared(nc, w):
    with ExitStack() as ctx:
        sem = lambda name: semaphore(nc, ctx, name)
        loaded, a_ready, b_ready, silu_ready, u_ready, z_ready, z_out = (
            sem(f"z_{n}") for n in ("loaded", "a_ready", "b_ready", "silu_ready", "u_ready", "z_ready", "z_out"))
        IB = I1 // P
        W1 = sbuf(nc, ctx, "z_W1", [P, KD, I1])
        W2 = sbuf(nc, ctx, "z_W2", [P, KD, I1])
        W3 = sbuf(nc, ctx, "z_W3", [P, IB, D])
        si = sbuf(nc, ctx, "z_si", [P, IB, CH])
        u = sbuf(nc, ctx, "z_u", [P, IB, CH])
        pa = psum(nc, ctx, "z_pa", [P, 2, CH])
        pb = psum(nc, ctx, "z_pb", [P, 2, CH])
        pz = psum(nc, ctx, "z_pz", [P, KD, CH])
        block = start(nc, ctx)

        @block.sync
        def _(sp):
            for dst, name in ((W1, 'L1_ffn_sw1'), (W2, 'L1_ffn_sw2'), (W3, 'L1_ffn_sw3')):
                sp.dma_start(dst[:, :, :], w.a[name].rearrange("(k p) n -> p k n", p=P)).then_inc(loaded, 16)

        @block.tensor
        def _(pe):
            pe.wait_ge(loaded, ONE + 48)
            with pe.Fori(0, NC) as c:
                h = lambda k: w.hT1[:, k, bass.ds(c * CH, CH)]
                for i in range(IB):
                    if i < 2:
                        pe.wait_ge(u_ready, ONE + IB * c)
                    else:
                        pe.wait_ge(u_ready, ONE + IB * c + i - 1)
                    for k in range(KD):
                        last = pe.matmul(pa[:, i % 2, :], W1[:, k, i * P:(i + 1) * P], h(k), start=k == 0, stop=k == KD - 1)
                    last.then_inc(a_ready, 1)
                    for k in range(KD):
                        last = pe.matmul(pb[:, i % 2, :], W2[:, k, i * P:(i + 1) * P], h(k), start=k == 0, stop=k == KD - 1)
                    last.then_inc(b_ready, 1)
                pe.wait_ge(u_ready, ONE + IB * c + IB)
                pe.wait_ge(z_out, ONE + c)
                for f in range(KD):
                    for i in range(IB):
                        last = pe.matmul(pz[:, f, :], W3[:, i, f * P:(f + 1) * P], u[:, i, :], start=i == 0, stop=i == IB - 1)
                last.then_inc(z_ready, 1)

        @block.scalar
        def _(act):
            with act.Fori(0, NC) as c:
                act.wait_ge(u_ready, ONE + IB * c)
                for i in range(IB):
                    act.wait_ge(a_ready, ONE + IB * c + i + 1)
                    act.activation(si[:, i, :], pa[:, i % 2, :], ACT.Silu).then_inc(silu_ready, 1)

        @block.vector
        def _(dve):
            with dve.Fori(0, NC) as c:
                dve.wait_ge(z_ready, ONE + c)
                for i in range(IB):
                    dve.wait_ge(silu_ready, ONE + IB * c + i + 1)
                    dve.wait_ge(b_ready, ONE + IB * c + i + 1)
                    dve.tensor_tensor(u[:, i, :], si[:, i, :], pb[:, i % 2, :], ALU.mult).then_inc(u_ready, 1)
                dve.wait_ge(z_ready, ONE + c + 1)
                dve.tensor_copy(w.yT[:, :, bass.ds(c * CH, CH)], pz[:, :, :]).then_inc(z_out, 1)


def stage_experts1(nc, w):
    with ExitStack() as ctx:
        sem = lambda name: semaphore(nc, ctx, name)
        biases_loaded = sem("y_biases_loaded")
        w_loaded = [sem(f"y_w_loaded{q}") for q in range(2)]
        g_loaded = [sem(f"y_g_loaded{q}") for q in range(2)]
        xs_ready, p1_ready, p3_ready, silu_ready, x3_ready, p2_ready, t_ready, y_added = (
            sem(f"y_{n}") for n in ("xs_ready", "p1_ready", "p3_ready", "silu_ready", "x3_ready", "p2_ready", "t_ready", "y_added"))
        W = [[sbuf(nc, ctx, f"y_W{i}{q}", [P, KD, D]) for i in (1, 2, 3)] for q in range(2)]
        bias = sbuf(nc, ctx, "y_bias", [P, 3, KD, E1])
        score = [sbuf(nc, ctx, f"y_score{q}", [P, 1, CH]) for q in range(2)]
        mask = [sbuf(nc, ctx, f"y_mask{q}", [P, 1, CH]) for q in range(2)]
        xs = [sbuf(nc, ctx, f"y_xs{q}", [P, KD, CH]) for q in range(2)]
        hh = sbuf(nc, ctx, "y_hh", [P, KD, CH])
        x3 = sbuf(nc, ctx, "y_x3", [P, KD, CH])
        tt = [sbuf(nc, ctx, f"y_tt{q}", [P, KD, CH]) for q in range(2)]
        p1 = psum(nc, ctx, "y_p1", [P, KD, CH])
        p2 = psum(nc, ctx, "y_p2", [P, KD, CH])
        p3 = psum(nc, ctx, "y_p3", [P, KD, CH])
        block = start(nc, ctx)
        a = w.a

        @block.sync
        def _(sp):
            for i, name in enumerate(('L1_ffn_b1', 'L1_ffn_b2', 'L1_ffn_b3')):
                sp.dma_start(bias[:, i, :, :], a[name].rearrange("(k p) e -> p k e", p=P)).then_inc(biases_loaded, 16)
            with sp.Fori(0, E1 // 2) as g:
                for eq in range(2):
                    e = g * 2 + eq
                    sp.wait_ge(p2_ready, ONE + g * (2 * NC))
                    for i, name in enumerate(('L1_ffn_w1', 'L1_ffn_w2', 'L1_ffn_w3')):
                        sp.dma_start(W[eq][i][:, :, :], a[name][bass.ds(e, 1), :, :].rearrange("o (k p) n -> p (o k) n", p=P)).then_inc(w_loaded[eq], 16)
                    with sp.Fori(0, NC // 2) as cg:
                        for q in range(2):
                            n = e * NC + cg * 2 + q
                            wait_alone(w, sp, xs_ready, ONE + n - q)
                            sp.wait_ge(x3_ready, ONE + KD * (n - q))
                            cols = bass.ds(cg * (2 * CH) + q * CH, CH)
                            sp.dma_start(score[q][:, 0, :], w.gates_dram[bass.ds(e, 1), cols].broadcast_to([P, CH])).then_inc(g_loaded[q], 16)
                            sp.dma_start(mask[q][:, 0, :], w.gates_dram[bass.ds(e + E1, 1), cols].broadcast_to([P, CH])).then_inc(g_loaded[q], 16)

        @block.tensor
        def _(pe):
            with pe.Fori(0, E1 // 2) as g:
                for eq in range(2):
                    wait_alone(w, pe, w_loaded[eq], ONE + 48 * g + 48)
                    with pe.Fori(0, NC // 2) as cg:
                        for q in range(2):
                            n = (g * 2 + eq) * NC + cg * 2 + q
                            pe.wait_ge(xs_ready, ONE + n + 1)
                            pe.wait_ge(silu_ready, ONE + KD * n)
                            for f in range(KD):
                                for k in range(KD):
                                    last = pe.matmul(p1[:, f, :], W[eq][0][:, k, f * P:(f + 1) * P], xs[q][:, k, :], start=k == 0, stop=k == KD - 1)
                                last.then_inc(p1_ready, 1)
                            pe.wait_ge(x3_ready, ONE + KD * n)
                            for f in range(KD):
                                for k in range(KD):
                                    last = pe.matmul(p3[:, f, :], W[eq][2][:, k, f * P:(f + 1) * P], xs[q][:, k, :], start=k == 0, stop=k == KD - 1)
                                last.then_inc(p3_ready, 1)
                            pe.wait_ge(silu_ready, ONE + KD * n + KD)
                            pe.wait_ge(t_ready, ONE + KD * n)
                            for f in range(KD):
                                for k in range(KD):
                                    last = pe.matmul(p2[:, f, :], W[eq][1][:, k, f * P:(f + 1) * P], hh[:, k, :], start=k == 0, stop=k == KD - 1)
                                if f == KD - 1:
                                    last.then_inc(p2_ready, 1)

        @block.scalar
        def _(act):
            act.wait_ge(biases_loaded, ONE + 48)
            with act.Fori(0, E1) as e:
                with act.Fori(0, NC) as c:
                    n = e * NC + c
                    wait_alone(w, act, p2_ready, ONE + n)
                    for f in range(KD):
                        wait_alone(w, act, p1_ready, ONE + KD * n + f + 1)
                        act.activation(hh[:, f, :], p1[:, f, :], ACT.Silu, bias=bias[:, 0, f, bass.ds(e, 1)]).then_inc(silu_ready, 1)

        @block.vector
        def _(dve):
            dve.wait_ge(biases_loaded, ONE + 48)
            with dve.Fori(0, E1) as e:
                with dve.Fori(0, NC // 2) as cg:
                    for q in range(2):
                        n = e * NC + cg * 2 + q
                        dve.wait_ge(g_loaded[q], ONE + e * (16 * NC) + cg * 32 + 32)
                        if q == 0:
                            dve.wait_ge(p3_ready, ONE + KD * n)
                        else:
                            dve.wait_ge(p3_ready, ONE + KD * (n - 1))
                        c = cg * 2 + q
                        dve.tensor_tensor(xs[q][:, :, :], w.hT1[:, :, bass.ds(c * CH, CH)], score[q][:, :, :].broadcast_to([P, KD, CH]), ALU.mult).then_inc(xs_ready, 1)
                        for f in range(KD):
                            dve.wait_ge(p3_ready, ONE + KD * n + f + 1)
                            if f == 0:
                                dve.wait_ge(t_ready, ONE + KD * n)
                            dve.scalar_tensor_tensor(x3[:, f, :], p3[:, f, :], bias[:, 2, f, bass.ds(e, 1)], mask[q][:, 0, :], op0=ALU.add, op1=ALU.mult).then_inc(x3_ready, 1)
                        dve.wait_ge(p2_ready, ONE + n + 1)
                        dve.wait_ge(x3_ready, ONE + KD * n + KD)
                        dve.wait_ge(y_added, ONE + n)
                        for f in range(KD):
                            dve.scalar_tensor_tensor(tt[q][:, f, :], p2[:, f, :], bias[:, 1, f, bass.ds(e, 1)], x3[:, f, :], op0=ALU.add, op1=ALU.mult).then_inc(t_ready, 1)

        @block.gpsimd
        def _(pool):
            with pool.Fori(0, E1) as e:
                with pool.Fori(0, NC // 2) as cg:
                    for q in range(2):
                        n = e * NC + cg * 2 + q
                        pool.wait_ge(t_ready, ONE + KD * n + KD)
                        ys = w.yT[:, :, bass.ds(cg * (2 * CH) + q * CH, CH)]
                        pool.tensor_tensor(ys, ys, tt[q][:, :, :], ALU.add).then_inc(y_added, 1)


def stage_output(nc, w):
    with ExitStack() as ctx:
        sem = lambda name: semaphore(nc, ctx, name)
        staged, turned, gated, added, stored = (sem(f"o_{n}") for n in ("staged", "turned", "gated", "added", "stored"))
        ys = [sbuf(nc, ctx, f"o_ys{q}", [P, KD, CH]) for q in range(2)]
        t = [sbuf(nc, ctx, f"o_t{q}", [P, CT, D]) for q in range(2)]
        py = [psum(nc, ctx, f"o_py{q}", [P, CT, D]) for q in range(2)]
        block = start(nc, ctx)

        @block.scalar
        def _(act):
            with act.Fori(0, NC // 2) as g:
                for q in range(2):
                    wait_alone(w, act, turned, ONE + g * 2)
                    act.activation(ys[q][:, :, :], w.yT[:, :, bass.ds(g * (2 * CH) + q * CH, CH)], ACT.Copy).then_inc(staged, 1)

        @block.tensor
        def _(pe):
            with pe.Fori(0, NC // 2) as g:
                for q in range(2):
                    pe.wait_ge(staged, ONE + g * 2 + q + 1)
                    pe.wait_ge(gated, ONE + g * 2)
                    for i in range(CT):
                        for k in range(KD):
                            last = pe.transpose(py[q][:, i, k * P:(k + 1) * P], ys[q][:, k, i * P:(i + 1) * P], w.ident[:, :])
                    last.then_inc(turned, 1)

        @block.vector
        def _(dve):
            with dve.Fori(0, B) as b:
                with dve.Fori(0, NC // B // 2) as gb:
                    for q in range(2):
                        c = b * (NC // B) + gb * 2 + q
                        dve.wait_ge(turned, ONE + c + 1)
                        dve.tensor_tensor(t[q][:, :, :], py[q][:, :, :], w.modrow[1][:, bass.ds(b, 1), GB * D:(GB + 1) * D].broadcast_to([P, CT, D]), ALU.mult).then_inc(gated, 1)
                        dve.wait_ge(gated, ONE + c + 1)
                        xs = w.x[:, bass.ds(c * CT, CT), :]
                        dve.tensor_tensor(xs, xs, t[q][:, :, :], ALU.add).then_inc(added, 1)

        @block.sync
        def _(sp):
            with sp.Fori(0, NC) as c:
                sp.wait_ge(added, ONE + c + 1)
                sp.dma_start(w.out[bass.ds(c * CH, CH), :].rearrange("(t p) n -> p t n", p=P), w.x[:, bass.ds(c * CT, CT), :]).then_inc(stored, 16)
            sp.wait_ge(stored, ONE + 16 * NC)


def clear_semaphores(nc):
    with nc.semaphore("first") as s:
        first = s.num
    numbers = [first]
    while True:
        with nc.semaphore("next") as s:
            if s.num == first:
                break
            numbers.append(s.num)
    nc.all_engine_barrier()
    nc.gpsimd.sem_clear(range(min(numbers), max(numbers) + 1))
    nc.all_engine_barrier()


def build(nc, a, out, stages=99):
    w = World()
    ctx = ExitStack()
    with ctx:
        w.passed = ctx.enter_context(nc.semaphore("passed"))
        w.SCALE = DH ** -0.5
        w.EXT = 2 * REL + 1 + 2 * (P - 1)
        w.c = [a['L0_c'], a['L1_c']]
        w.wmod = [a['L0_wmod'], a['L1_wmod']]
        w.rel_biasT = a['L0_attn_rel_bias']
        w.W_qkv0, w.W_out0, w.router_w = a['L0_attn_W_qkv'], a['L0_attn_W_out'], a['L0_ffn_router_w']
        w.b_qkv0, w.b_out0 = a['L0_attn_b_qkv'], a['L0_attn_b_out']
        w.x_dram = a['L0_attn_x'].rearrange("b s d -> (b s) d")
        w.a, w.out = a, out.rearrange("b s d -> (b s) d")
        dram = lambda name, shape, dt=F32: nc.dram_tensor(name, shape, dt).ap()
        w.ext_dram = dram("ext_dram", [NH, w.EXT])
        w.far_dram = dram("far_dram", [H, 2])
        w.qk_parts = [dram(f"{n}_parts", [3, NH * DH, S], BF16) for n in "qk"]
        w.attT_dram = dram("attT_dram", [NH, DH + 1, S])
        w.BAND = 2 * REL + P
        w.skew_dram = dram("skew_dram", [NH, P * (w.EXT + 1)])
        w.xe_dram = dram("xe_dram", [E0 * CAP, D])
        w.ye_dram = dram("ye_dram", [E0 * CAP, D])
        w.x2_dram = dram("x2_dram", [B * S, D])
        w.w1_0, w.w2_0 = a['L0_ffn_w1'], a['L0_ffn_w2']
        w.gates_dram = dram("gates_dram", [2 * E1, B * S])
        w.v_dram = dram("v_dram", [NH, S, DH])
        sb = lambda name, shape, dt=F32: sbuf(nc, ctx, name, shape, dt)
        w.ident = sb("ident", [P, P])
        w.zeros = sb("zeros", [P, 2048])
        w.eps = sb("eps", [P, 1])
        w.modrow = [sb(f"modrow{l}", [P, B, 6 * D]) for l in range(2)]
        w.modcol = sb("modcol", [P, 2, 12, B])
        w.far = sb("far", [P, NH, 2])
        w.Wout0 = sb("Wout0", [P, KD, D])
        w.Wr0 = sb("Wr0", [P, KD, 64])
        w.Wg1 = sb("Wg1", [P, KD, E1])
        w.bo0 = sb("bo0", [P, D])
        w.gbo0 = sb("gbo0", [P, B, D])
        w.x = sb("x", [P, NT, D])
        with ExitStack() as qkv:
            w.Wqkv0 = sbuf(nc, qkv, "Wqkv0", [P, KD, 3 * D])
            w.bqk = sbuf(nc, qkv, "bqk", [P, 2 * KD])
            w.bv0 = sbuf(nc, qkv, "bv0", [P, D])
            stage_constants(nc, w)
            stage_qkv(nc, w)
        stage_attention(nc, w)
        stage_project(nc, w)
        w.mean_var = sb("mean_var", [P, NT, 2])
        w.rstd = sb("rstd", [P, NT])
        with ExitStack() as moe:
            w.gate4 = sbuf(nc, moe, "gate4", [P, NT, K0])
            w.put_at = sbuf(nc, moe, "put_at", [P, NT, K0], I32)
            w.get_from = sbuf(nc, moe, "get_from", [P, NT + 2, K0], I32)
            with ExitStack() as tokens:
                w.h = sbuf(nc, tokens, "h", [P, NT, D])
                w.logits0 = sbuf(nc, tokens, "logits0", [P, NT, E0])
                stage_norm(nc, w, w.x, NT, w.mean_var, w.rstd, "n0")
                stage_router(nc, w, w.x, w.mean_var, w.rstd, w.h, None, 0, w.Wr0, w.logits0, "g0")
                stage_route(nc, w)
                stage_scatter(nc, w)
            stage_experts(nc, w)
            stage_combine(nc, w)
        clear_semaphores(nc)
        with ExitStack() as att:
            w.xg = sbuf(nc, att, "xg", [P, B * (U + UK), D])
            w.att1 = sbuf(nc, att, "att1", [P, B * U, D])
            w.Wqkv1 = sbuf(nc, att, "Wqkv1", [P, KD, 3 * D])
            w.Wproj1 = sbuf(nc, att, "Wproj1", [P, KD, D])
            w.bqk1 = sbuf(nc, att, "bqk1", [P, 2 * KD])
            w.bv1 = sbuf(nc, att, "bv1", [P, D])
            w.bo1 = sbuf(nc, att, "bo1", [P, D])
            w.gbo1 = sbuf(nc, att, "gbo1", [P, B, D])
            w.own_square = sbuf(nc, att, "own_square", [P, P])
            w.own = sbuf(nc, att, "own", [P, P // NK])
            w.hk = sbuf(nc, att, "hk", [P, KD, B, UK * P])
            w.kT = sbuf(nc, att, "kT", [P, KD, B, U * 2 * NK])
            stage_gather(nc, w)
            stage_norm(nc, w, w.xg, B * (U + UK), w.mean_var, w.rstd, "n1")
            stage_keys(nc, w)
            stage_blocks(nc, w)
            if stages == 5:
                return w
        w.hT1 = sb("hT1", [P, KD, B * S])
        w.yT = sb("yT", [P, KD, B * S])
        w.logits1 = sb("logits1", [P, NT, E1])
        stage_norm(nc, w, w.x, NT, w.mean_var, w.rstd, "n2")
        stage_router(nc, w, w.x, w.mean_var, w.rstd, None, w.hT1, 1, w.Wg1, w.logits1, "g1")
        stage_gates(nc, w)
        stage_shared(nc, w)
        stage_experts1(nc, w)
        stage_output(nc, w)
    return w


_INS = ['L0_attn_x', 'L0_attn_W_qkv', 'L0_attn_b_qkv', 'L0_attn_W_out', 'L0_attn_b_out', 'L0_attn_rel_bias',
        'L0_ffn_router_w', 'L0_ffn_w1', 'L0_ffn_w2', 'L0_c', 'L0_wmod', 'L1_attn_Wqkv', 'L1_attn_bqkv',
        'L1_attn_Wproj', 'L1_attn_bproj', 'L1_attn_mapping', 'L1_ffn_gate_w', 'L1_ffn_w1', 'L1_ffn_b1',
        'L1_ffn_w2', 'L1_ffn_b2', 'L1_ffn_w3', 'L1_ffn_b3', 'L1_ffn_sw1', 'L1_ffn_sw2', 'L1_ffn_sw3', 'L1_c', 'L1_wmod']
_TURNED = {'L1_ffn_b1', 'L1_ffn_b2', 'L1_ffn_b3', 'L0_c', 'L1_c', 'L0_attn_rel_bias', 'L1_ffn_gate_w', 'L1_ffn_w1', 'L1_ffn_w2', 'L1_ffn_w3', 'L1_ffn_sw1', 'L1_ffn_sw2', 'L1_ffn_sw3'}


def kernel(**inputs):
    import numpy as _np
    import concourse.bacc as _bacc
    from concourse import mybir as _mybir
    from concourse.bass_utils import run_bass_kernel_spmd as _run

    nc = _bacc.Bacc("TRN2", target_bir_lowering=False, num_devices=1)
    arrays, args = {}, {}
    for name in _INS:
        a = _np.asarray(inputs[name])
        a = _np.ascontiguousarray(_np.swapaxes(a, -1, -2) if name in _TURNED else a)
        arrays[f"in_{name}_dram"] = a
        args[name] = nc.dram_tensor(f"in_{name}_dram", a.shape, _mybir.dt.from_np(a.dtype), kind="ExternalInput").ap()
    out = nc.dram_tensor("out_dram", (B, S, D), _mybir.dt.from_np(_np.dtype("float32")), kind="ExternalOutput").ap()
    build(nc, args, out)
    r = _run(nc, [arrays], core_ids=[0])
    return r.results[0]["out_dram"]
```

```python
import numpy as np
import concourse.bass as bass
from concourse import mybir
from contextlib import ExitStack

F32 = mybir.dt.float32
BF16 = mybir.dt.bfloat16
I32 = mybir.dt.int32
U32 = mybir.dt.uint32
ALU = mybir.AluOpType
ACT = mybir.ActivationFunctionType
AX = mybir.AxisListType.X

P = 128
B, S, D = 2, 2048, 256
NT = B * S // P
TB = S // P
KD = D // P
CH = 512
NC = B * S // CH
CT = CH // P
H, DH = 16, 16
NH = B * H
REL = 256
EPS = 1e-5
SA, CA, GA, SB_, CB, GB = range(6)
ONE = 1


class World:
    pass


def sbuf(nc, ctx, name, shape, dt=F32):
    return ctx.enter_context(nc.sbuf_tensor(name, shape, dt))


def psum(nc, ctx, name, shape, dt=F32):
    return ctx.enter_context(nc.psum_tensor(name, shape, dt))


def semaphore(nc, ctx, name):
    s = ctx.enter_context(nc.semaphore(name))
    nc.gpsimd.sem_inc(s, ONE)
    return s


def gpsimd_dma_semaphore(nc, ctx, name):
    return ctx.enter_context(nc.semaphore(name))


def start(nc, ctx):
    nc.all_engine_barrier()
    return ctx.enter_context(nc.Block())


def linker(engine, sem, first=0):
    count = [first]

    def link(instruction):
        count[0] += 1
        instruction.then_inc(sem, 1)
        engine.wait_ge(sem, ONE + count[0])

    return link


def wait_alone(w, engine, sem, value):
    engine.wait_ge(sem, value)
    engine.sem_inc(w.passed, 1)


def stage_constants(nc, w):
    with ExitStack() as ctx:
        sem = lambda name: semaphore(nc, ctx, name)
        loaded = sem("a_loaded")
        filled = sem("a_filled")
        act_step = sem("a_act_step")
        dve_step = sem("a_dve_step")
        silu_ready = sem("a_silu_ready")
        mod_ready = [sem(f"a_mod_ready{i}") for i in range(2)]
        mod_used = [sem(f"a_mod_used{i}") for i in range(2)]
        col_ready = sem("a_col_ready")
        bias_exp_in = sem("a_bias_exp_in")
        bias_exp = sem("a_bias_exp")
        bias_rows_ready = sem("a_bias_rows_ready")
        bias_stored = sem("a_bias_stored")
        far_loaded = sem("a_far_loaded")
        pool_step = sem("a_pool_step")
        map_ready = sem("a_map_ready")
        map_loaded = sem("a_map_loaded")

        cT = sbuf(nc, ctx, "cT", [P, 2, KD, B])
        ce = sbuf(nc, ctx, "ce", [P, 2, KD, B])
        sc = sbuf(nc, ctx, "sc", [P, 2, KD, B])
        wm = sbuf(nc, ctx, "wm", [P, 2, KD, 6 * D])
        rb = sbuf(nc, ctx, "rb", [H, 2 * REL + 1])
        rbm = sbuf(nc, ctx, "rbm", [H, 1])
        rbd = sbuf(nc, ctx, "rbd", [H, 2 * REL + 1])
        ext = sbuf(nc, ctx, "ext", [H, w.EXT])
        row = sbuf(nc, ctx, "row", [P, D * 2])
        kp = sbuf(nc, ctx, "kp", [P, 6], I32)
        m0 = sbuf(nc, ctx, "m0", [P, 3], I32)
        ps = [psum(nc, ctx, f"a_ps{i}", [P, CH]) for i in range(2)]
        pc = psum(nc, ctx, "a_pc", [P, 2, 12, B])
        block = start(nc, ctx)

        small = [(cT[:, l, :, :], w.c[l].rearrange("(k p) b -> p k b", p=P)) for l in range(2)]
        wmods = [(wm[:, l, :, :], w.wmod[l].rearrange("(k p) n -> p k n", p=P)) for l in range(2)]
        big = wmods + [(rb[:, :], w.rel_biasT)]
        weights = [
            (w.Wqkv0[:, :, :], w.W_qkv0.rearrange("(k p) n -> p k n", p=P)),
            (w.Wout0[:, :, :], w.W_out0.rearrange("(k p) n -> p k n", p=P)),
            (w.Wr0[:, :, :], w.router_w.rearrange("(k p) n -> p k n", p=P)),
            (w.Wg1[:, :, :], w.a['L1_ffn_gate_w'].rearrange("(k p) n -> p k n", p=P)),
            (w.bqk[:, :], w.b_qkv0[0:2 * D].rearrange("(c p) -> p c", p=P)),
            (w.bv0[:, :], w.b_qkv0[2 * D:3 * D].rearrange("(o n) -> o n", o=1).broadcast_to([P, D])),
            (w.bo0[:, :], w.b_out0.rearrange("(o n) -> o n", o=1).broadcast_to([P, D])),
        ]
        MAPS = 6

        @block.sync
        def _(sp):
            for dst, src in small + big + weights:
                sp.dma_start(dst, src, allow_slow_non_contiguous=True).then_inc(loaded, 16)
            sp.wait_ge(bias_rows_ready, ONE + 1)
            for b in range(B):
                sp.dma_start(w.ext_dram[b * H:(b + 1) * H, :], ext[:, :]).then_inc(bias_stored, 16)
            sp.dma_start(w.far_dram[:, 0:1], rbd[:, 0:1], allow_slow_non_contiguous=True).then_inc(bias_stored, 16)
            sp.dma_start(w.far_dram[:, 1:2], rbd[:, 2 * REL:2 * REL + 1], allow_slow_non_contiguous=True).then_inc(bias_stored, 16)
            sp.wait_ge(bias_stored, ONE + 64)
            for b in range(B):
                sp.dma_start(w.far[:, b * H:(b + 1) * H, :], w.far_dram.rearrange("h (o t) -> o h t", o=1).broadcast_to([P, H, 2])).then_inc(far_loaded, 16)
            sp.wait_ge(far_loaded, ONE + 32)

        @block.scalar
        def _(act):
            act.wait_ge(loaded, ONE + 16 * len(small + big + weights))
            act.activation(ce[:, :, :, :], cT[:, :, :, :], ACT.Exp, scale=-1.0).then_inc(act_step, 1)
            act.wait_ge(bias_exp_in, ONE + 1)
            act.activation(ext[:, P - 1:P + 2 * REL], rbd[:, :], ACT.Exp).then_inc(bias_exp, 1)

        @block.tensor
        def _(pe):
            pe.wait_ge(silu_ready, ONE + 1)
            n = 0
            for l in range(2):
                for b in range(B):
                    for j in range(3):
                        if n >= 2:
                            pe.wait_ge(mod_used[n % 2], ONE + n // 2)
                        for k in range(KD):
                            last = pe.matmul(ps[n % 2][:, :], sc[:, l, k, b:b + 1].broadcast_to([P, P]),
                                             wm[:, l, k, j * CH:(j + 1) * CH], start=k == 0, stop=k == KD - 1)
                        last.then_inc(mod_ready[n % 2], 1)
                        n += 1
            for l in range(2):
                for j in range(12):
                    for k in range(KD):
                        last = pe.matmul(pc[:, l, j, :], wm[:, l, k, j * P:(j + 1) * P], sc[:, l, k, :],
                                         start=k == 0, stop=k == KD - 1)
            last.then_inc(col_ready, 1)

        @block.vector
        def _(dve):
            link = linker(dve, dve_step)
            dve.wait_ge(act_step, ONE + 1)
            link(dve.tensor_scalar_add(ce[:, :, :, :], ce[:, :, :, :], 1.0))
            link(dve.reciprocal(ce[:, :, :, :], ce[:, :, :, :]))
            dve.tensor_tensor(sc[:, :, :, :], cT[:, :, :, :], ce[:, :, :, :], ALU.mult).then_inc(silu_ready, 1)
            link(dve.reduce_max(rbm[:, :], rb[:, :], AX))
            link(dve.tensor_scalar(rbd[:, :], rb[:, :], rbm[:, 0:1], None, ALU.subtract))
            dve.sem_inc(bias_exp_in, 1)
            dve.wait_ge(bias_exp, ONE + 1)
            dve.tensor_copy(ext[:, 0:P - 1], ext[:, P - 1:P].broadcast_to([H, P - 1]))
            link(dve.tensor_copy(ext[:, P + 2 * REL:w.EXT], ext[:, P + 2 * REL - 1:P + 2 * REL].broadcast_to([H, P - 1])))
            dve.sem_inc(bias_rows_ready, 1)
            n = 0
            for l in range(2):
                for b in range(B):
                    for j in range(3):
                        dve.wait_ge(mod_ready[n % 2], ONE + n // 2 + 1)
                        dve.tensor_copy(w.modrow[l][:, b, j * CH:(j + 1) * CH], ps[n % 2][:, :]).then_inc(mod_used[n % 2], 1)
                        n += 1
            dve.wait_ge(mod_used[0], ONE + 6)
            dve.wait_ge(mod_used[1], ONE + 6)
            dve.wait_ge(col_ready, ONE + 1)
            link(dve.tensor_copy(w.modcol[:, :, :, :], pc[:, :, :, :]))
            for l in range(2):
                for part in (CA, CB):
                    link(dve.tensor_scalar_add(w.modcol[:, l, 2 * part:2 * part + 2, :], w.modcol[:, l, 2 * part:2 * part + 2, :], 1.0))
                    r = w.modrow[l][:, :, part * D:(part + 1) * D]
                    link(dve.tensor_scalar_add(r, r, 1.0))
                for part in (GA, GB):
                    g = w.modrow[l][:, :, part * D:(part + 1) * D]
                    t = row[:, :].rearrange("p (b n) -> p b n", b=B)
                    link(dve.scalar_tensor_tensor(t, g, -1.0, g, op0=ALU.mult, op1=ALU.max))
                    link(dve.tensor_scalar(g, g, 0.0, 2.0, ALU.is_ge, ALU.mult))
                    link(dve.tensor_scalar_add(g, g, -1.0))
                    link(dve.tensor_scalar_max(t, t, 0.25))
                    link(dve.tensor_tensor(g, g, t, ALU.mult))
            link(dve.tensor_scalar_mul(w.bqk[:, 0:KD], w.bqk[:, 0:KD], w.SCALE))
            for b in range(B):
                link(dve.tensor_tensor(w.gbo0[:, b, :], w.modrow[0][:, b, GA * D:(GA + 1) * D], w.bo0[:, :], ALU.mult))

        @block.gpsimd
        def _(pool):
            link = linker(pool, pool_step)
            link(pool.memset(w.ident[:, :], 0.0))
            link(pool.affine_select(out=w.ident[:, :], in_=w.ident[:, :], compare_op=ALU.not_equal, fill=1.0,
                                    base=0, pattern=[[-1, P]], channel_multiplier=1))
            link(pool.memset(w.zeros[:, :], 0.0))
            link(pool.memset(w.eps[:, :], EPS))


def stage_qkv(nc, w):
    with ExitStack() as ctx:
        sem = lambda name: semaphore(nc, ctx, name)
        x_loaded = [sem(f"b_x_loaded{c}") for c in range(NC)]
        stat_step = sem("b_stat_step")
        var_ready = sem("b_var_ready")
        std_ready = sem("b_std_ready")
        norm_ready = sem("b_norm_ready")
        norm_used = sem("b_norm_used")
        turned = sem("b_turned")
        hT_ready = sem("b_hT_ready")
        hT_used = sem("b_hT_used")
        qk_ready = sem("b_qk_ready")
        v_ready = sem("b_v_ready")
        v_used = sem("b_v_used")
        whole_ready = sem("b_whole_ready")
        hi_ready = sem("b_hi_ready")
        rest_ready = sem("b_rest_ready")
        mid_ready = sem("b_mid_ready")
        low_ready = sem("b_low_ready")
        vout_ready = sem("b_vout_ready")
        stored = [sem(f"b_stored{q}") for q in range(2)]
        stored_v = sem("b_stored_v")

        st = sbuf(nc, ctx, "b_st", [P, NT, 6])
        std = sbuf(nc, ctx, "b_std", [P, NT])
        mv = sbuf(nc, ctx, "b_mv", [P, NT, 2])
        xn = sbuf(nc, ctx, "b_xn", [P, CT, D])
        hT = sbuf(nc, ctx, "b_hT", [P, KD, CH])
        NB = 4
        whole = [sbuf(nc, ctx, f"b_whole{q}", [P, NB, CH]) for q in range(2)]
        parts = [sbuf(nc, ctx, f"b_parts{q}", [P, 3, NB, CH], BF16) for q in range(2)]
        vout = sbuf(nc, ctx, "b_vout", [P, CT, D])
        pT = psum(nc, ctx, "b_pT", [P, KD, CH])
        pqk = psum(nc, ctx, "b_pqk", [P, NB, CH])
        pv = psum(nc, ctx, "b_pv", [P, CT, D])
        block = start(nc, ctx)

        @block.sync
        def _(sp):
            for c in range(NC):
                sp.dma_start(w.x[:, c * CT:(c + 1) * CT, :],
                             w.x_dram[c * CH:(c + 1) * CH, :].rearrange("(t p) n -> p t n", p=P)).then_inc(x_loaded[c], 16)
            with sp.Fori(0, B) as b:
                with sp.Fori(0, NC // B // 2) as gb:
                    for q in range(2):
                        c = (b * (NC // B // 2) + gb) * 2 + q
                        sp.wait_ge(vout_ready, ONE + c + 1)
                        for t in range(CT):
                            sp.dma_start(
                                w.v_dram[bass.ds(b * H, H), bass.ds(gb * (2 * CH) + q * CH + t * P, P), :].rearrange("h p d -> p h d"),
                                vout[:, t, :].rearrange("p (h d) -> p h d", d=DH)).then_inc(stored_v, 16)
                        sp.wait_ge(low_ready, ONE + NB * c + NB)
                        for part in range(3):
                            for i in range(2):
                                sp.dma_start(
                                    w.qk_parts[i][part, bass.ds(b * D, D), bass.ds(gb * (2 * CH) + q * CH, CH)].rearrange("(k p) t -> p k t", p=P),
                                    parts[q][:, part, i * KD:(i + 1) * KD, :]).then_inc(stored[q], 16)
            for q in range(2):
                sp.wait_ge(stored[q], ONE + 16 * 6 * (NC // 2))
            sp.wait_ge(stored_v, ONE + 16 * CT * NC)

        @block.vector
        def _(dve):
            for t in range(NT):
                if t % CT == 0:
                    dve.wait_ge(x_loaded[t // CT], ONE + 16)
                dve.bn_stats(st[:, t, :], w.x[:, t, :]).then_inc(stat_step, 1)
            for t in range(NT):
                dve.wait_ge(stat_step, ONE + t + 1)
                dve.bn_aggr(mv[:, t, :], st[:, t, :]).then_inc(var_ready, 1)
            dve.wait_ge(std_ready, ONE + 1)
            dve.reciprocal(std[:, :], std[:, :]).then_inc(stat_step, 1)
            dve.wait_ge(stat_step, ONE + NT + 1)
            def norm(c):
                dve.wait_ge(norm_used, ONE + c + 1)
                for t in range(CT):
                    i = c * CT + t
                    last = dve.tensor_scalar(xn[:, t:t + 1, :], w.x[:, bass.ds(i, 1), :], mv[:, bass.ds(i, 1), 0:1].rearrange("p a b -> p (a b)"),
                                             std[:, bass.ds(i, 1)], ALU.subtract, ALU.mult)
                last.then_inc(norm_ready, 1)

            def pair(g, last_pair):
                for q in range(2):
                    c = g * 2 + q
                    if not last_pair or q == 0:
                        norm(c + 1)
                    for blk in range(NB):
                        dve.wait_ge(hi_ready, ONE + NB * c + blk + 1)
                        dve.wait_ge(whole_ready, ONE + NB * c + blk + 1)
                        dve.tensor_tensor(whole[q][:, blk, :], whole[q][:, blk, :], parts[q][:, 0, blk, :], ALU.subtract).then_inc(rest_ready, 1)
                    for blk in range(NB):
                        dve.wait_ge(mid_ready, ONE + NB * c + blk + 1)
                        dve.tensor_tensor(parts[q][:, 2, blk, :], whole[q][:, blk, :], parts[q][:, 1, blk, :], ALU.subtract).then_inc(low_ready, 1)
                    dve.wait_ge(v_ready, ONE + c + 1)
                    dve.wait_ge(stored_v, ONE + 16 * CT * c)
                    dve.tensor_tensor(vout[:, :, :], pv[:, :, :], w.bv0[:, :].rearrange("p (o n) -> p o n", o=1).broadcast_to([P, CT, D]),
                                      ALU.add).then_inc(vout_ready, 1)

            norm(0)
            with dve.Fori(0, NC // 2 - 1) as g:
                pair(g, False)
            pair(NC // 2 - 1, True)

        @block.tensor
        def _(pe):
            pe.sem_inc(norm_used, 1)
            with pe.Fori(0, NC) as c:
                pe.wait_ge(norm_ready, ONE + c + 1)
                for t in range(CT):
                    for k in range(KD):
                        last = pe.transpose(pT[:, k, t * P:(t + 1) * P], xn[:, t, k * P:(k + 1) * P], w.ident[:, :])
                last.then_inc(norm_used, 1)
                pe.wait_ge(hT_ready, ONE + c * KD + KD)
                pe.wait_ge(hi_ready, ONE + NB * c)
                pe.wait_ge(whole_ready, ONE + NB * c)
                for blk in range(NB):
                    for k in range(KD):
                        last = pe.matmul(pqk[:, blk, :], w.Wqkv0[:, k, blk * P:(blk + 1) * P], hT[:, k, :],
                                         start=k == 0, stop=k == KD - 1)
                    last.then_inc(qk_ready, 1)
                pe.wait_ge(vout_ready, ONE + c)
                for t in range(CT):
                    for k in range(KD):
                        last = pe.matmul(pv[:, t, :], hT[:, k, t * P:(t + 1) * P], w.Wqkv0[:, k, 2 * D:3 * D],
                                         start=k == 0, stop=k == KD - 1)
                last.then_inc(v_ready, 1)

        @block.scalar
        def _(act):
            act.wait_ge(var_ready, ONE + NT)
            act.activation(std[:, :], mv[:, :, 1], ACT.Sqrt, bias=w.eps[:, 0:1]).then_inc(std_ready, 1)
            with act.Fori(0, B) as b:
              with act.Fori(0, NC // B // 2) as gb:
                for q in range(2):
                    g = b * (NC // B // 2) + gb
                    c = g * 2 + q
                    wait_alone(w, act, norm_used, ONE + c + 2)
                    wait_alone(w, act, v_ready, ONE + c)
                    for k in range(KD):
                        act.activation(hT[:, k, :], pT[:, k, :], ACT.Identity,
                                       scale=w.modcol[:, 0, 2 * CA + k, bass.ds(b, 1)], bias=w.modcol[:, 0, 2 * SA + k, bass.ds(b, 1)]).then_inc(hT_ready, 1)
                    act.wait_ge(low_ready, ONE + NB * 2 * g)
                    act.wait_ge(stored[q], ONE + 16 * 6 * g)
                    for blk in range(NB):
                        s = w.SCALE if blk < KD else 1.0
                        act.wait_ge(qk_ready, ONE + NB * c + blk + 1)
                        act.activation(parts[q][:, 0, blk, :], pqk[:, blk, :], ACT.Identity, scale=s, bias=w.bqk[:, blk:blk + 1]).then_inc(hi_ready, 1)
                        act.activation(whole[q][:, blk, :], pqk[:, blk, :], ACT.Identity, scale=s, bias=w.bqk[:, blk:blk + 1]).then_inc(whole_ready, 1)
                    for blk in range(NB):
                        act.wait_ge(rest_ready, ONE + NB * c + blk + 1)
                        act.activation(parts[q][:, 1, blk, :], whole[q][:, blk, :], ACT.Copy).then_inc(mid_ready, 1)

        @block.gpsimd
        def _(pool):
            for n in range(NH):
                pool.dma_start(w.skew_dram[n, :].rearrange("(p r) -> p r", r=w.EXT + 1)[:, 0:w.EXT],
                               w.ext_dram[n:n + 1, :].broadcast_to([P, w.EXT])).then_inc(w.band_stored, 16)
            pool.wait_ge(w.band_stored, 16 * NH)


def stage_attention(nc, w):
    R6 = 6 * DH
    R8 = R6 + 2
    JT = S // P
    HALF = S // 2
    BANDT = w.BAND // P
    NBUF = 4
    VW = 32
    GROUPS = JT * (S // CH)
    PER_STEP = GROUPS // JT
    SHIFT = 6
    AHEAD = 2

    def band(t):
        return max(0, (t - 2) * P), min(S, (t + BANDT - 2) * P)

    def segments(t, half):
        lo, hi = band(t)
        a, z = half * HALF, (half + 1) * HALF
        cuts = [(a, min(z, lo), "left"), (max(a, lo), min(z, hi), "band"), (max(a, hi), z, "right")]
        return [c for c in cuts if c[0] < c[1]]

    band_parts = [[sum(k == "band" for _, _, k in segments(t, half)) for half in range(2)] for t in range(JT)]
    POOL_STEPS = sum(map(sum, band_parts))
    pool_after = [sum(map(sum, band_parts[:t + 1])) for t in range(JT)]

    with ExitStack() as ctx:
        sem = lambda name: semaphore(nc, ctx, name)
        max_loaded = [sem(f"c_max_loaded{q}") for q in range(2)]
        score_loaded = [sem(f"c_score_loaded{q}") for q in range(2)]
        consts_ready = sem("c_consts_ready")
        value_pad_ready = sem("c_value_pad_ready")
        group_ready = sem("c_group_ready")
        group_done = sem("c_group_done")
        max_ready = sem("c_max_ready")
        maxT_ready = sem("c_maxT_ready")
        max_parts_hi = sem("c_max_parts_hi")
        max_parts_ready = sem("c_max_parts_ready")
        max_rows_loaded = sem("c_max_rows_loaded")
        scores_ready = sem("c_scores_ready")
        probs_ready = sem("c_probs_ready")
        band_ready = sem("c_band_ready")
        summed = sem("c_summed")
        out_taken = sem("c_out_taken")
        out_stored = sem("c_out_stored")
        max_step = sem("c_max_step")
        zeroed = sem("c_zeroed")

        QM = [sbuf(nc, ctx, f"QM{q}", [R6, S], BF16) for q in range(2)]
        KM = [sbuf(nc, ctx, f"KM{q}", [R6, S], BF16) for q in range(2)]
        QS = [sbuf(nc, ctx, f"QS{q}", [R8, S], BF16) for q in range(2)]
        KS = [sbuf(nc, ctx, f"KS{q}", [R8, S], BF16) for q in range(2)]
        V = [sbuf(nc, ctx, f"V{q}", [P, JT, VW]) for q in range(2)]
        EB = [sbuf(nc, ctx, f"EB{q}", [P, BANDT * P]) for q in range(2)]
        probs = [sbuf(nc, ctx, f"probs{i}", [P, S]) for i in range(NBUF)]
        gmax = sbuf(nc, ctx, "gmax", [P, JT, S // CH])
        qmax = sbuf(nc, ctx, "qmax", [P, JT])
        mhi = sbuf(nc, ctx, "mhi", [JT, P], BF16)
        mlo = sbuf(nc, ctx, "mlo", [JT, P], BF16)
        osb = sbuf(nc, ctx, "osb", [P, CH])
        GB = 3
        pg = [psum(nc, ctx, f"pg{i}", [P, CH]) for i in range(GB)]
        psc = [psum(nc, ctx, f"psc{i}", [P, HALF]) for i in range(2)]
        po = psum(nc, ctx, "po", [P, CH])
        pm = pg[GROUPS % GB]
        block = start(nc, ctx)

        @block.sync
        def _(sp):
            def load_parts(dst, order, src, n, loaded):
                at = 0
                for part, times in order:
                    for _ in range(times):
                        sp.dma_start(dst[at:at + DH, :], src[part, bass.ds(n * DH, DH), :]).then_inc(loaded, 16)
                        at += DH

            Q_ORDER = [(0, 3), (1, 2), (2, 1)]
            K_ORDER = [(0, 1), (1, 1), (2, 1), (0, 1), (1, 1), (0, 1)]

            def load_max(n, q):
                load_parts(QM[q], Q_ORDER, w.qk_parts[0], n, max_loaded[q])
                load_parts(KM[q], K_ORDER, w.qk_parts[1], n, max_loaded[q])

            def load_scores(n, q):
                load_parts(QS[q], Q_ORDER, w.qk_parts[0], n, score_loaded[q])
                load_parts(KS[q], K_ORDER, w.qk_parts[1], n, score_loaded[q])
                sp.dma_start(V[q][:, :, 0:DH], w.v_dram[bass.ds(n, 1), :, :].rearrange("o (t p) d -> p (o t) d", p=P)).then_inc(score_loaded[q], 16)
                sp.dma_start(EB[q][:, :], 
                             w.skew_dram[bass.ds(n, 1), P - 1:P - 1 + P * w.EXT].rearrange("o (p r) -> p (o r)", r=w.EXT)[:, 0:BANDT * P]).then_inc(score_loaded[q], 16)

            def move_max(n, q):
                sp.wait_ge(max_parts_ready, ONE + n + 1)
                sp.dma_start(QS[q][R6:R6 + 1, :], mhi[:, :]).then_inc(max_rows_loaded, 16)
                sp.dma_start(QS[q][R6 + 1:R8, :], mlo[:, :]).then_inc(max_rows_loaded, 16)

            def store_out(n):
                sp.wait_ge(out_taken, ONE + n + 1)
                for c in range(S // CH):
                    sp.dma_start(w.attT_dram[bass.ds(n, 1), :, c * CH:(c + 1) * CH].rearrange("o r t -> (o r) t"),
                                 osb[VW * c:VW * c + DH + 1, :]).then_inc(out_stored, 16)

            load_max(0, 0)
            rows = w.xe_dram.rearrange("(n p k) d -> n p (k d)", p=P, k=w.zeros.shape[1] // D)
            for i in range(rows.shape[0]):
                sp.dma_start(rows[i], w.zeros[:, :]).then_inc(zeroed, 16)
            sp.wait_ge(value_pad_ready, ONE + 1)
            load_scores(0, 0)
            load_max(1, 1)
            load_scores(1, 1)
            move_max(0, 0)

            def pair(g, last):
                for q in range(2):
                    n = g * 2 + q
                    if not last:
                        sp.wait_ge(group_ready, ONE + GROUPS * n + GROUPS)
                        load_max(n + 2, q)
                    if not last or q == 0:
                        move_max(n + 1, 1 - q)
                    if not last:
                        sp.wait_ge(summed, ONE + JT * n + JT + NBUF - 1)
                        sp.wait_ge(band_ready, ONE + POOL_STEPS * n + POOL_STEPS)
                        load_scores(n + 2, q)
                    store_out(n)

            with sp.Fori(0, NH // 2 - 1) as g:
                pair(g, False)
            pair(NH // 2 - 1, True)
            sp.wait_ge(out_stored, ONE + 16 * (S // CH) * NH)
            sp.wait_ge(zeroed, ONE + 16 * rows.shape[0])

        @block.tensor
        def _(pe):
            def group(n, q, k):
                tile, c = divmod(k, S // CH)
                if k == 0:
                    pe.wait_ge(group_done, ONE + GROUPS * n)
                elif k >= GB:
                    pe.wait_ge(group_done, ONE + GROUPS * n + k - GB + 1)
                if k == GROUPS % GB:
                    pe.wait_ge(max_parts_ready, ONE + n)
                pe.matmul(pg[k % GB][:, :], QM[q][:, tile * P:(tile + 1) * P], KM[q][:, c * CH:(c + 1) * CH],
                          start=True, stop=True).then_inc(group_ready, 1)

            def turn_max(n):
                pe.wait_ge(max_ready, ONE + n + 1)
                pe.transpose(pm[0:JT, 0:P], qmax[:, :], w.ident[:, :]).then_inc(maxT_ready, 1)

            def scores(n, q, t, half):
                pe.wait_ge(probs_ready, ONE + 2 * JT * n + 2 * t + half)
                for c in range(HALF // CH):
                    at = half * HALF + c * CH
                    last = pe.matmul(psc[half][:, c * CH:(c + 1) * CH], KS[q][:, t * P:(t + 1) * P], QS[q][:, at:at + CH],
                                     start=True, stop=True)
                last.then_inc(scores_ready, 1)

            def sums(n, q, t):
                pe.wait_ge(probs_ready, ONE + 2 * JT * n + 2 * t + 3)
                pe.wait_ge(band_ready, ONE + POOL_STEPS * n + pool_after[t])
                if t == 0:
                    pe.wait_ge(out_taken, ONE + n)
                for c in range(S // CH):
                    last = pe.matmul(po[VW * c:VW * (c + 1), :], V[q][:, t, :], probs[t % NBUF][:, c * CH:(c + 1) * CH],
                                     start=t == 0, stop=t == JT - 1)
                last.then_inc(summed, 1)

            pe.sem_inc(summed, NBUF - 1)
            pe.wait_ge(consts_ready, ONE + 1)
            pe.wait_ge(max_loaded[0], ONE + 192)
            for k in range(GROUPS):
                group(0, 0, k)
            turn_max(0)
            pe.wait_ge(max_loaded[1], ONE + 192)
            pe.wait_ge(score_loaded[0], ONE + 224)
            pe.wait_ge(max_rows_loaded, ONE + 32)
            for t in range(AHEAD):
                scores(0, 0, t, 0)
                scores(0, 0, t, 1)
                for k in range(SHIFT * PER_STEP // AHEAD):
                    group(1, 1, k + t * (SHIFT * PER_STEP // AHEAD))

            def pair(g, last):
                for q in range(2):
                    n = g * 2 + q
                    more = not last or q == 0
                    for t in range(JT):
                        if t == JT - SHIFT and not last:
                            pe.wait_ge(max_loaded[q], ONE + 192 * g + 384)
                        if t == JT - AHEAD and more:
                            pe.wait_ge(max_rows_loaded, ONE + 32 * n + 64)
                            pe.wait_ge(score_loaded[1 - q], ONE + 224 * g + 224 * (1 + q))

                        def next_group(i):
                            if t < JT - SHIFT and more:
                                group(n + 1, 1 - q, (t + SHIFT) * PER_STEP + i)
                            elif t >= JT - SHIFT and not last:
                                group(n + 2, q, (t + SHIFT - JT) * PER_STEP + i)

                        for half in range(2):
                            if t < JT - AHEAD:
                                scores(n, q, t + AHEAD, half)
                            elif more:
                                scores(n + 1, 1 - q, t + AHEAD - JT, half)
                            next_group(half)
                            if half == 0 and t == JT - SHIFT and more:
                                turn_max(n + 1)
                        next_group(2)
                        sums(n, q, t)
                        next_group(3)

            with pe.Fori(0, NH // 2 - 1) as g:
                pair(g, False)
            pair(NH // 2 - 1, True)

        @block.vector
        def _(dve):
            for q in range(2):
                dve.memset(KS[q][R6:R8, :], 1.0)
                dve.memset(V[q][:, :, :], 0.0).then_inc(max_step, 1)
            dve.wait_ge(max_step, ONE + 2)
            for q in range(2):
                last = dve.memset(V[q][:, :, DH:DH + 1], 1.0)
            last.then_inc(value_pad_ready, 1)
            dve.wait_ge(value_pad_ready, ONE + 1)
            dve.sem_inc(consts_ready, 1)

            def head_max(n):
                for k in range(GROUPS):
                    tile, c = divmod(k, S // CH)
                    dve.wait_ge(group_ready, ONE + GROUPS * n + k + 1)
                    dve.reduce_max(gmax[:, tile, c:c + 1], pg[k % GB][:, :], AX).then_inc(group_done, 1)
                dve.wait_ge(group_done, ONE + GROUPS * n + GROUPS)
                dve.reduce_max(qmax[:, :], gmax[:, :, :], AX).then_inc(max_ready, 1)
                dve.wait_ge(maxT_ready, ONE + n + 1)
                dve.wait_ge(max_rows_loaded, ONE + 32 * n)
                dve.tensor_scalar_mul(mhi[:, :], pm[0:JT, 0:P], -1.0).then_inc(max_parts_hi, 1)
                dve.wait_ge(max_parts_hi, ONE + n + 1)
                dve.scalar_tensor_tensor(mlo[:, :], pm[0:JT, 0:P], -1.0, mhi[:, :], op0=ALU.mult, op1=ALU.subtract).then_inc(max_parts_ready, 1)

            head_max(0)
            with dve.Fori(1, NH) as n:
                head_max(n)

        @block.scalar
        def _(act):
            def exps(n, t, half):
                if half == 0:
                    act.wait_ge(summed, ONE + JT * n + t)
                wait_alone(w, act, scores_ready, ONE + 2 * JT * n + 2 * t + half + 1)
                for a, z, kind in segments(t, half):
                    bias = {"left": w.far[:, bass.ds(n, 1), 0:1], "right": w.far[:, bass.ds(n, 1), 1:2], "band": None}[kind]
                    more = {} if bias is None else {"bias": bias.rearrange("p a b -> p (a b)")}
                    last = act.activation(probs[t % NBUF][:, a:z], psc[half][:, a - half * HALF:z - half * HALF], ACT.Exp, **more)
                last.then_inc(probs_ready, 1)

            act.sem_inc(probs_ready, 1)
            for t in range(AHEAD):
                exps(0, t, 0)
                exps(0, t, 1)

            def head(n, last):
                for t in range(AHEAD, JT):
                    exps(n, t, 0)
                    exps(n, t, 1)
                if not last:
                    for t in range(AHEAD):
                        exps(n + 1, t, 0)
                        exps(n + 1, t, 1)
                act.wait_ge(summed, ONE + JT * n + JT + NBUF - 1)
                act.wait_ge(out_stored, ONE + 16 * (S // CH) * n)
                act.activation(osb[:, :], po[:, :], ACT.Copy).then_inc(out_taken, 1)

            with act.Fori(0, NH - 1) as n:
                head(n, False)
            head(NH - 1, True)

        @block.gpsimd
        def _(pool):
            with pool.Fori(0, NH // 2) as g:
                for q in range(2):
                    n = g * 2 + q
                    pool.wait_ge(score_loaded[q], ONE + 224 * g + 224)
                    for t in range(JT):
                        lo = (t - 2) * P
                        for half in range(2):
                            for a, z, kind in segments(t, half):
                                if kind == "band":
                                    pool.wait_ge(probs_ready, ONE + 2 * JT * n + 2 * t + half + 2)
                                    part = probs[t % NBUF][:, a:z]
                                    pool.tensor_tensor(part, part, EB[q][:, a - lo:z - lo], ALU.mult).then_inc(band_ready, 1)


E0, K0, I0, CAP = 64, 4, 128, 256


def stage_project(nc, w):
    with ExitStack() as ctx:
        sem = lambda name: semaphore(nc, ctx, name)
        loaded = [sem(f"d_loaded{q}") for q in range(2)]
        att_ready = sem("d_att_ready")
        sums_loaded = sem("d_sums_loaded")
        inverse_ready = sem("d_inverse_ready")
        inverse_stored = sem("d_inverse_stored")
        sums = sbuf(nc, ctx, "d_sums", [P, CH])
        projected = sem("d_projected")
        gated = sem("d_gated")
        biased = sem("d_biased")
        raw = [sbuf(nc, ctx, f"d_raw{q}", [P, KD, CH]) for q in range(2)]
        inv = [sbuf(nc, ctx, f"d_inv{q}", [P, KD, CH]) for q in range(2)]
        att = [sbuf(nc, ctx, f"d_att{q}", [P, KD, CH]) for q in range(2)]
        gate = [sbuf(nc, ctx, f"d_gate{q}", [P, CT, D]) for q in range(2)]
        pp = [psum(nc, ctx, f"d_pp{q}", [P, CT, D]) for q in range(2)]
        block = start(nc, ctx)
        HB = P // DH
        GBATCH = NC // B // 2

        @block.sync
        def _(sp):
            for n in range(NH):
                rows = slice(n * (S // CH), (n + 1) * (S // CH))
                sp.dma_start(sums[rows, :], w.attT_dram[n, DH, :].rearrange("(c t) -> c t", t=CH)).then_inc(sums_loaded, 16)
            sp.wait_ge(inverse_ready, ONE + 1)
            sp.dma_start(w.inverse_dram.rearrange("n (c t) -> (n c) t", t=CH), sums[:, :]).then_inc(inverse_stored, 16)
            sp.wait_ge(inverse_stored, ONE + 16)
            with sp.Fori(0, B) as b:
                with sp.Fori(0, GBATCH) as gb:
                    g = b * GBATCH + gb
                    sp.wait_ge(att_ready, ONE + g * 2)
                    for q in range(2):
                        cols = bass.ds(gb * (2 * CH) + q * CH, CH)
                        for k in range(KD):
                            heads = bass.ds(b * H + k * HB, HB)
                            sp.dma_start(raw[q][:, k, :], w.attT_dram[heads, 0:DH, cols]).then_inc(loaded[q], 16)
                            sp.dma_start(inv[q][:, k, :], w.inverse_dram[heads, cols].rearrange("h (o t) -> h o t", o=1).broadcast_to([HB, DH, CH])).then_inc(loaded[q], 16)

        @block.gpsimd
        def _(pool):
            with pool.Fori(0, B) as b:
                with pool.Fori(0, NC // B) as cb:
                    xs = w.x[:, bass.ds(b * TB + cb * CT, CT), :]
                    pool.tensor_tensor(xs, xs, w.gbo0[:, bass.ds(b, 1), :].broadcast_to([P, CT, D]), ALU.add).then_inc(biased, 1)

        @block.vector
        def _(dve):
            dve.wait_ge(sums_loaded, ONE + 16 * NH)
            dve.reciprocal(sums[:, :], sums[:, :]).then_inc(inverse_ready, 1)
            with dve.Fori(0, B) as b:
                with dve.Fori(0, GBATCH) as gb:
                    g = b * GBATCH + gb
                    for q in range(2):
                        dve.wait_ge(loaded[q], ONE + 16 * 2 * KD * g + 16 * 2 * KD)
                        dve.wait_ge(projected, ONE + g * 2)
                        dve.tensor_tensor(att[q][:, :, :], raw[q][:, :, :], inv[q][:, :, :], ALU.mult).then_inc(att_ready, 1)
                    for q in range(2):
                        c = g * 2 + q
                        dve.wait_ge(projected, ONE + c + 1)
                        ga = w.modrow[0][:, bass.ds(b, 1), GA * D:(GA + 1) * D].broadcast_to([P, CT, D])
                        dve.tensor_tensor(gate[q][:, :, :], pp[q][:, :, :], ga, ALU.mult).then_inc(gated, 1)
                    for q in range(2):
                        c = g * 2 + q
                        xs = w.x[:, bass.ds(c * CT, CT), :]
                        dve.wait_ge(gated, ONE + c + 1)
                        dve.wait_ge(biased, ONE + c + 1)
                        dve.tensor_tensor(xs, xs, gate[q][:, :, :], ALU.add)

        @block.tensor
        def _(pe):
            with pe.Fori(0, NC // 2) as g:
                for q in range(2):
                    pe.wait_ge(att_ready, ONE + g * 2 + q + 1)
                    pe.wait_ge(gated, ONE + g * 2)
                    for t in range(CT):
                        for k in range(KD):
                            last = pe.matmul(pp[q][:, t, :], att[q][:, k, t * P:(t + 1) * P], w.Wout0[:, k, :], start=k == 0, stop=k == KD - 1)
                    last.then_inc(projected, 1)


def stage_norm(nc, w, x, tiles, mean_var, rstd, name):
    with ExitStack() as ctx:
        sem = lambda n: semaphore(nc, ctx, f"{name}_{n}")
        stats_ready, var_ready, std_ready = sem("stats_ready"), sem("var_ready"), sem("std_ready")
        st = sbuf(nc, ctx, f"{name}_st", [P, tiles, 6])
        block = start(nc, ctx)

        @block.vector
        def _(dve):
            for t in range(tiles):
                dve.bn_stats(st[:, t, :], x[:, t, :]).then_inc(stats_ready, 1)
            for t in range(tiles):
                dve.wait_ge(stats_ready, ONE + t + 1)
                dve.bn_aggr(mean_var[:, t, :], st[:, t, :]).then_inc(var_ready, 1)
            dve.wait_ge(std_ready, ONE + 1)
            dve.reciprocal(rstd[:, 0:tiles], rstd[:, 0:tiles])

        @block.scalar
        def _(act):
            act.wait_ge(var_ready, ONE + tiles)
            act.activation(rstd[:, 0:tiles], mean_var[:, 0:tiles, 1], ACT.Sqrt, bias=w.eps[:, 0:1]).then_inc(std_ready, 1)


def stage_router(nc, w, x, mean_var, rstd, h, hT_all, layer, Wg, logits, name):
    n_experts = logits.shape[2]
    with ExitStack() as ctx:
        sem = lambda n: semaphore(nc, ctx, f"{name}_{n}")
        norm_ready, norm_turned, hT_ready, logits_ready = sem("norm_ready"), sem("norm_turned"), sem("hT_ready"), sem("logits_ready")
        logits_out, scaled, shifted, hT_kept = sem("logits_out"), sem("scaled"), sem("shifted"), sem("hT_kept")
        xn = [sbuf(nc, ctx, f"{name}_xn{q}", [P, CT, D]) for q in range(2)]
        hT = [sbuf(nc, ctx, f"{name}_hT{q}", [P, KD, CH]) for q in range(2)]
        tmp = sbuf(nc, ctx, f"{name}_tmp", [P, CT, D])
        pT = [psum(nc, ctx, f"{name}_pT{q}", [P, KD, CH]) for q in range(2)]
        pl = [psum(nc, ctx, f"{name}_pl{q}", [P, CT, n_experts]) for q in range(2)]
        block = start(nc, ctx)
        natural = h is not None
        GBATCH = NC // B // 2

        @block.vector
        def _(dve):
            with dve.Fori(0, NC // 2) as g:
                for q in range(2):
                    c = g * 2 + q
                    dve.wait_ge(norm_turned, ONE + g * 2)
                    if natural:
                        dve.wait_ge(scaled, ONE + g * 2)
                    for t in range(CT):
                        i = c * CT + t
                        last = dve.tensor_scalar(xn[q][:, t:t + 1, :], x[:, bass.ds(i, 1), :], mean_var[:, bass.ds(i, 1), 0:1].rearrange("p a b -> p (a b)"),
                                                 rstd[:, bass.ds(i, 1)], ALU.subtract, ALU.mult)
                    last.then_inc(norm_ready, 1)
                for q in range(2):
                    c = g * 2 + q
                    dve.wait_ge(logits_ready, ONE + c + 1)
                    dve.tensor_copy(logits[:, bass.ds(c * CT, CT), :], pl[q][:, :, :]).then_inc(logits_out, 1)

        @block.tensor
        def _(pe):
            with pe.Fori(0, NC // 2) as g:
                for q in range(2):
                    pe.wait_ge(norm_ready, ONE + g * 2 + q + 1)
                    pe.wait_ge(hT_ready, ONE + KD * 2 * g)
                    for t in range(CT):
                        for k in range(KD):
                            last = pe.transpose(pT[q][:, k, t * P:(t + 1) * P], xn[q][:, t, k * P:(k + 1) * P], w.ident[:, :])
                    last.then_inc(norm_turned, 1)
                for q in range(2):
                    pe.wait_ge(hT_ready, ONE + KD * 2 * g + KD * q + KD)
                    pe.wait_ge(logits_out, ONE + g * 2)
                    for t in range(CT):
                        for k in range(KD):
                            last = pe.matmul(pl[q][:, t, :], hT[q][:, k, t * P:(t + 1) * P], Wg[:, k, :], start=k == 0, stop=k == KD - 1)
                    last.then_inc(logits_ready, 1)

        @block.scalar
        def _(act):
            with act.Fori(0, B) as b:
                with act.Fori(0, GBATCH) as gb:
                    g = b * GBATCH + gb
                    for q in range(2):
                        wait_alone(w, act, norm_turned, ONE + g * 2 + q + 1)
                        wait_alone(w, act, logits_ready, ONE + g * 2)
                        if hT_all is not None:
                            wait_alone(w, act, hT_kept, ONE + g * 2)
                        for k in range(KD):
                            act.activation(hT[q][:, k, :], pT[q][:, k, :], ACT.Identity, scale=w.modcol[:, layer, 2 * CB + k, bass.ds(b, 1)],
                                           bias=w.modcol[:, layer, 2 * SB_ + k, bass.ds(b, 1)]).then_inc(hT_ready, 1)

        @block.gpsimd
        def _(pool):
            with pool.Fori(0, B) as b:
                with pool.Fori(0, GBATCH) as gb:
                    for q in range(2):
                        c = (b * GBATCH + gb) * 2 + q
                        if hT_all is not None:
                            pool.wait_ge(hT_ready, ONE + KD * c + KD)
                            pool.tensor_copy(hT_all[:, :, bass.ds(c * CH, CH)], hT[q][:, :, :]).then_inc(hT_kept, 1)
                        if natural:
                            wait_alone(w, pool, norm_ready, ONE + c + 1)
                            wait_alone(w, pool, shifted, ONE + c)
                            row = lambda part: w.modrow[layer][:, bass.ds(b, 1), part * D:(part + 1) * D].broadcast_to([P, CT, D])
                            pool.tensor_tensor(tmp[:, :, :], xn[q][:, :, :], row(CB), ALU.mult).then_inc(scaled, 1)
                            pool.wait_ge(scaled, ONE + c + 1)
                            pool.tensor_tensor(h[:, bass.ds(c * CT, CT), :], tmp[:, :, :], row(SB_), ALU.add).then_inc(shifted, 1)


def softmax_rows(dve, link, logits, top, total, exp_request, exp_done):
    tiles, n = logits.shape[1], logits.shape[2]
    over = lambda v: v[:, :].rearrange("p (t o) -> p t o", o=1).broadcast_to([P, tiles, n])
    link(dve.reduce_max(top[:, :], logits[:, :, :], AX))
    dve.tensor_tensor(logits[:, :, :], logits[:, :, :], over(top), ALU.subtract).then_inc(exp_request, 1)
    dve.wait_ge(exp_done, ONE + 1)
    link(dve.reduce_sum(total[:, :], logits[:, :, :], AX))
    link(dve.reciprocal(total[:, :], total[:, :]))
    link(dve.tensor_tensor(logits[:, :, :], logits[:, :, :], over(total), ALU.mult))


def stage_route(nc, w):
    with ExitStack() as ctx:
        sem = lambda name: semaphore(nc, ctx, name)
        step = sem("r_step")
        exp_request, exp_done = sem("r_exp_request"), sem("r_exp_done")
        made = sem("r_made")
        mask_ready, counted, base_step = sem("r_mask_ready"), sem("r_counted"), sem("r_base_step")
        N = NT * K0
        top = sbuf(nc, ctx, "r_top", [P, NT])
        total = sbuf(nc, ctx, "r_total", [P, NT])
        m8 = sbuf(nc, ctx, "r_m8", [P, NT, 8])
        i8 = sbuf(nc, ctx, "r_i8", [P, NT, 8], U32)
        i4 = sbuf(nc, ctx, "r_i4", [P, N])
        col_i = sbuf(nc, ctx, "r_col_i", [P, E0], I32)
        col = sbuf(nc, ctx, "r_col", [P, E0])
        chosen = sbuf(nc, ctx, "r_chosen", [P, N, E0], BF16)
        mask = sbuf(nc, ctx, "r_mask", [P, NT, E0], BF16)
        before = sbuf(nc, ctx, "r_before", [P, P], BF16)
        ones = sbuf(nc, ctx, "r_ones", [P, P], BF16)
        base = sbuf(nc, ctx, "r_base", [P, NT, E0])
        tot = sbuf(nc, ctx, "r_tot", [P, NT, E0])
        prod = sbuf(nc, ctx, "r_prod", [P, N, E0])
        place = sbuf(nc, ctx, "r_place", [P, N])
        over = sbuf(nc, ctx, "r_over", [P, N])
        slot = sbuf(nc, ctx, "r_slot", [P, N])
        G = CH // E0
        pw = psum(nc, ctx, "r_pw", [P, NT, E0])
        pt = psum(nc, ctx, "r_pt", [P, NT, E0])
        block = start(nc, ctx)
        BIG = float(1 << 22)

        @block.gpsimd
        def _(pool):
            pool.iota(col_i[:, :], [[1, E0]], base=0, channel_multiplier=0).then_inc(made, 1)
            pool.memset(ones[:, :], 1.0).then_inc(made, 1)
            pool.wait_ge(made, ONE + 2)
            pool.affine_select(out=before[:, :], in_=ones[:, :], compare_op=ALU.is_gt, fill=0.0, base=0,
                               pattern=[[1, P]], channel_multiplier=-1).then_inc(made, 1)

        @block.scalar
        def _(act):
            act.wait_ge(exp_request, ONE + 1)
            act.activation(w.logits0[:, :, :], w.logits0[:, :, :], ACT.Exp).then_inc(exp_done, 1)

        @block.tensor
        def _(pe):
            pe.wait_ge(made, ONE + 3)
            pe.wait_ge(mask_ready, ONE + 1)
            for g in range(NT // G):
                pe.matmul(pw[:, g * G:(g + 1) * G, :], before[:, :], mask[:, g * G:(g + 1) * G, :], start=True, stop=True)
                last = pe.matmul(pt[:, g * G:(g + 1) * G, :], ones[:, :], mask[:, g * G:(g + 1) * G, :], start=True, stop=True)
            last.then_inc(counted, 1)

        @block.vector
        def _(dve):
            link = linker(dve, step)
            probs = w.logits0
            softmax_rows(dve, link, probs, top, total, exp_request, exp_done)
            for t in range(NT):
                last = dve.max(m8[:, t, :], probs[:, t, :])
            link(last)
            for t in range(NT):
                last = dve.max_index(i8[:, t, :], m8[:, t, :], probs[:, t, :])
            dve.tensor_copy(w.gate4[:, :, :], m8[:, :, 0:K0])
            link(last)
            link(dve.tensor_copy(i4[:, :].rearrange("p (t k) -> p t k", k=K0), i8[:, :, 0:K0]))
            dve.wait_ge(made, ONE + 1)
            link(dve.tensor_copy(col[:, :], col_i[:, :]))
            link(dve.tensor_tensor(chosen[:, :, :], col[:, :].rearrange("p (o e) -> p o e", o=1).broadcast_to([P, N, E0]),
                                   i4[:, :].rearrange("p (n o) -> p n o", o=1).broadcast_to([P, N, E0]), ALU.is_equal))
            by_k = chosen[:, :, :].rearrange("p (t k) e -> p t k e", k=K0)
            link(dve.tensor_tensor(mask[:, :, :], by_k[:, :, 0, :], by_k[:, :, 1, :], ALU.add))
            link(dve.tensor_tensor(mask[:, :, :], mask[:, :, :], by_k[:, :, 2, :], ALU.add))
            dve.tensor_tensor(mask[:, :, :], mask[:, :, :], by_k[:, :, 3, :], ALU.add).then_inc(mask_ready, 1)
            dve.wait_ge(counted, ONE + 1)
            dve.tensor_copy(tot[:, :, :], pt[:, :, :]).then_inc(base_step, 1)
            dve.memset(base[:, 0:1, :], 0.0).then_inc(base_step, 1)
            dve.wait_ge(base_step, ONE + 2)
            with dve.Fori(0, NT - 1) as t:
                dve.wait_ge(base_step, ONE + t + 2)
                dve.tensor_tensor(base[:, bass.ds(t + 1, 1), :], base[:, bass.ds(t, 1), :], tot[:, bass.ds(t, 1), :], ALU.add).then_inc(base_step, 1)
            dve.wait_ge(base_step, ONE + NT + 1)
            link(dve.tensor_tensor(base[:, :, :], pw[:, :, :], base[:, :, :], ALU.add))
            for k in range(K0):
                last = dve.tensor_tensor(prod[:, :, :].rearrange("p (t k) e -> p t k e", k=K0)[:, :, k, :], by_k[:, :, k, :], base[:, :, :], ALU.mult)
            link(last)
            link(dve.reduce_sum(place[:, :], prod[:, :, :], AX))
            link(dve.tensor_scalar(over[:, :], place[:, :], float(CAP), BIG, ALU.is_ge, ALU.mult))
            link(dve.scalar_tensor_tensor(slot[:, :], i4[:, :], float(CAP), place[:, :], op0=ALU.mult, op1=ALU.add))
            link(dve.tensor_tensor(slot[:, :], slot[:, :], over[:, :], ALU.add))
            link(dve.tensor_copy(w.put_at[:, :, :].rearrange("p t k -> p (t k)"), slot[:, :]))
            link(dve.tensor_scalar_min(place[:, :], place[:, :], float(CAP - 1)))
            link(dve.scalar_tensor_tensor(slot[:, :], i4[:, :], float(CAP), place[:, :], op0=ALU.mult, op1=ALU.add))
            dve.memset(w.get_from[:, NT:NT + 2, :], 0)
            link(dve.tensor_copy(w.get_from[:, 0:NT, :].rearrange("p t k -> p (t k)"), slot[:, :]))


def stage_scatter(nc, w):
    with ExitStack() as ctx:
        sem = lambda name: semaphore(nc, ctx, name)
        staged = sem("s_staged")
        sent = [gpsimd_dma_semaphore(nc, ctx, f"s_sent{q}") for q in range(2)]
        rows = [sbuf(nc, ctx, f"s_rows{q}", [P, D]) for q in range(2)]
        at = [sbuf(nc, ctx, f"s_at{q}", [P, K0], I32) for q in range(2)]
        block = start(nc, ctx)

        @block.vector
        def _(dve):
            def stage(t, q):
                dve.tensor_copy(at[q][:, :].rearrange("p (o k) -> p o k", o=1), w.put_at[:, bass.ds(t, 1), :])
                dve.tensor_copy(rows[q][:, :].rearrange("p (o n) -> p o n", o=1), w.h[:, bass.ds(t, 1), :]).then_inc(staged, 1)

            for q in range(2):
                stage(q, q)
            with dve.Fori(1, NT // 2) as g:
                for q in range(2):
                    dve.wait_ge(sent[q], 16 * K0 * g)
                    stage(g * 2 + q, q)

        @block.gpsimd
        def _(pool):
            with pool.Fori(0, NT // 2) as g:
                for q in range(2):
                    wait_alone(w, pool, staged, ONE + g * 2 + q + 1)
                    for k in range(K0):
                        pool.indirect_dma_start(out=w.xe_dram[:, :], out_offset=bass.IndirectOffsetOnAxis(ap=at[q][:, k:k + 1], axis=0),
                                                in_=rows[q][:, :], in_offset=None, bounds_check=E0 * CAP - 1, oob_is_err=False).then_inc(sent[q], 16)
            for q in range(2):
                pool.wait_ge(sent[q], 16 * K0 * (NT // 2))


def stage_experts(nc, w):
    NB = 4
    with ExitStack() as ctx:
        sem = lambda name: semaphore(nc, ctx, name)
        loaded = [sem(f"e_loaded{q}") for q in range(NB)]
        turned, xT_ready = sem("e_turned"), sem("e_xT_ready")
        up_ready, silu_ready, g_ready, down_ready = sem("e_up_ready"), sem("e_silu_ready"), sem("e_g_ready"), sem("e_down_ready")
        y_ready = sem("e_y_ready")
        stored = [sem(f"e_stored{q}") for q in range(2)]
        SC = CAP // P
        X = [sbuf(nc, ctx, f"e_X{q}", [P, SC, D]) for q in range(NB)]
        W1 = [sbuf(nc, ctx, f"e_W1{q}", [P, KD, 2 * I0]) for q in range(NB)]
        W2 = [sbuf(nc, ctx, f"e_W2{q}", [P, D]) for q in range(NB)]
        XT = [sbuf(nc, ctx, f"e_XT{q}", [P, KD, CAP]) for q in range(2)]
        SG = [sbuf(nc, ctx, f"e_SG{q}", [P, CAP]) for q in range(2)]
        G = [sbuf(nc, ctx, f"e_G{q}", [P, CAP]) for q in range(2)]
        Y = [sbuf(nc, ctx, f"e_Y{q}", [P, SC, D]) for q in range(2)]
        px = [psum(nc, ctx, f"e_px{q}", [P, KD, CAP]) for q in range(2)]
        ph = [psum(nc, ctx, f"e_ph{q}", [P, 2, CAP]) for q in range(2)]
        py = [psum(nc, ctx, f"e_py{q}", [P, SC, D]) for q in range(2)]
        block = start(nc, ctx)

        @block.sync
        def _(sp):
            with sp.Fori(0, E0 // NB) as g:
                for q in range(NB):
                    e = g * NB + q
                    if q % 2 == 0:
                        sp.wait_ge(down_ready, ONE + g * NB + q + 2)
                    sp.dma_start(W1[q][:, :, :], w.w1_0[bass.ds(e, 1), :, :].rearrange("o (k p) n -> p (o k) n", p=P)).then_inc(loaded[q], 16)
                    sp.dma_start(W2[q][:, :], w.w2_0[bass.ds(e, 1), :, :].rearrange("o p n -> p (o n)")).then_inc(loaded[q], 16)
                    sp.dma_start(X[q][:, :, :], w.xe_dram[bass.ds(e * CAP, CAP), :].rearrange("(s p) n -> p s n", p=P)).then_inc(loaded[q], 16)

        @block.tensor
        def _(pe):
            def turn(g, i):
                n = g * 2 + i
                for q in range(2):
                    pe.wait_ge(loaded[i * 2 + q], ONE + 48 * g + 48)
                    pe.wait_ge(xT_ready, ONE + n * 2)
                    for s in range(SC):
                        for k in range(KD):
                            last = pe.transpose(px[q][:, k, s * P:(s + 1) * P], X[i * 2 + q][:, s, k * P:(k + 1) * P], w.ident[:, :])
                    last.then_inc(turned, 1)
                for q in range(2):
                    pe.wait_ge(xT_ready, ONE + n * 2 + q + 1)
                    pe.wait_ge(g_ready, ONE + n * 2)
                    for f in range(2):
                        for k in range(KD):
                            last = pe.matmul(ph[q][:, f, :], W1[i * 2 + q][:, k, f * I0:(f + 1) * I0], XT[q][:, k, :], start=k == 0, stop=k == KD - 1)
                    last.then_inc(up_ready, 1)
                for q in range(2):
                    pe.wait_ge(g_ready, ONE + n * 2 + q + 1)
                    pe.wait_ge(y_ready, ONE + n * 2)
                    for s in range(SC):
                        last = pe.matmul(py[q][:, s, :], G[q][:, s * P:(s + 1) * P], W2[i * 2 + q][:, :], start=True, stop=True)
                    last.then_inc(down_ready, 1)

            pe.sem_inc(down_ready, NB)
            with pe.Fori(0, E0 // NB) as g:
                for i in range(NB // 2):
                    turn(g, i)

        @block.scalar
        def _(act):
            with act.Fori(0, E0 // 2) as g:
                for q in range(2):
                    act.wait_ge(up_ready, ONE + g * 2 + q + 1)
                    act.wait_ge(g_ready, ONE + g * 2)
                    act.activation(SG[q][:, :], ph[q][:, 0, :], ACT.Silu).then_inc(silu_ready, 1)
                for q in range(2):
                    act.wait_ge(y_ready, ONE + g * 2 + q + 1)
                    act.dma_start(w.ye_dram[bass.ds((g * 2 + q) * CAP, CAP), :].rearrange("(s p) n -> p s n", p=P), Y[q][:, :, :]).then_inc(stored[q], 16)
            for q in range(2):
                act.wait_ge(stored[q], ONE + 16 * (E0 // 2))

        @block.vector
        def _(dve):
            with dve.Fori(0, E0 // 2) as g:
                for q in range(2):
                    dve.wait_ge(turned, ONE + g * 2 + q + 1)
                    dve.wait_ge(up_ready, ONE + g * 2)
                    dve.tensor_copy(XT[q][:, :, :], px[q][:, :, :]).then_inc(xT_ready, 1)
                for q in range(2):
                    dve.wait_ge(silu_ready, ONE + g * 2 + q + 1)
                    dve.wait_ge(down_ready, ONE + NB + g * 2)
                    dve.tensor_tensor(G[q][:, :], SG[q][:, :], ph[q][:, 1, :], ALU.mult).then_inc(g_ready, 1)
                for q in range(2):
                    dve.wait_ge(down_ready, ONE + NB + g * 2 + q + 1)
                    dve.wait_ge(stored[q], ONE + 16 * g)
                    dve.tensor_copy(Y[q][:, :, :], py[q][:, :, :]).then_inc(y_ready, 1)


def stage_combine(nc, w):
    with ExitStack() as ctx:
        sem = lambda name: semaphore(nc, ctx, name)
        staged, summed, scaled, added = sem("f_staged"), sem("f_summed"), sem("f_scaled"), sem("f_added")
        got = [gpsimd_dma_semaphore(nc, ctx, f"f_got{q}") for q in range(2)]
        stored = sem("f_stored")
        at = [sbuf(nc, ctx, f"f_at{q}", [P, K0], I32) for q in range(2)]
        y = [sbuf(nc, ctx, f"f_y{q}", [P, K0, D]) for q in range(2)]
        acc = [sbuf(nc, ctx, f"f_acc{q}", [P, 1, D]) for q in range(2)]
        block = start(nc, ctx)

        @block.gpsimd
        def _(pool):
            with pool.Fori(0, NT // 2) as g:
                for q in range(2):
                    wait_alone(w, pool, staged, ONE + g * 2 + q + 1)
                    for k in range(K0):
                        pool.indirect_dma_start(out=y[q][:, k, :], out_offset=None, in_=w.ye_dram[:, :],
                                                in_offset=bass.IndirectOffsetOnAxis(ap=at[q][:, k:k + 1], axis=0)).then_inc(got[q], 16)

        @block.vector
        def _(dve):
            def stage(t, q):
                dve.tensor_copy(at[q][:, :].rearrange("p (o k) -> p o k", o=1), w.get_from[:, bass.ds(t, 1), :]).then_inc(staged, 1)

            for q in range(2):
                stage(q, q)
            with dve.Fori(0, B) as b:
                with dve.Fori(0, TB // 2) as gb:
                    g = b * (TB // 2) + gb
                    for q in range(2):
                        t = g * 2 + q
                        dve.wait_ge(got[q], 16 * K0 * g + 16 * K0)
                        p4 = lambda k: w.gate4[:, bass.ds(t, 1), k:k + 1].rearrange("p a b -> p (a b)")
                        y1 = lambda k: y[q][:, k:k + 1, :]
                        dve.tensor_scalar(acc[q][:, :, :], y1(0), p4(0), None, ALU.mult).then_inc(summed, 1)
                        for k in range(1, K0):
                            dve.wait_ge(summed, ONE + K0 * t + k)
                            dve.scalar_tensor_tensor(acc[q][:, :, :], y1(k), p4(k), acc[q][:, :, :], op0=ALU.mult, op1=ALU.add).then_inc(summed, 1)
                        dve.wait_ge(summed, ONE + K0 * t + K0)
                        stage_t = t + 2
                        dve.tensor_copy(at[q][:, :].rearrange("p (o k) -> p o k", o=1), w.get_from[:, bass.ds(stage_t, 1), :]).then_inc(staged, 1)
                        dve.tensor_tensor(acc[q][:, :, :], acc[q][:, :, :], w.modrow[0][:, bass.ds(b, 1), GB * D:(GB + 1) * D], ALU.mult).then_inc(scaled, 1)
                        dve.wait_ge(scaled, ONE + t + 1)
                        xs = w.x[:, bass.ds(t, 1), :]
                        dve.tensor_tensor(xs, xs, acc[q][:, :, :], ALU.add).then_inc(added, 1)

        @block.sync
        def _(sp):
            with sp.Fori(0, NT // 4) as g:
                sp.wait_ge(added, ONE + g * 4 + 4)
                sp.dma_start(w.x2_dram[bass.ds(g * 4 * P, 4 * P), :].rearrange("(t p) n -> p t n", p=P), w.x[:, bass.ds(g * 4, 4), :]).then_inc(stored, 16)
            sp.wait_ge(stored, ONE + 16 * (NT // 4))


MAP = 1024
BLOCK, SEG, DIL = 64, 64, 4
NK = SEG // DIL
U = MAP // P + 1
UK = 3
TPT = 3


def stage_gather(nc, w):
    with ExitStack() as ctx:
        sem = lambda name: semaphore(nc, ctx, name)
        loaded, step, made = sem("i_loaded"), sem("i_step"), sem("i_made")
        key_at_ready, keys_got, all_ready, got = sem("i_key_at_ready"), gpsimd_dma_semaphore(nc, ctx, "i_keys_got"), sem("i_all_ready"), gpsimd_dma_semaphore(nc, ctx, "i_got")
        first = sbuf(nc, ctx, "i_first", [P, UK], I32)
        offs = sbuf(nc, ctx, "i_offs", [P, 1], I32)
        key_at = sbuf(nc, ctx, "i_key_at", [P, UK], I32)
        keys = sbuf(nc, ctx, "i_keys", [P, UK], I32)
        index = sbuf(nc, ctx, "i_index", [P, B, U + UK], I32)
        block = start(nc, ctx)
        m = w.a['L1_attn_mapping']
        by_block = m.rearrange("(n r) -> n r", r=BLOCK)
        last = m[MAP - 1:MAP].rearrange("(n r) -> n r", r=1)
        NBT = P // NK

        @block.sync
        def _(sp):
            sp.dma_start(index[:, 0, 0:U - 1], m.rearrange("(u p) -> p u", p=P), allow_slow_non_contiguous=True).then_inc(loaded, 16)
            sp.dma_start(index[:, 0, U - 1:U], last.broadcast_to([P, 1])).then_inc(loaded, 16)
            for j in range(UK - 1):
                for i in range(NBT):
                    n = j * NBT + i
                    sp.dma_start(first[i * NK:(i + 1) * NK, j:j + 1], by_block[n:n + 1, 0:1].broadcast_to([NK, 1])).then_inc(loaded, 16)
            sp.dma_start(first[:, UK - 1:UK], last.broadcast_to([P, 1])).then_inc(loaded, 16)

        @block.gpsimd
        def _(pool):
            pool.iota(offs[:, :], [[0, 1]], base=0, channel_multiplier=1).then_inc(made, 1)
            pool.wait_ge(key_at_ready, ONE + 1)
            for j in range(UK):
                pool.indirect_dma_start(out=keys[:, j:j + 1], out_offset=None, in_=m.rearrange("(n o) -> n o", o=1),
                                        in_offset=bass.IndirectOffsetOnAxis(ap=key_at[:, j:j + 1], axis=0)).then_inc(keys_got, 16)
            pool.wait_ge(all_ready, ONE + 1)
            for b in range(B):
                for u in range(U + UK):
                    pool.indirect_dma_start(out=w.xg[:, b * (U + UK) + u, :], out_offset=None, in_=w.x2_dram[:, :],
                                            in_offset=bass.IndirectOffsetOnAxis(ap=index[:, b, u:u + 1], axis=0)).then_inc(got, 16)
            pool.wait_ge(got, 16 * B * (U + UK))

        @block.vector
        def _(dve):
            link = linker(dve, step)
            dve.wait_ge(made, ONE + 1)
            link(dve.tensor_scalar(offs[:, :], offs[:, :], NK - 1, DIL.bit_length() - 1, ALU.bitwise_and, ALU.logical_shift_left))
            dve.wait_ge(loaded, ONE + 16 * (3 + (UK - 1) * NBT))
            link(dve.tensor_scalar(key_at[:, :], first[:, :], -SEG, None, ALU.bitwise_and))
            link(dve.tensor_tensor(key_at[:, :], key_at[:, :], offs[:, :].broadcast_to([P, UK]), ALU.add))
            link(dve.tensor_scalar_min(key_at[:, :], key_at[:, :], float(MAP - 1)))
            dve.sem_inc(key_at_ready, 1)
            dve.wait_ge(keys_got, 16 * UK)
            link(dve.tensor_copy(index[:, 0, U:U + UK], keys[:, :]))
            for b in range(1, B):
                link(dve.tensor_scalar_add(index[:, b, :], index[:, 0, :], float(b * S)))
            dve.sem_inc(all_ready, 1)


def stage_keys(nc, w):
    with ExitStack() as ctx:
        sem = lambda name: semaphore(nc, ctx, name)
        norm_ready, turned, hk_ready, projected, kT_ready, made, step = (
            sem(f"k_{n}") for n in ("norm_ready", "turned", "hk_ready", "projected", "kT_ready", "made", "step"))
        loaded = sem("k_loaded")
        xn = sbuf(nc, ctx, "k_xn", [P, UK, D])
        pT = psum(nc, ctx, "k_pT", [P, KD, CH])
        pk = psum(nc, ctx, "k_pk", [P, KD, CH])
        block = start(nc, ctx)
        R = U * 2 * NK

        @block.sync
        def _(sp):
            sp.dma_start(w.Wqkv1[:, :, :], w.a['L1_attn_Wqkv'].rearrange("(k p) n -> p k n", p=P)).then_inc(loaded, 16)
            sp.dma_start(w.Wproj1[:, :, :], w.a['L1_attn_Wproj'].rearrange("(k p) n -> p k n", p=P)).then_inc(loaded, 16)
            sp.dma_start(w.bqk1[:, :], w.a['L1_attn_bqkv'][0:2 * D].rearrange("(c p) -> p c", p=P), allow_slow_non_contiguous=True).then_inc(loaded, 16)
            sp.dma_start(w.bv1[:, :], w.a['L1_attn_bqkv'][2 * D:3 * D].rearrange("(o n) -> o n", o=1).broadcast_to([P, D])).then_inc(loaded, 16)
            sp.dma_start(w.bo1[:, :], w.a['L1_attn_bproj'].rearrange("(o n) -> o n", o=1).broadcast_to([P, D])).then_inc(loaded, 16)

        @block.gpsimd
        def _(pool):
            pool.memset(w.own[:, :], 1.0).then_inc(made, 1)
            pool.wait_ge(made, ONE + 1)
            pool.affine_select(out=w.own[:, :], in_=w.own[:, :], compare_op=ALU.is_ge, fill=0.0, base=0,
                               pattern=[[-NK, P // NK]], channel_multiplier=1).then_inc(made, 1)
            pool.wait_ge(made, ONE + 2)
            pool.affine_select(out=w.own[:, :], in_=w.own[:, :], compare_op=ALU.is_ge, fill=0.0, base=NK - 1,
                               pattern=[[NK, P // NK]], channel_multiplier=-1).then_inc(made, 1)
            pool.wait_ge(made, ONE + 3)

        @block.vector
        def _(dve):
            link = linker(dve, step)
            for b in range(B):
                if b:
                    dve.wait_ge(turned, ONE + b)
                for j in range(UK):
                    i = b * (U + UK) + U + j
                    last = dve.tensor_scalar(xn[:, j, :], w.xg[:, i, :], w.mean_var[:, i, 0:1], w.rstd[:, i:i + 1], ALU.subtract, ALU.mult)
                last.then_inc(norm_ready, 1)
            dve.wait_ge(loaded, ONE + 80)
            link(dve.tensor_scalar_mul(w.bqk1[:, 0:KD], w.bqk1[:, 0:KD], w.SCALE))
            dve.wait_ge(made, ONE + 3)
            link(dve.tensor_copy(w.own_square[:, :].rearrange("p (h d) -> p h d", d=DH), w.own[:, :].rearrange("p (h o) -> p h o", o=1).broadcast_to([P, P // DH, DH])))
            for b in range(B):
                link(dve.tensor_tensor(w.gbo1[:, b, :], w.modrow[1][:, b, GA * D:(GA + 1) * D], w.bo1[:, :], ALU.mult))

        @block.tensor
        def _(pe):
            for b in range(B):
                pe.wait_ge(norm_ready, ONE + b + 1)
                if b:
                    pe.wait_ge(hk_ready, ONE + KD * b)
                for j in range(UK):
                    for k in range(KD):
                        last = pe.transpose(pT[:, k, j * P:(j + 1) * P], xn[:, j, k * P:(k + 1) * P], w.ident[:, :])
                last.then_inc(turned, 1)
                pe.wait_ge(hk_ready, ONE + KD * b + KD)
                if not b:
                    pe.wait_ge(loaded, ONE + 80)
                else:
                    pe.wait_ge(kT_ready, ONE + KD * b)
                for f in range(KD):
                    for k in range(KD):
                        last = pe.matmul(pk[:, f, 0:R], w.Wqkv1[:, k, D + f * P:D + (f + 1) * P], w.hk[:, k, b, 0:R], start=k == 0, stop=k == KD - 1)
                last.then_inc(projected, 1)

        @block.scalar
        def _(act):
            for b in range(B):
                act.wait_ge(turned, ONE + b + 1)
                for k in range(KD):
                    act.activation(w.hk[:, k, b, :], pT[:, k, 0:UK * P], ACT.Identity, scale=w.modcol[:, 1, 2 * CA + k, b:b + 1],
                                   bias=w.modcol[:, 1, 2 * SA + k, b:b + 1]).then_inc(hk_ready, 1)
                act.wait_ge(projected, ONE + b + 1)
                for f in range(KD):
                    act.activation(w.kT[:, f, b, :], pk[:, f, 0:R], ACT.Identity, bias=w.bqk1[:, KD + f:KD + f + 1]).then_inc(kT_ready, 1)


def stage_blocks(nc, w):
    with ExitStack() as ctx:
        sem = lambda name: semaphore(nc, ctx, name)
        s = World()
        s.norm_ready = sem("l_norm_ready")
        s.turned = sem("l_turned")
        s.hT_ready = sem("l_hT_ready")
        s.projected = sem("l_projected")
        s.q_ready = sem("l_q_ready")
        s.kd_ready = sem("l_kd_ready")
        s.scored = sem("l_scored")
        s.top_ready = sem("l_top_ready")
        s.less_ready = sem("l_less_ready")
        s.exp_ready = sem("l_exp_ready")
        s.eps_ready = sem("l_eps_ready")
        s.inverse_ready = sem("l_inverse_ready")
        s.total_ready = sem("l_total_ready")
        s.rep_ready = sem("l_rep_ready")
        s.v_ready = sem("l_v_ready")
        s.vb_ready = sem("l_vb_ready")
        s.vd_ready = sem("l_vd_ready")
        s.summed = sem("l_summed")
        s.oT_ready = sem("l_oT_ready")
        s.out_ready = sem("l_out_ready")
        s.gated = sem("l_gated")
        s.kept = sem("l_kept")
        GH = P // NK
        xn = sbuf(nc, ctx, "l_xn", [P, TPT, D])
        hT = sbuf(nc, ctx, "l_hT", [P, KD, TPT * P])
        qT = sbuf(nc, ctx, "l_qT", [P, KD, TPT * P])
        kd = sbuf(nc, ctx, "l_kd", [P, KD, TPT * 2, GH, NK])
        hr = sbuf(nc, ctx, "l_hr", [P, KD, TPT * 2, GH, NK])
        sc = sbuf(nc, ctx, "l_sc", [P, KD, TPT * P])
        top = sbuf(nc, ctx, "l_top", [P, KD, TPT * 2])
        tot = sbuf(nc, ctx, "l_tot", [P, KD, TPT * P])
        vb = sbuf(nc, ctx, "l_vb", [P, TPT * 2, D])
        vd = sbuf(nc, ctx, "l_vd", [P, TPT * 2, D])
        oT = sbuf(nc, ctx, "l_oT", [P, KD, TPT * P])
        gate = sbuf(nc, ctx, "l_gate", [P, TPT, D])
        pa = psum(nc, ctx, "l_pa", [P, 2, CH])
        pb = psum(nc, ctx, "l_pb", [P, 2, CH])
        pv = psum(nc, ctx, "l_pv", [P, TPT * 2, D])
        block = start(nc, ctx)
        wide = lambda t: t[:, :, :].rearrange("p a n -> p (a n)")[:, 0:TPT * D]
        TURNS = U // TPT

        @block.vector
        def _(dve):
            with dve.Fori(0, B) as b:
                with dve.Fori(0, TURNS) as j:
                    n = b * TURNS + j
                    dve.wait_ge(s.turned, ONE + n)
                    for u in range(TPT):
                        i = b * (U + UK) + j * TPT + u
                        last = dve.tensor_scalar(xn[:, u:u + 1, :], w.xg[:, bass.ds(i, 1), :], w.mean_var[:, bass.ds(i, 1), 0:1].rearrange("p a b -> p (a b)"),
                                                 w.rstd[:, bass.ds(i, 1)], ALU.subtract, ALU.mult)
                    last.then_inc(s.norm_ready, 1)
                    own = w.own[:, :].rearrange("p (o h q) -> p o h q", o=1, q=1).broadcast_to([P, TPT * 2, GH, NK])
                    dve.wait_ge(s.scored, ONE + n + 1)
                    by_block = lambda v: v[:, :, 0:TPT * P].rearrange("p k (m q) -> p k m q", q=BLOCK)
                    over = top[:, :, :].rearrange("p k (m o) -> p k m o", o=1).broadcast_to([P, KD, TPT * 2, BLOCK])
                    dve.reduce_max(top[:, :, :], by_block(pb), AX).then_inc(s.top_ready, 1)
                    dve.wait_ge(s.top_ready, ONE + n + 1)
                    dve.tensor_tensor(by_block(sc), by_block(pb), over, ALU.subtract).then_inc(s.less_ready, 1)
                    dve.wait_ge(s.summed, ONE + n)
                    dve.wait_ge(s.v_ready, ONE + n + 1)
                    dve.tensor_tensor(vb[:, :, :], pv[:, :, :], w.bv1[:, :].rearrange("p (o n) -> p o n", o=1).broadcast_to([P, TPT * 2, D]), ALU.add).then_inc(s.vb_ready, 1)
                    dve.wait_ge(s.vb_ready, ONE + n + 1)
                    for k in range(KD):
                        cols = lambda v: v[:, :, k * P:(k + 1) * P].rearrange("p m (h d) -> p m h d", d=DH)
                        dve.tensor_tensor(cols(vd), cols(vb), own, ALU.mult).then_inc(s.vd_ready, 1)
                    dve.wait_ge(s.total_ready, ONE + n + 1)
                    dve.tensor_scalar_add(tot[:, :, :], pa[:, :, 0:TPT * P], 1e-6).then_inc(s.eps_ready, 1)
                    dve.wait_ge(s.eps_ready, ONE + n + 1)
                    dve.reciprocal(tot[:, :, :], tot[:, :, :]).then_inc(s.inverse_ready, 1)
                    dve.wait_ge(s.inverse_ready, ONE + n + 1)
                    dve.wait_ge(s.summed, ONE + n + 1)
                    dve.tensor_tensor(oT[:, :, :], pb[:, :, 0:TPT * P], tot[:, :, :], ALU.mult).then_inc(s.oT_ready, 1)
                    dve.wait_ge(s.out_ready, ONE + n + 1)
                    dve.tensor_tensor(gate[:, :, :], wide(pa).rearrange("p (t n) -> p t n", t=TPT),
                                      w.modrow[1][:, bass.ds(b, 1), GA * D:(GA + 1) * D].broadcast_to([P, TPT, D]), ALU.mult).then_inc(s.gated, 1)
                    dve.wait_ge(s.gated, ONE + n + 1)
                    dve.tensor_tensor(w.att1[:, bass.ds(n * TPT, TPT), :], gate[:, :, :], w.gbo1[:, bass.ds(b, 1), :].broadcast_to([P, TPT, D]), ALU.add).then_inc(s.kept, 1)
            for b in range(B):
                if b == 0:
                    dve.wait_ge(s.kept, ONE + B * TURNS)
                t0, a0 = b * TB, b * U
                for x, y in ((w.x[:, t0:t0 + U - 1, :], w.att1[:, a0:a0 + U - 1, :]),
                             (w.x[:, t0 + U - 1:t0 + TB, :], w.att1[:, a0 + U - 1:a0 + U, :].broadcast_to([P, TB - U + 1, D]))):
                    dve.tensor_tensor(x, x, y, ALU.add)

        @block.gpsimd
        def _(pool):
            with pool.Fori(0, B) as b:
                with pool.Fori(0, TURNS) as j:
                    n = b * TURNS + j
                    keys = bass.ds(j * TPT * 2 * NK, TPT * 2 * NK)
                    own = w.own[:, :].rearrange("p (o h q) -> p o h q", o=1, q=1).broadcast_to([P, TPT * 2, GH, NK])
                    spread = lambda v: v.rearrange("p a (n o r) -> p (a n) o r", o=1, r=NK).broadcast_to([P, TPT * 2, GH, NK])
                    pool.wait_ge(s.v_ready, ONE + n)
                    for k in range(KD):
                        pool.tensor_copy(hr[:, k, :, :, :], spread(w.hk[:, k, bass.ds(b, 1), keys])).then_inc(s.rep_ready, 1)
                    pool.wait_ge(s.scored, ONE + n)
                    for k in range(KD):
                        pool.tensor_tensor(kd[:, k, :, :, :], spread(w.kT[:, k, bass.ds(b, 1), keys]), own, ALU.mult).then_inc(s.kd_ready, 1)

        @block.tensor
        def _(pe):
            with pe.Fori(0, B * TURNS) as n:
                pe.wait_ge(s.norm_ready, ONE + n + 1)
                pe.wait_ge(s.gated, ONE + n)
                for u in range(TPT):
                    for k in range(KD):
                        last = pe.transpose(pa[:, k, u * P:(u + 1) * P], xn[:, u, k * P:(k + 1) * P], w.ident[:, :])
                last.then_inc(s.turned, 1)
                pe.wait_ge(s.hT_ready, ONE + KD * n + KD)
                pe.wait_ge(s.oT_ready, ONE + n)
                for f in range(KD):
                    for k in range(KD):
                        last = pe.matmul(pb[:, f, 0:TPT * P], w.Wqkv1[:, k, f * P:(f + 1) * P], hT[:, k, :], start=k == 0, stop=k == KD - 1)
                last.then_inc(s.projected, 1)
                pe.wait_ge(s.q_ready, ONE + KD * n + KD)
                pe.wait_ge(s.kd_ready, ONE + KD * n + KD)
                for k in range(KD):
                    for m in range(TPT * 2):
                        at = slice(m * BLOCK, (m + 1) * BLOCK)
                        last = pe.matmul(pb[:, k, at], kd[:, k, m, :, :], qT[:, k, at], start=True, stop=True)
                last.then_inc(s.scored, 1)
                pe.wait_ge(s.rep_ready, ONE + KD * n + KD)
                pe.wait_ge(s.vb_ready, ONE + n)
                for m in range(TPT * 2):
                    for k in range(KD):
                        last = pe.matmul(pv[:, m, :], hr[:, k, m, :, :], w.Wqkv1[:, k, 2 * D:3 * D], start=k == 0, stop=k == KD - 1)
                last.then_inc(s.v_ready, 1)
                pe.wait_ge(s.exp_ready, ONE + n + 1)
                for k in range(KD):
                    last = pe.matmul(pa[:, k, 0:TPT * P], w.own_square[:, :], sc[:, k, :], start=True, stop=True)
                last.then_inc(s.total_ready, 1)
                pe.wait_ge(s.vd_ready, ONE + KD * n + KD)
                for k in range(KD):
                    for m in range(TPT * 2):
                        at = slice(m * BLOCK, (m + 1) * BLOCK)
                        last = pe.matmul(pb[:, k, at], vd[:, m, k * P:(k + 1) * P], sc[:, k, at], start=True, stop=True)
                last.then_inc(s.summed, 1)
                pe.wait_ge(s.oT_ready, ONE + n + 1)
                for u in range(TPT):
                    for k in range(KD):
                        last = pe.matmul(wide(pa)[:, u * D:(u + 1) * D], oT[:, k, u * P:(u + 1) * P], w.Wproj1[:, k, :], start=k == 0, stop=k == KD - 1)
                last.then_inc(s.out_ready, 1)

        @block.scalar
        def _(act):
            with act.Fori(0, B) as b:
                with act.Fori(0, TURNS) as j:
                    n = b * TURNS + j
                    wait_alone(w, act, s.turned, ONE + n + 1)
                    for k in range(KD):
                        act.activation(hT[:, k, :], pa[:, k, 0:TPT * P], ACT.Identity, scale=w.modcol[:, 1, 2 * CA + k, bass.ds(b, 1)],
                                       bias=w.modcol[:, 1, 2 * SA + k, bass.ds(b, 1)]).then_inc(s.hT_ready, 1)
                    act.wait_ge(s.projected, ONE + n + 1)
                    for f in range(KD):
                        act.activation(qT[:, f, :], pb[:, f, 0:TPT * P], ACT.Identity, scale=w.SCALE, bias=w.bqk1[:, f:f + 1]).then_inc(s.q_ready, 1)
                    act.wait_ge(s.less_ready, ONE + n + 1)
                    act.activation(sc[:, :, :], sc[:, :, :], ACT.Exp).then_inc(s.exp_ready, 1)


E1, K1, I1 = 8, 2, 512


def stage_gates(nc, w):
    with ExitStack() as ctx:
        sem = lambda name: semaphore(nc, ctx, name)
        step, exp_request, exp_done, made = sem("t_step"), sem("t_exp_request"), sem("t_exp_done"), sem("t_made")
        cols_ready, turned, rows_ready, stored = sem("t_cols_ready"), sem("t_turned"), sem("t_rows_ready"), sem("t_stored")
        N = NT * K1
        top = sbuf(nc, ctx, "t_top", [P, NT])
        total = sbuf(nc, ctx, "t_total", [P, NT])
        m8 = sbuf(nc, ctx, "t_m8", [P, NT, 8])
        i8 = sbuf(nc, ctx, "t_i8", [P, NT, 8], U32)
        i2 = sbuf(nc, ctx, "t_i2", [P, N])
        col_i = sbuf(nc, ctx, "t_col_i", [P, E1], I32)
        col = sbuf(nc, ctx, "t_col", [P, E1])
        chosen = sbuf(nc, ctx, "t_chosen", [P, N, E1])
        both = sbuf(nc, ctx, "t_both", [P, NT, 2 * E1])
        rows = sbuf(nc, ctx, "t_rows", [2 * E1, NT, P])
        pr = psum(nc, ctx, "t_pr", [2 * E1, NT, P])
        block = start(nc, ctx)

        @block.gpsimd
        def _(pool):
            pool.iota(col_i[:, :], [[1, E1]], base=0, channel_multiplier=0).then_inc(made, 1)

        @block.scalar
        def _(act):
            act.wait_ge(exp_request, ONE + 1)
            act.activation(w.logits1[:, :, :], w.logits1[:, :, :], ACT.Exp).then_inc(exp_done, 1)

        @block.vector
        def _(dve):
            link = linker(dve, step)
            probs = w.logits1
            softmax_rows(dve, link, probs, top, total, exp_request, exp_done)
            for t in range(NT):
                last = dve.max(m8[:, t, :], probs[:, t, :])
            link(last)
            for t in range(NT):
                last = dve.max_index(i8[:, t, :], m8[:, t, :], probs[:, t, :])
            link(last)
            link(dve.tensor_copy(i2[:, :].rearrange("p (t k) -> p t k", k=K1), i8[:, :, 0:K1]))
            dve.wait_ge(made, ONE + 1)
            link(dve.tensor_copy(col[:, :], col_i[:, :]))
            link(dve.tensor_tensor(chosen[:, :, :], col[:, :].rearrange("p (o e) -> p o e", o=1).broadcast_to([P, N, E1]),
                                   i2[:, :].rearrange("p (n o) -> p n o", o=1).broadcast_to([P, N, E1]), ALU.is_equal))
            by_k = chosen[:, :, :].rearrange("p (t k) e -> p t k e", k=K1)
            dve.tensor_copy(both[:, :, 0:E1], probs[:, :, :])
            link(dve.tensor_tensor(both[:, :, E1:2 * E1], by_k[:, :, 0, :], by_k[:, :, 1, :], ALU.add))
            dve.sem_inc(cols_ready, 1)
            dve.wait_ge(turned, ONE + 1)
            dve.tensor_copy(rows[:, :, :], pr[:, :, :]).then_inc(rows_ready, 1)

        @block.tensor
        def _(pe):
            pe.wait_ge(cols_ready, ONE + 1)
            for t in range(NT):
                last = pe.transpose(pr[:, t, :], both[:, t, :], w.ident[:, :])
            last.then_inc(turned, 1)

        @block.sync
        def _(sp):
            sp.wait_ge(rows_ready, ONE + 1)
            sp.dma_start(w.gates_dram[:, :], rows[:, :, :].rearrange("e t p -> e (t p)")).then_inc(stored, 16)
            sp.wait_ge(stored, ONE + 16)


def stage_shared(nc, w):
    with ExitStack() as ctx:
        sem = lambda name: semaphore(nc, ctx, name)
        loaded, a_ready, b_ready, silu_ready, u_ready, z_ready, z_out = (
            sem(f"z_{n}") for n in ("loaded", "a_ready", "b_ready", "silu_ready", "u_ready", "z_ready", "z_out"))
        IB = I1 // P
        W1 = sbuf(nc, ctx, "z_W1", [P, KD, I1])
        W2 = sbuf(nc, ctx, "z_W2", [P, KD, I1])
        W3 = sbuf(nc, ctx, "z_W3", [P, IB, D])
        si = sbuf(nc, ctx, "z_si", [P, IB, CH])
        u = sbuf(nc, ctx, "z_u", [P, IB, CH])
        pa = psum(nc, ctx, "z_pa", [P, 2, CH])
        pb = psum(nc, ctx, "z_pb", [P, 2, CH])
        pz = psum(nc, ctx, "z_pz", [P, KD, CH])
        block = start(nc, ctx)

        @block.sync
        def _(sp):
            for dst, name in ((W1, 'L1_ffn_sw1'), (W2, 'L1_ffn_sw2'), (W3, 'L1_ffn_sw3')):
                sp.dma_start(dst[:, :, :], w.a[name].rearrange("(k p) n -> p k n", p=P)).then_inc(loaded, 16)

        @block.tensor
        def _(pe):
            pe.wait_ge(loaded, ONE + 48)
            with pe.Fori(0, NC) as c:
                h = lambda k: w.hT1[:, k, bass.ds(c * CH, CH)]
                for i in range(IB):
                    if i < 2:
                        pe.wait_ge(u_ready, ONE + IB * c)
                    else:
                        pe.wait_ge(u_ready, ONE + IB * c + i - 1)
                    for k in range(KD):
                        last = pe.matmul(pa[:, i % 2, :], W1[:, k, i * P:(i + 1) * P], h(k), start=k == 0, stop=k == KD - 1)
                    last.then_inc(a_ready, 1)
                    for k in range(KD):
                        last = pe.matmul(pb[:, i % 2, :], W2[:, k, i * P:(i + 1) * P], h(k), start=k == 0, stop=k == KD - 1)
                    last.then_inc(b_ready, 1)
                pe.wait_ge(u_ready, ONE + IB * c + IB)
                pe.wait_ge(z_out, ONE + c)
                for f in range(KD):
                    for i in range(IB):
                        last = pe.matmul(pz[:, f, :], W3[:, i, f * P:(f + 1) * P], u[:, i, :], start=i == 0, stop=i == IB - 1)
                last.then_inc(z_ready, 1)

        @block.scalar
        def _(act):
            with act.Fori(0, NC) as c:
                act.wait_ge(u_ready, ONE + IB * c)
                for i in range(IB):
                    act.wait_ge(a_ready, ONE + IB * c + i + 1)
                    act.activation(si[:, i, :], pa[:, i % 2, :], ACT.Silu).then_inc(silu_ready, 1)

        @block.vector
        def _(dve):
            with dve.Fori(0, NC) as c:
                dve.wait_ge(z_ready, ONE + c)
                for i in range(IB):
                    dve.wait_ge(silu_ready, ONE + IB * c + i + 1)
                    dve.wait_ge(b_ready, ONE + IB * c + i + 1)
                    dve.tensor_tensor(u[:, i, :], si[:, i, :], pb[:, i % 2, :], ALU.mult).then_inc(u_ready, 1)
                dve.wait_ge(z_ready, ONE + c + 1)
                dve.tensor_copy(w.yT[:, :, bass.ds(c * CH, CH)], pz[:, :, :]).then_inc(z_out, 1)


def stage_experts1(nc, w):
    with ExitStack() as ctx:
        sem = lambda name: semaphore(nc, ctx, name)
        biases_loaded = sem("y_biases_loaded")
        w_loaded = [sem(f"y_w_loaded{q}") for q in range(2)]
        g_loaded = [sem(f"y_g_loaded{q}") for q in range(4)]
        gates_used = sem("y_gates_used")
        xs_ready, p1_ready, p3_ready, silu_ready, x3_ready, p2_ready, t_ready, y_added = (
            sem(f"y_{n}") for n in ("xs_ready", "p1_ready", "p3_ready", "silu_ready", "x3_ready", "p2_ready", "t_ready", "y_added"))
        W = [[sbuf(nc, ctx, f"y_W{i}{q}", [P, KD, D]) for i in (1, 2, 3)] for q in range(2)]
        bias = sbuf(nc, ctx, "y_bias", [P, 3, KD, E1])
        score = [sbuf(nc, ctx, f"y_score{q}", [P, 1, CH]) for q in range(4)]
        mask = [sbuf(nc, ctx, f"y_mask{q}", [P, 1, CH]) for q in range(4)]
        xs = [sbuf(nc, ctx, f"y_xs{q}", [P, KD, CH]) for q in range(2)]
        hh = sbuf(nc, ctx, "y_hh", [P, KD, CH])
        x3 = sbuf(nc, ctx, "y_x3", [P, KD, CH])
        tt = [sbuf(nc, ctx, f"y_tt{q}", [P, KD, CH]) for q in range(2)]
        p1 = psum(nc, ctx, "y_p1", [P, KD, CH])
        p2 = psum(nc, ctx, "y_p2", [P, KD, CH])
        p3 = psum(nc, ctx, "y_p3", [P, KD, CH])
        block = start(nc, ctx)
        a = w.a

        def load_weights(engine, e, eq):
            for i, name in enumerate(('L1_ffn_w1', 'L1_ffn_w2', 'L1_ffn_w3')):
                engine.dma_start(W[eq][i][:, :, :], a[name][bass.ds(e, 1), :, :].rearrange("o (k p) n -> p (o k) n", p=P)).then_inc(w_loaded[eq], 16)

        @block.sync
        def _(sp):
            for i, name in enumerate(('L1_ffn_b1', 'L1_ffn_b2', 'L1_ffn_b3')):
                sp.dma_start(bias[:, i, :, :], a[name].rearrange("(k p) e -> p k e", p=P)).then_inc(biases_loaded, 16)
            load_weights(sp, 0, 0)
            with sp.Fori(0, E1) as e:
                with sp.Fori(0, NC // 4) as cg:
                    for q in range(4):
                        n = e * NC + cg * 4 + q
                        if q % 2 == 0:
                            sp.wait_ge(gates_used, ONE + n)
                        cols = bass.ds(cg * (4 * CH) + q * CH, CH)
                        sp.dma_start(score[q][:, 0, :], w.gates_dram[bass.ds(e, 1), cols].broadcast_to([P, CH])).then_inc(g_loaded[q], 16)
                        sp.dma_start(mask[q][:, 0, :], w.gates_dram[bass.ds(e + E1, 1), cols].broadcast_to([P, CH])).then_inc(g_loaded[q], 16)

        @block.tensor
        def _(pe):
            with pe.Fori(0, E1 // 2) as g:
                for eq in range(2):
                    wait_alone(w, pe, w_loaded[eq], ONE + 48 * g + 48)
                    with pe.Fori(0, NC // 2) as cg:
                        for q in range(2):
                            n = (g * 2 + eq) * NC + cg * 2 + q
                            pe.wait_ge(xs_ready, ONE + n + 1)
                            pe.wait_ge(silu_ready, ONE + KD * n)
                            for f in range(KD):
                                for k in range(KD):
                                    last = pe.matmul(p1[:, f, :], W[eq][0][:, k, f * P:(f + 1) * P], xs[q][:, k, :], start=k == 0, stop=k == KD - 1)
                                last.then_inc(p1_ready, 1)
                            pe.wait_ge(x3_ready, ONE + KD * n)
                            for f in range(KD):
                                for k in range(KD):
                                    last = pe.matmul(p3[:, f, :], W[eq][2][:, k, f * P:(f + 1) * P], xs[q][:, k, :], start=k == 0, stop=k == KD - 1)
                                last.then_inc(p3_ready, 1)
                            pe.wait_ge(silu_ready, ONE + KD * n + KD)
                            pe.wait_ge(t_ready, ONE + KD * n)
                            for f in range(KD):
                                for k in range(KD):
                                    last = pe.matmul(p2[:, f, :], W[eq][1][:, k, f * P:(f + 1) * P], hh[:, k, :], start=k == 0, stop=k == KD - 1)
                                if f == KD - 1:
                                    last.then_inc(p2_ready, 1)

        @block.scalar
        def _(act):
            act.wait_ge(biases_loaded, ONE + 48)
            act.sem_inc(gates_used, 2)

            def pair(g, last):
                for eq in range(2):
                    e = g * 2 + eq
                    for c in range(NC):
                        n = e * NC + c
                        if last:
                            act.wait_ge(p2_ready, ONE + n)
                        else:
                            wait_alone(w, act, p2_ready, ONE + n)
                        if c == 1 and not (last and eq == 1):
                            load_weights(act, e + 1, 1 - eq)
                        for f in range(KD):
                            if last:
                                act.wait_ge(p1_ready, ONE + KD * n + f + 1)
                            else:
                                wait_alone(w, act, p1_ready, ONE + KD * n + f + 1)
                            act.activation(hh[:, f, :], p1[:, f, :], ACT.Silu, bias=bias[:, 0, f, bass.ds(e, 1)]).then_inc(silu_ready, 1)

            with act.Fori(0, E1 // 2 - 1) as g:
                pair(g, False)
            pair(E1 // 2 - 1, True)

        @block.vector
        def _(dve):
            def scale(e, c):
                q, n = c % 2, e * NC + c
                dve.wait_ge(g_loaded[c % 4], ONE + e * (8 * NC) + c // 4 * 32 + 32)
                if not (isinstance(e, int) and n < 2):
                    dve.wait_ge(p3_ready, ONE + KD * (n - 1))
                dve.tensor_tensor(xs[q][:, :, :], w.hT1[:, :, c * CH:(c + 1) * CH], score[c % 4][:, :, :].broadcast_to([P, KD, CH]), ALU.mult).then_inc(xs_ready, 1)

            def expert(e, last):
                for c in range(NC):
                    q, n = c % 2, e * NC + c
                    for f in range(KD):
                        dve.wait_ge(p3_ready, ONE + KD * n + f + 1)
                        if f == 0:
                            dve.wait_ge(t_ready, ONE + KD * n)
                        dve.scalar_tensor_tensor(x3[:, f, :], p3[:, f, :], bias[:, 2, f, bass.ds(e, 1)], mask[c % 4][:, 0, :], op0=ALU.add, op1=ALU.mult).then_inc(x3_ready, 1)
                    if c < NC - 1:
                        scale(e, c + 1)
                    elif not last:
                        scale(e + 1, 0)
                    dve.wait_ge(p2_ready, ONE + n + 1)
                    dve.wait_ge(x3_ready, ONE + KD * n + KD)
                    dve.sem_inc(gates_used, 1)
                    dve.wait_ge(y_added, ONE + n)
                    for f in range(KD):
                        dve.scalar_tensor_tensor(tt[q][:, f, :], p2[:, f, :], bias[:, 1, f, bass.ds(e, 1)], x3[:, f, :], op0=ALU.add, op1=ALU.mult).then_inc(t_ready, 1)

            dve.wait_ge(biases_loaded, ONE + 48)
            scale(0, 0)
            with dve.Fori(0, E1 - 1) as e:
                expert(e, False)
            expert(E1 - 1, True)

        @block.gpsimd
        def _(pool):
            with pool.Fori(0, E1) as e:
                with pool.Fori(0, NC // 2) as cg:
                    for q in range(2):
                        n = e * NC + cg * 2 + q
                        pool.wait_ge(t_ready, ONE + KD * n + KD)
                        ys = w.yT[:, :, bass.ds(cg * (2 * CH) + q * CH, CH)]
                        pool.tensor_tensor(ys, ys, tt[q][:, :, :], ALU.add).then_inc(y_added, 1)


def stage_output(nc, w):
    with ExitStack() as ctx:
        sem = lambda name: semaphore(nc, ctx, name)
        staged, turned, gated, added, stored = (sem(f"o_{n}") for n in ("staged", "turned", "gated", "added", "stored"))
        ys = [sbuf(nc, ctx, f"o_ys{q}", [P, KD, CH]) for q in range(2)]
        t = [sbuf(nc, ctx, f"o_t{q}", [P, CT, D]) for q in range(2)]
        py = [psum(nc, ctx, f"o_py{q}", [P, CT, D]) for q in range(2)]
        block = start(nc, ctx)

        @block.scalar
        def _(act):
            with act.Fori(0, NC // 2) as g:
                for q in range(2):
                    wait_alone(w, act, turned, ONE + g * 2)
                    act.activation(ys[q][:, :, :], w.yT[:, :, bass.ds(g * (2 * CH) + q * CH, CH)], ACT.Copy).then_inc(staged, 1)

        @block.tensor
        def _(pe):
            with pe.Fori(0, NC // 2) as g:
                for q in range(2):
                    pe.wait_ge(staged, ONE + g * 2 + q + 1)
                    pe.wait_ge(gated, ONE + g * 2)
                    for i in range(CT):
                        for k in range(KD):
                            last = pe.transpose(py[q][:, i, k * P:(k + 1) * P], ys[q][:, k, i * P:(i + 1) * P], w.ident[:, :])
                    last.then_inc(turned, 1)

        @block.vector
        def _(dve):
            with dve.Fori(0, B) as b:
                with dve.Fori(0, NC // B // 2) as gb:
                    for q in range(2):
                        c = b * (NC // B) + gb * 2 + q
                        dve.wait_ge(turned, ONE + c + 1)
                        dve.tensor_tensor(t[q][:, :, :], py[q][:, :, :], w.modrow[1][:, bass.ds(b, 1), GB * D:(GB + 1) * D].broadcast_to([P, CT, D]), ALU.mult).then_inc(gated, 1)
                        dve.wait_ge(gated, ONE + c + 1)
                        xs = w.x[:, bass.ds(c * CT, CT), :]
                        dve.tensor_tensor(xs, xs, t[q][:, :, :], ALU.add).then_inc(added, 1)

        @block.sync
        def _(sp):
            with sp.Fori(0, NC) as c:
                sp.wait_ge(added, ONE + c + 1)
                sp.dma_start(w.out[bass.ds(c * CH, CH), :].rearrange("(t p) n -> p t n", p=P), w.x[:, bass.ds(c * CT, CT), :]).then_inc(stored, 16)
            sp.wait_ge(stored, ONE + 16 * NC)


def clear_semaphores(nc):
    with nc.semaphore("first") as s:
        first = s.num
    numbers = [first]
    while True:
        with nc.semaphore("next") as s:
            if s.num == first:
                break
            numbers.append(s.num)
    nc.all_engine_barrier()
    nc.gpsimd.sem_clear(range(min(numbers), max(numbers) + 1))
    nc.all_engine_barrier()


def build(nc, a, out, stages=99):
    w = World()
    ctx = ExitStack()
    with ctx:
        w.passed = ctx.enter_context(nc.semaphore("passed"))
        w.band_stored = gpsimd_dma_semaphore(nc, ctx, "band_stored")
        w.SCALE = DH ** -0.5
        w.EXT = 2 * REL + 1 + 2 * (P - 1)
        w.c = [a['L0_c'], a['L1_c']]
        w.wmod = [a['L0_wmod'], a['L1_wmod']]
        w.rel_biasT = a['L0_attn_rel_bias']
        w.W_qkv0, w.W_out0, w.router_w = a['L0_attn_W_qkv'], a['L0_attn_W_out'], a['L0_ffn_router_w']
        w.b_qkv0, w.b_out0 = a['L0_attn_b_qkv'], a['L0_attn_b_out']
        w.x_dram = a['L0_attn_x'].rearrange("b s d -> (b s) d")
        w.a, w.out = a, out.rearrange("b s d -> (b s) d")
        dram = lambda name, shape, dt=F32: nc.dram_tensor(name, shape, dt).ap()
        w.ext_dram = dram("ext_dram", [NH, w.EXT])
        w.far_dram = dram("far_dram", [H, 2])
        w.qk_parts = [dram(f"{n}_parts", [3, NH * DH, S], BF16) for n in "qk"]
        w.attT_dram = dram("attT_dram", [NH, DH + 1, S])
        w.inverse_dram = dram("inverse_dram", [NH, S])
        w.BAND = 2 * REL + P
        w.skew_dram = dram("skew_dram", [NH, P * (w.EXT + 1)])
        w.xe_dram = dram("xe_dram", [E0 * CAP, D])
        w.ye_dram = dram("ye_dram", [E0 * CAP, D])
        w.x2_dram = dram("x2_dram", [B * S, D])
        w.w1_0, w.w2_0 = a['L0_ffn_w1'], a['L0_ffn_w2']
        w.gates_dram = dram("gates_dram", [2 * E1, B * S])
        w.v_dram = dram("v_dram", [NH, S, DH])
        sb = lambda name, shape, dt=F32: sbuf(nc, ctx, name, shape, dt)
        w.ident = sb("ident", [P, P])
        w.zeros = sb("zeros", [P, 2048])
        w.eps = sb("eps", [P, 1])
        w.modrow = [sb(f"modrow{l}", [P, B, 6 * D]) for l in range(2)]
        w.modcol = sb("modcol", [P, 2, 12, B])
        w.far = sb("far", [P, NH, 2])
        w.Wout0 = sb("Wout0", [P, KD, D])
        w.Wr0 = sb("Wr0", [P, KD, 64])
        w.Wg1 = sb("Wg1", [P, KD, E1])
        w.bo0 = sb("bo0", [P, D])
        w.gbo0 = sb("gbo0", [P, B, D])
        w.x = sb("x", [P, NT, D])
        with ExitStack() as qkv:
            w.Wqkv0 = sbuf(nc, qkv, "Wqkv0", [P, KD, 3 * D])
            w.bqk = sbuf(nc, qkv, "bqk", [P, 2 * KD])
            w.bv0 = sbuf(nc, qkv, "bv0", [P, D])
            stage_constants(nc, w)
            stage_qkv(nc, w)
        stage_attention(nc, w)
        stage_project(nc, w)
        w.mean_var = sb("mean_var", [P, NT, 2])
        w.rstd = sb("rstd", [P, NT])
        with ExitStack() as moe:
            w.gate4 = sbuf(nc, moe, "gate4", [P, NT, K0])
            w.put_at = sbuf(nc, moe, "put_at", [P, NT, K0], I32)
            w.get_from = sbuf(nc, moe, "get_from", [P, NT + 2, K0], I32)
            with ExitStack() as tokens:
                w.h = sbuf(nc, tokens, "h", [P, NT, D])
                w.logits0 = sbuf(nc, tokens, "logits0", [P, NT, E0])
                stage_norm(nc, w, w.x, NT, w.mean_var, w.rstd, "n0")
                stage_router(nc, w, w.x, w.mean_var, w.rstd, w.h, None, 0, w.Wr0, w.logits0, "g0")
                stage_route(nc, w)
                stage_scatter(nc, w)
            stage_experts(nc, w)
            stage_combine(nc, w)
        clear_semaphores(nc)
        with ExitStack() as att:
            w.xg = sbuf(nc, att, "xg", [P, B * (U + UK), D])
            w.att1 = sbuf(nc, att, "att1", [P, B * U, D])
            w.Wqkv1 = sbuf(nc, att, "Wqkv1", [P, KD, 3 * D])
            w.Wproj1 = sbuf(nc, att, "Wproj1", [P, KD, D])
            w.bqk1 = sbuf(nc, att, "bqk1", [P, 2 * KD])
            w.bv1 = sbuf(nc, att, "bv1", [P, D])
            w.bo1 = sbuf(nc, att, "bo1", [P, D])
            w.gbo1 = sbuf(nc, att, "gbo1", [P, B, D])
            w.own_square = sbuf(nc, att, "own_square", [P, P])
            w.own = sbuf(nc, att, "own", [P, P // NK])
            w.hk = sbuf(nc, att, "hk", [P, KD, B, UK * P])
            w.kT = sbuf(nc, att, "kT", [P, KD, B, U * 2 * NK])
            stage_gather(nc, w)
            stage_norm(nc, w, w.xg, B * (U + UK), w.mean_var, w.rstd, "n1")
            stage_keys(nc, w)
            stage_blocks(nc, w)
            if stages == 5:
                return w
        w.hT1 = sb("hT1", [P, KD, B * S])
        w.yT = sb("yT", [P, KD, B * S])
        w.logits1 = sb("logits1", [P, NT, E1])
        stage_norm(nc, w, w.x, NT, w.mean_var, w.rstd, "n2")
        stage_router(nc, w, w.x, w.mean_var, w.rstd, None, w.hT1, 1, w.Wg1, w.logits1, "g1")
        stage_gates(nc, w)
        stage_shared(nc, w)
        stage_experts1(nc, w)
        stage_output(nc, w)
    return w


_INS = ['L0_attn_x', 'L0_attn_W_qkv', 'L0_attn_b_qkv', 'L0_attn_W_out', 'L0_attn_b_out', 'L0_attn_rel_bias',
        'L0_ffn_router_w', 'L0_ffn_w1', 'L0_ffn_w2', 'L0_c', 'L0_wmod', 'L1_attn_Wqkv', 'L1_attn_bqkv',
        'L1_attn_Wproj', 'L1_attn_bproj', 'L1_attn_mapping', 'L1_ffn_gate_w', 'L1_ffn_w1', 'L1_ffn_b1',
        'L1_ffn_w2', 'L1_ffn_b2', 'L1_ffn_w3', 'L1_ffn_b3', 'L1_ffn_sw1', 'L1_ffn_sw2', 'L1_ffn_sw3', 'L1_c', 'L1_wmod']
_TURNED = {'L1_ffn_b1', 'L1_ffn_b2', 'L1_ffn_b3', 'L0_c', 'L1_c', 'L0_attn_rel_bias', 'L1_ffn_gate_w', 'L1_ffn_w1', 'L1_ffn_w2', 'L1_ffn_w3', 'L1_ffn_sw1', 'L1_ffn_sw2', 'L1_ffn_sw3'}


def kernel(**inputs):
    import numpy as _np
    import concourse.bacc as _bacc
    from concourse import mybir as _mybir
    from concourse.bass_utils import run_bass_kernel_spmd as _run

    nc = _bacc.Bacc("TRN2", target_bir_lowering=False, num_devices=1)
    arrays, args = {}, {}
    for name in _INS:
        a = _np.asarray(inputs[name])
        a = _np.ascontiguousarray(_np.swapaxes(a, -1, -2) if name in _TURNED else a)
        arrays[f"in_{name}_dram"] = a
        args[name] = nc.dram_tensor(f"in_{name}_dram", a.shape, _mybir.dt.from_np(a.dtype), kind="ExternalInput").ap()
    out = nc.dram_tensor("out_dram", (B, S, D), _mybir.dt.from_np(_np.dtype("float32")), kind="ExternalOutput").ap()
    build(nc, args, out)
    r = _run(nc, [arrays], core_ids=[0])
    return r.results[0]["out_dram"]
```

```python
import numpy as np
import concourse.bass as bass
from concourse import mybir
from contextlib import ExitStack

F32 = mybir.dt.float32
BF16 = mybir.dt.bfloat16
I32 = mybir.dt.int32
U32 = mybir.dt.uint32
ALU = mybir.AluOpType
ACT = mybir.ActivationFunctionType
AX = mybir.AxisListType.X

P = 128
B, S, D = 2, 2048, 256
NT = B * S // P
TB = S // P
KD = D // P
CH = 512
NC = B * S // CH
CT = CH // P
H, DH = 16, 16
NH = B * H
REL = 256
EPS = 1e-5
SA, CA, GA, SB_, CB, GB = range(6)
ONE = 1


class World:
    pass


def sbuf(nc, ctx, name, shape, dt=F32):
    return ctx.enter_context(nc.sbuf_tensor(name, shape, dt))


def psum(nc, ctx, name, shape, dt=F32):
    return ctx.enter_context(nc.psum_tensor(name, shape, dt))


def semaphore(nc, ctx, name):
    s = ctx.enter_context(nc.semaphore(name))
    nc.gpsimd.sem_inc(s, ONE)
    return s


def gpsimd_dma_semaphore(nc, ctx, name):
    return ctx.enter_context(nc.semaphore(name))


def start(nc, ctx):
    nc.all_engine_barrier()
    return ctx.enter_context(nc.Block())


def linker(engine, sem, first=0):
    count = [first]

    def link(instruction):
        count[0] += 1
        instruction.then_inc(sem, 1)
        engine.wait_ge(sem, ONE + count[0])

    return link


def wait_alone(w, engine, sem, value):
    engine.wait_ge(sem, value)
    engine.sem_inc(w.passed, 1)


def stage_constants(nc, w):
    with ExitStack() as ctx:
        sem = lambda name: semaphore(nc, ctx, name)
        loaded = sem("a_loaded")
        c_loaded = sem("a_c_loaded")
        mod_loaded = sem("a_mod_loaded")
        x_loaded = [sem(f"a_x_loaded{c}") for c in range(NC)]
        stat_step = sem("a_stat_step")
        var_ready = sem("a_var_ready")
        std_ready = sem("a_std_ready")
        filled = sem("a_filled")
        act_step = sem("a_act_step")
        dve_step = sem("a_dve_step")
        silu_ready = sem("a_silu_ready")
        mod_ready = [sem(f"a_mod_ready{i}") for i in range(2)]
        mod_used = [sem(f"a_mod_used{i}") for i in range(2)]
        col_ready = sem("a_col_ready")
        bias_exp_in = sem("a_bias_exp_in")
        bias_exp = sem("a_bias_exp")
        bias_rows_ready = sem("a_bias_rows_ready")
        bias_stored = sem("a_bias_stored")
        far_loaded = sem("a_far_loaded")
        pool_step = sem("a_pool_step")
        map_ready = sem("a_map_ready")
        map_loaded = sem("a_map_loaded")

        cT = sbuf(nc, ctx, "cT", [P, 2, KD, B])
        ce = sbuf(nc, ctx, "ce", [P, 2, KD, B])
        sc = sbuf(nc, ctx, "sc", [P, 2, KD, B])
        wm = sbuf(nc, ctx, "wm", [P, 2, KD, 6 * D])
        rb = sbuf(nc, ctx, "rb", [H, 2 * REL + 1])
        rbm = sbuf(nc, ctx, "rbm", [H, 1])
        rbd = sbuf(nc, ctx, "rbd", [H, 2 * REL + 1])
        ext = sbuf(nc, ctx, "ext", [H, w.EXT])
        row = sbuf(nc, ctx, "row", [P, D * 2])
        kp = sbuf(nc, ctx, "kp", [P, 6], I32)
        m0 = sbuf(nc, ctx, "m0", [P, 3], I32)
        st = sbuf(nc, ctx, "a_st", [P, NT, 6])
        ps = [psum(nc, ctx, f"a_ps{i}", [P, CH]) for i in range(2)]
        pc = psum(nc, ctx, "a_pc", [P, 2, 12, B])
        block = start(nc, ctx)

        small = [(cT[:, l, :, :], w.c[l].rearrange("(k p) b -> p k b", p=P)) for l in range(2)]
        wmods = [(wm[:, l, :, :], w.wmod[l].rearrange("(k p) n -> p k n", p=P)) for l in range(2)]
        weights = [
            (rb[:, :], w.rel_biasT),
            (w.Wqkv0[:, :, :], w.W_qkv0.rearrange("(k p) n -> p k n", p=P)),
            (w.Wout0[:, :, :], w.W_out0.rearrange("(k p) n -> p k n", p=P)),
            (w.Wr0[:, :, :], w.router_w.rearrange("(k p) n -> p k n", p=P)),
            (w.Wg1[:, :, :], w.a['L1_ffn_gate_w'].rearrange("(k p) n -> p k n", p=P)),
            (w.bqk[:, :], w.b_qkv0[0:2 * D].rearrange("(c p) -> p c", p=P)),
            (w.bv0[:, :], w.b_qkv0[2 * D:3 * D].rearrange("(o n) -> o n", o=1).broadcast_to([P, D])),
            (w.bo0[:, :], w.b_out0.rearrange("(o n) -> o n", o=1).broadcast_to([P, D])),
        ]
        MAPS = 6

        @block.sync
        def _(sp):
            for dst, src in small:
                sp.dma_start(dst, src, allow_slow_non_contiguous=True).then_inc(c_loaded, 16)
            for dst, src in wmods:
                sp.dma_start(dst, src).then_inc(mod_loaded, 16)
            for dst, src in weights:
                sp.dma_start(dst, src, allow_slow_non_contiguous=True).then_inc(loaded, 16)
            sp.wait_ge(bias_rows_ready, ONE + 1)
            for b in range(B):
                sp.dma_start(w.ext_dram[b * H:(b + 1) * H, :], ext[:, :]).then_inc(bias_stored, 16)
            sp.dma_start(w.far_dram[:, 0:1], rbd[:, 0:1], allow_slow_non_contiguous=True).then_inc(bias_stored, 16)
            sp.dma_start(w.far_dram[:, 1:2], rbd[:, 2 * REL:2 * REL + 1], allow_slow_non_contiguous=True).then_inc(bias_stored, 16)
            sp.wait_ge(bias_stored, ONE + 64)
            for b in range(B):
                sp.dma_start(w.far[:, b * H:(b + 1) * H, :], w.far_dram.rearrange("h (o t) -> o h t", o=1).broadcast_to([P, H, 2])).then_inc(far_loaded, 16)
            sp.wait_ge(far_loaded, ONE + 32)

        @block.scalar
        def _(act):
            for c in range(NC):
                act.dma_start(w.x[:, c * CT:(c + 1) * CT, :],
                              w.x_dram[c * CH:(c + 1) * CH, :].rearrange("(t p) n -> p t n", p=P)).then_inc(x_loaded[c], 16)
            act.wait_ge(c_loaded, ONE + 16 * len(small))
            act.activation(ce[:, :, :, :], cT[:, :, :, :], ACT.Exp, scale=-1.0).then_inc(act_step, 1)
            act.wait_ge(bias_exp_in, ONE + 1)
            act.activation(ext[:, P - 1:P + 2 * REL], rbd[:, :], ACT.Exp).then_inc(bias_exp, 1)
            act.wait_ge(var_ready, ONE + NT)
            act.wait_ge(pool_step, ONE + 4)
            act.activation(w.rstd0[:, :], w.mean_var0[:, :, 1], ACT.Sqrt, bias=w.eps[:, 0:1]).then_inc(std_ready, 1)

        @block.tensor
        def _(pe):
            pe.wait_ge(silu_ready, ONE + 1)
            pe.wait_ge(mod_loaded, ONE + 16 * len(wmods))
            n = 0
            for l in range(2):
                for b in range(B):
                    for j in range(3):
                        if n >= 2:
                            pe.wait_ge(mod_used[n % 2], ONE + n // 2)
                        for k in range(KD):
                            last = pe.matmul(ps[n % 2][:, :], sc[:, l, k, b:b + 1].broadcast_to([P, P]),
                                             wm[:, l, k, j * CH:(j + 1) * CH], start=k == 0, stop=k == KD - 1)
                        last.then_inc(mod_ready[n % 2], 1)
                        n += 1
            for l in range(2):
                for j in range(12):
                    for k in range(KD):
                        last = pe.matmul(pc[:, l, j, :], wm[:, l, k, j * P:(j + 1) * P], sc[:, l, k, :],
                                         start=k == 0, stop=k == KD - 1)
            last.then_inc(col_ready, 1)

        @block.vector
        def _(dve):
            link = linker(dve, dve_step)
            dve.wait_ge(act_step, ONE + 1)
            link(dve.tensor_scalar_add(ce[:, :, :, :], ce[:, :, :, :], 1.0))
            link(dve.reciprocal(ce[:, :, :, :], ce[:, :, :, :]))
            dve.tensor_tensor(sc[:, :, :, :], cT[:, :, :, :], ce[:, :, :, :], ALU.mult).then_inc(silu_ready, 1)
            dve.wait_ge(loaded, ONE + 16 * len(weights))
            link(dve.reduce_max(rbm[:, :], rb[:, :], AX))
            link(dve.tensor_scalar(rbd[:, :], rb[:, :], rbm[:, 0:1], None, ALU.subtract))
            dve.sem_inc(bias_exp_in, 1)
            dve.wait_ge(bias_exp, ONE + 1)
            dve.tensor_copy(ext[:, 0:P - 1], ext[:, P - 1:P].broadcast_to([H, P - 1]))
            link(dve.tensor_copy(ext[:, P + 2 * REL:w.EXT], ext[:, P + 2 * REL - 1:P + 2 * REL].broadcast_to([H, P - 1])))
            dve.sem_inc(bias_rows_ready, 1)
            def stats(c):
                dve.wait_ge(x_loaded[c], ONE + 16)
                for t in range(c * CT, (c + 1) * CT):
                    dve.bn_stats(st[:, t, :], w.x[:, t, :]).then_inc(stat_step, 1)
                for t in range(c * CT, (c + 1) * CT):
                    dve.wait_ge(stat_step, ONE + t + 1)
                    dve.bn_aggr(w.mean_var0[:, t, :], st[:, t, :]).then_inc(var_ready, 1)

            n = 0
            for l in range(2):
                for b in range(B):
                    for j in range(3):
                        if n < NC:
                            stats(n)
                        dve.wait_ge(mod_ready[n % 2], ONE + n // 2 + 1)
                        dve.tensor_copy(w.modrow[l][:, b, j * CH:(j + 1) * CH], ps[n % 2][:, :]).then_inc(mod_used[n % 2], 1)
                        n += 1
            dve.wait_ge(mod_used[0], ONE + 6)
            dve.wait_ge(mod_used[1], ONE + 6)
            dve.wait_ge(col_ready, ONE + 1)
            link(dve.tensor_copy(w.modcol[:, :, :, :], pc[:, :, :, :]))
            for l in range(2):
                for part in (CA, CB):
                    link(dve.tensor_scalar_add(w.modcol[:, l, 2 * part:2 * part + 2, :], w.modcol[:, l, 2 * part:2 * part + 2, :], 1.0))
                    r = w.modrow[l][:, :, part * D:(part + 1) * D]
                    link(dve.tensor_scalar_add(r, r, 1.0))
                for part in (GA, GB):
                    g = w.modrow[l][:, :, part * D:(part + 1) * D]
                    t = row[:, :].rearrange("p (b n) -> p b n", b=B)
                    link(dve.scalar_tensor_tensor(t, g, -1.0, g, op0=ALU.mult, op1=ALU.max))
                    link(dve.tensor_scalar(g, g, 0.0, 2.0, ALU.is_ge, ALU.mult))
                    link(dve.tensor_scalar_add(g, g, -1.0))
                    link(dve.tensor_scalar_max(t, t, 0.25))
                    link(dve.tensor_tensor(g, g, t, ALU.mult))
            dve.wait_ge(std_ready, ONE + 1)
            dve.reciprocal(w.rstd0[:, :], w.rstd0[:, :])
            link(dve.tensor_scalar_mul(w.bqk[:, 0:KD], w.bqk[:, 0:KD], w.SCALE))
            for b in range(B):
                link(dve.tensor_tensor(w.gbo0[:, b, :], w.modrow[0][:, b, GA * D:(GA + 1) * D], w.bo0[:, :], ALU.mult))

        @block.gpsimd
        def _(pool):
            link = linker(pool, pool_step)
            link(pool.memset(w.ident[:, :], 0.0))
            link(pool.affine_select(out=w.ident[:, :], in_=w.ident[:, :], compare_op=ALU.not_equal, fill=1.0,
                                    base=0, pattern=[[-1, P]], channel_multiplier=1))
            link(pool.memset(w.zeros[:, :], 0.0))
            link(pool.memset(w.eps[:, :], EPS))


def stage_qkv(nc, w):
    with ExitStack() as ctx:
        sem = lambda name: semaphore(nc, ctx, name)
        norm_ready = sem("b_norm_ready")
        norm_used = sem("b_norm_used")
        turned = sem("b_turned")
        hT_ready = sem("b_hT_ready")
        hT_used = sem("b_hT_used")
        qk_ready = sem("b_qk_ready")
        v_ready = sem("b_v_ready")
        v_used = sem("b_v_used")
        whole_ready = sem("b_whole_ready")
        hi_ready = sem("b_hi_ready")
        rest_ready = sem("b_rest_ready")
        mid_ready = sem("b_mid_ready")
        low_ready = sem("b_low_ready")
        vout_ready = sem("b_vout_ready")
        stored = [sem(f"b_stored{q}") for q in range(2)]
        stored_v = sem("b_stored_v")

        std, mv = w.rstd0, w.mean_var0
        xn = sbuf(nc, ctx, "b_xn", [P, CT, D])
        hT = sbuf(nc, ctx, "b_hT", [P, KD, CH])
        NB = 4
        whole = [sbuf(nc, ctx, f"b_whole{q}", [P, NB, CH]) for q in range(2)]
        parts = [sbuf(nc, ctx, f"b_parts{q}", [P, 3, NB, CH], BF16) for q in range(2)]
        vout = sbuf(nc, ctx, "b_vout", [P, CT, D])
        pT = psum(nc, ctx, "b_pT", [P, KD, CH])
        pqk = psum(nc, ctx, "b_pqk", [P, NB, CH])
        pv = psum(nc, ctx, "b_pv", [P, CT, D])
        block = start(nc, ctx)

        @block.sync
        def _(sp):
            with sp.Fori(0, B) as b:
                with sp.Fori(0, NC // B // 2) as gb:
                    for q in range(2):
                        c = (b * (NC // B // 2) + gb) * 2 + q
                        sp.wait_ge(vout_ready, ONE + c + 1)
                        for t in range(CT):
                            sp.dma_start(
                                w.v_dram[bass.ds(b * H, H), bass.ds(gb * (2 * CH) + q * CH + t * P, P), :].rearrange("h p d -> p h d"),
                                vout[:, t, :].rearrange("p (h d) -> p h d", d=DH)).then_inc(stored_v, 16)
                        sp.wait_ge(low_ready, ONE + NB * c + NB)
                        for part in range(3):
                            for i in range(2):
                                sp.dma_start(
                                    w.qk_parts[i][part, bass.ds(b * D, D), bass.ds(gb * (2 * CH) + q * CH, CH)].rearrange("(k p) t -> p k t", p=P),
                                    parts[q][:, part, i * KD:(i + 1) * KD, :]).then_inc(stored[q], 16)
            for q in range(2):
                sp.wait_ge(stored[q], ONE + 16 * 6 * (NC // 2))
            sp.wait_ge(stored_v, ONE + 16 * CT * NC)

        @block.vector
        def _(dve):
            def norm(c):
                dve.wait_ge(norm_used, ONE + c + 1)
                for t in range(CT):
                    i = c * CT + t
                    last = dve.tensor_scalar(xn[:, t:t + 1, :], w.x[:, bass.ds(i, 1), :], mv[:, bass.ds(i, 1), 0:1].rearrange("p a b -> p (a b)"),
                                             std[:, bass.ds(i, 1)], ALU.subtract, ALU.mult)
                last.then_inc(norm_ready, 1)

            def pair(g, last_pair):
                for q in range(2):
                    c = g * 2 + q
                    if not last_pair or q == 0:
                        norm(c + 1)
                    for blk in range(NB):
                        dve.wait_ge(hi_ready, ONE + NB * c + blk + 1)
                        dve.wait_ge(whole_ready, ONE + NB * c + blk + 1)
                        dve.tensor_tensor(whole[q][:, blk, :], whole[q][:, blk, :], parts[q][:, 0, blk, :], ALU.subtract).then_inc(rest_ready, 1)
                    for blk in range(NB):
                        dve.wait_ge(mid_ready, ONE + NB * c + blk + 1)
                        dve.tensor_tensor(parts[q][:, 2, blk, :], whole[q][:, blk, :], parts[q][:, 1, blk, :], ALU.subtract).then_inc(low_ready, 1)
                    dve.wait_ge(v_ready, ONE + c + 1)
                    dve.wait_ge(stored_v, ONE + 16 * CT * c)
                    dve.tensor_tensor(vout[:, :, :], pv[:, :, :], w.bv0[:, :].rearrange("p (o n) -> p o n", o=1).broadcast_to([P, CT, D]),
                                      ALU.add).then_inc(vout_ready, 1)

            norm(0)
            with dve.Fori(0, NC // 2 - 1) as g:
                pair(g, False)
            pair(NC // 2 - 1, True)

        @block.tensor
        def _(pe):
            pe.sem_inc(norm_used, 1)
            with pe.Fori(0, NC) as c:
                pe.wait_ge(norm_ready, ONE + c + 1)
                for t in range(CT):
                    for k in range(KD):
                        last = pe.transpose(pT[:, k, t * P:(t + 1) * P], xn[:, t, k * P:(k + 1) * P], w.ident[:, :])
                last.then_inc(norm_used, 1)
                pe.wait_ge(hT_ready, ONE + c * KD + KD)
                pe.wait_ge(hi_ready, ONE + NB * c)
                pe.wait_ge(whole_ready, ONE + NB * c)
                for blk in range(NB):
                    for k in range(KD):
                        last = pe.matmul(pqk[:, blk, :], w.Wqkv0[:, k, blk * P:(blk + 1) * P], hT[:, k, :],
                                         start=k == 0, stop=k == KD - 1)
                    last.then_inc(qk_ready, 1)
                pe.wait_ge(vout_ready, ONE + c)
                for t in range(CT):
                    for k in range(KD):
                        last = pe.matmul(pv[:, t, :], hT[:, k, t * P:(t + 1) * P], w.Wqkv0[:, k, 2 * D:3 * D],
                                         start=k == 0, stop=k == KD - 1)
                last.then_inc(v_ready, 1)

        @block.scalar
        def _(act):
            with act.Fori(0, B) as b:
              with act.Fori(0, NC // B // 2) as gb:
                for q in range(2):
                    g = b * (NC // B // 2) + gb
                    c = g * 2 + q
                    wait_alone(w, act, norm_used, ONE + c + 2)
                    wait_alone(w, act, v_ready, ONE + c)
                    for k in range(KD):
                        act.activation(hT[:, k, :], pT[:, k, :], ACT.Identity,
                                       scale=w.modcol[:, 0, 2 * CA + k, bass.ds(b, 1)], bias=w.modcol[:, 0, 2 * SA + k, bass.ds(b, 1)]).then_inc(hT_ready, 1)
                    act.wait_ge(low_ready, ONE + NB * 2 * g)
                    act.wait_ge(stored[q], ONE + 16 * 6 * g)
                    for blk in range(NB):
                        s = w.SCALE if blk < KD else 1.0
                        act.wait_ge(qk_ready, ONE + NB * c + blk + 1)
                        act.activation(parts[q][:, 0, blk, :], pqk[:, blk, :], ACT.Identity, scale=s, bias=w.bqk[:, blk:blk + 1]).then_inc(hi_ready, 1)
                        act.activation(whole[q][:, blk, :], pqk[:, blk, :], ACT.Identity, scale=s, bias=w.bqk[:, blk:blk + 1]).then_inc(whole_ready, 1)
                    for blk in range(NB):
                        act.wait_ge(rest_ready, ONE + NB * c + blk + 1)
                        act.activation(parts[q][:, 1, blk, :], whole[q][:, blk, :], ACT.Copy).then_inc(mid_ready, 1)

        @block.gpsimd
        def _(pool):
            for n in range(NH):
                pool.dma_start(w.skew_dram[n, :].rearrange("(p r) -> p r", r=w.EXT + 1)[:, 0:w.EXT],
                               w.ext_dram[n:n + 1, :].broadcast_to([P, w.EXT])).then_inc(w.band_stored, 16)
            pool.wait_ge(w.band_stored, 16 * NH)


def stage_attention(nc, w):
    R6 = 6 * DH
    R8 = R6 + 2
    JT = S // P
    HALF = S // 2
    BANDT = w.BAND // P
    NBUF = 4
    VW = 32
    GROUPS = JT * (S // CH)
    PER_STEP = GROUPS // JT
    SHIFT = 4
    AHEAD = 2

    def band(t):
        return max(0, (t - 2) * P), min(S, (t + BANDT - 2) * P)

    def segments(t, half):
        lo, hi = band(t)
        a, z = half * HALF, (half + 1) * HALF
        cuts = [(a, min(z, lo), "left"), (max(a, lo), min(z, hi), "band"), (max(a, hi), z, "right")]
        return [c for c in cuts if c[0] < c[1]]

    band_parts = [[sum(k == "band" for _, _, k in segments(t, half)) for half in range(2)] for t in range(JT)]
    POOL_STEPS = sum(map(sum, band_parts))
    pool_after = [sum(map(sum, band_parts[:t + 1])) for t in range(JT)]

    with ExitStack() as ctx:
        sem = lambda name: semaphore(nc, ctx, name)
        max_loaded = [sem(f"c_max_loaded{q}") for q in range(2)]
        score_loaded = [sem(f"c_score_loaded{q}") for q in range(2)]
        consts_ready = sem("c_consts_ready")
        value_pad_ready = sem("c_value_pad_ready")
        group_ready = sem("c_group_ready")
        group_done = sem("c_group_done")
        max_ready = sem("c_max_ready")
        maxT_ready = sem("c_maxT_ready")
        max_parts_hi = sem("c_max_parts_hi")
        max_parts_ready = sem("c_max_parts_ready")
        max_rows_loaded = sem("c_max_rows_loaded")
        scores_ready = sem("c_scores_ready")
        probs_ready = sem("c_probs_ready")
        band_ready = sem("c_band_ready")
        summed = sem("c_summed")
        out_taken = sem("c_out_taken")
        out_stored = sem("c_out_stored")
        max_step = sem("c_max_step")
        zeroed = sem("c_zeroed")

        QM = [sbuf(nc, ctx, f"QM{q}", [R6, S], BF16) for q in range(2)]
        KM = [sbuf(nc, ctx, f"KM{q}", [R6, S], BF16) for q in range(2)]
        QS = [sbuf(nc, ctx, f"QS{q}", [R8, S], BF16) for q in range(2)]
        KS = [sbuf(nc, ctx, f"KS{q}", [R8, S], BF16) for q in range(2)]
        V = [sbuf(nc, ctx, f"V{q}", [P, JT, VW]) for q in range(2)]
        EB = [sbuf(nc, ctx, f"EB{q}", [P, BANDT * P]) for q in range(2)]
        probs = [sbuf(nc, ctx, f"probs{i}", [P, S]) for i in range(NBUF)]
        gmax = sbuf(nc, ctx, "gmax", [P, JT, S // CH])
        qmax = sbuf(nc, ctx, "qmax", [P, JT])
        mhi = sbuf(nc, ctx, "mhi", [JT, P], BF16)
        mlo = sbuf(nc, ctx, "mlo", [JT, P], BF16)
        osb = sbuf(nc, ctx, "osb", [P, CH])
        GB = 3
        pg = [psum(nc, ctx, f"pg{i}", [P, CH]) for i in range(GB)]
        psc = [psum(nc, ctx, f"psc{i}", [P, HALF]) for i in range(2)]
        po = psum(nc, ctx, "po", [P, CH])
        pm = pg[GROUPS % GB]
        block = start(nc, ctx)

        @block.sync
        def _(sp):
            def load_parts(dst, order, src, n, loaded):
                at = 0
                for part, times in order:
                    for _ in range(times):
                        sp.dma_start(dst[at:at + DH, :], src[part, bass.ds(n * DH, DH), :]).then_inc(loaded, 16)
                        at += DH

            Q_ORDER = [(0, 3), (1, 2), (2, 1)]
            K_ORDER = [(0, 1), (1, 1), (2, 1), (0, 1), (1, 1), (0, 1)]

            def load_max(n, q):
                load_parts(QM[q], Q_ORDER, w.qk_parts[0], n, max_loaded[q])
                load_parts(KM[q], K_ORDER, w.qk_parts[1], n, max_loaded[q])

            def load_scores(n, q):
                load_parts(QS[q], Q_ORDER, w.qk_parts[0], n, score_loaded[q])
                load_parts(KS[q], K_ORDER, w.qk_parts[1], n, score_loaded[q])
                sp.dma_start(V[q][:, :, 0:DH], w.v_dram[bass.ds(n, 1), :, :].rearrange("o (t p) d -> p (o t) d", p=P)).then_inc(score_loaded[q], 16)
                sp.dma_start(EB[q][:, :], 
                             w.skew_dram[bass.ds(n, 1), P - 1:P - 1 + P * w.EXT].rearrange("o (p r) -> p (o r)", r=w.EXT)[:, 0:BANDT * P]).then_inc(score_loaded[q], 16)

            def move_max(n, q):
                sp.wait_ge(max_parts_ready, ONE + n + 1)
                sp.dma_start(QS[q][R6:R6 + 1, :], mhi[:, :]).then_inc(max_rows_loaded, 16)
                sp.dma_start(QS[q][R6 + 1:R8, :], mlo[:, :]).then_inc(max_rows_loaded, 16)

            def store_out(n):
                sp.wait_ge(out_taken, ONE + n + 1)
                for c in range(S // CH):
                    sp.dma_start(w.attT_dram[bass.ds(n, 1), :, c * CH:(c + 1) * CH].rearrange("o r t -> (o r) t"),
                                 osb[VW * c:VW * c + DH + 1, :]).then_inc(out_stored, 16)

            load_max(0, 0)
            rows = w.xe_dram.rearrange("(n p k) d -> n p (k d)", p=P, k=w.zeros.shape[1] // D)
            for i in range(rows.shape[0]):
                sp.dma_start(rows[i], w.zeros[:, :]).then_inc(zeroed, 16)
            sp.wait_ge(value_pad_ready, ONE + 1)
            load_scores(0, 0)
            load_max(1, 1)
            load_scores(1, 1)
            move_max(0, 0)

            def pair(g, last):
                for q in range(2):
                    n = g * 2 + q
                    if not last:
                        sp.wait_ge(group_ready, ONE + GROUPS * n + GROUPS)
                        load_max(n + 2, q)
                    if not last or q == 0:
                        move_max(n + 1, 1 - q)
                    if not last:
                        sp.wait_ge(summed, ONE + JT * n + JT + NBUF - 1)
                        sp.wait_ge(band_ready, ONE + POOL_STEPS * n + POOL_STEPS)
                        load_scores(n + 2, q)
                    store_out(n)

            with sp.Fori(0, NH // 2 - 1) as g:
                pair(g, False)
            pair(NH // 2 - 1, True)
            sp.wait_ge(out_stored, ONE + 16 * (S // CH) * NH)
            sp.wait_ge(zeroed, ONE + 16 * rows.shape[0])

        @block.tensor
        def _(pe):
            def group(n, q, k):
                tile, c = divmod(k, S // CH)
                if k == 0:
                    pe.wait_ge(group_done, ONE + GROUPS * n)
                elif k >= GB:
                    pe.wait_ge(group_done, ONE + GROUPS * n + k - GB + 1)
                if k == GROUPS % GB:
                    pe.wait_ge(max_parts_ready, ONE + n)
                pe.matmul(pg[k % GB][:, :], QM[q][:, tile * P:(tile + 1) * P], KM[q][:, c * CH:(c + 1) * CH],
                          start=True, stop=True).then_inc(group_ready, 1)

            def turn_max(n):
                pe.wait_ge(max_ready, ONE + n + 1)
                pe.transpose(pm[0:JT, 0:P], qmax[:, :], w.ident[:, :]).then_inc(maxT_ready, 1)

            def scores(n, q, t, half):
                pe.wait_ge(probs_ready, ONE + 2 * JT * n + 2 * t + half)
                for c in range(HALF // CH):
                    at = half * HALF + c * CH
                    last = pe.matmul(psc[half][:, c * CH:(c + 1) * CH], KS[q][:, t * P:(t + 1) * P], QS[q][:, at:at + CH],
                                     start=True, stop=True)
                last.then_inc(scores_ready, 1)

            def sums(n, q, t):
                pe.wait_ge(probs_ready, ONE + 2 * JT * n + 2 * t + 3)
                pe.wait_ge(band_ready, ONE + POOL_STEPS * n + pool_after[t])
                if t == 0:
                    pe.wait_ge(out_taken, ONE + n)
                for c in range(S // CH):
                    last = pe.matmul(po[VW * c:VW * (c + 1), :], V[q][:, t, :], probs[t % NBUF][:, c * CH:(c + 1) * CH],
                                     start=t == 0, stop=t == JT - 1)
                last.then_inc(summed, 1)

            pe.sem_inc(summed, NBUF - 1)
            pe.wait_ge(consts_ready, ONE + 1)
            pe.wait_ge(max_loaded[0], ONE + 192)
            for k in range(GROUPS):
                group(0, 0, k)
            turn_max(0)
            pe.wait_ge(max_loaded[1], ONE + 192)
            pe.wait_ge(score_loaded[0], ONE + 224)
            pe.wait_ge(max_rows_loaded, ONE + 32)
            for t in range(AHEAD):
                scores(0, 0, t, 0)
                scores(0, 0, t, 1)
                for k in range(SHIFT * PER_STEP // AHEAD):
                    group(1, 1, k + t * (SHIFT * PER_STEP // AHEAD))

            def pair(g, last):
                for q in range(2):
                    n = g * 2 + q
                    more = not last or q == 0
                    for t in range(JT):
                        if t == JT - SHIFT and not last:
                            pe.wait_ge(max_loaded[q], ONE + 192 * g + 384)
                        if t == JT - AHEAD and more:
                            pe.wait_ge(max_rows_loaded, ONE + 32 * n + 64)
                            pe.wait_ge(score_loaded[1 - q], ONE + 224 * g + 224 * (1 + q))

                        def next_group(i):
                            if t < JT - SHIFT and more:
                                group(n + 1, 1 - q, (t + SHIFT) * PER_STEP + i)
                            elif t >= JT - SHIFT and not last:
                                group(n + 2, q, (t + SHIFT - JT) * PER_STEP + i)

                        for half in range(2):
                            if t < JT - AHEAD:
                                scores(n, q, t + AHEAD, half)
                            elif more:
                                scores(n + 1, 1 - q, t + AHEAD - JT, half)
                            next_group(half)
                            if half == 0 and t == JT - SHIFT and more:
                                turn_max(n + 1)
                        next_group(2)
                        sums(n, q, t)
                        next_group(3)

            with pe.Fori(0, NH // 2 - 1) as g:
                pair(g, False)
            pair(NH // 2 - 1, True)

        @block.vector
        def _(dve):
            for q in range(2):
                dve.memset(KS[q][R6:R8, :], 1.0)
                dve.memset(V[q][:, :, :], 0.0).then_inc(max_step, 1)
            dve.wait_ge(max_step, ONE + 2)
            for q in range(2):
                last = dve.memset(V[q][:, :, DH:DH + 1], 1.0)
            last.then_inc(value_pad_ready, 1)
            dve.wait_ge(value_pad_ready, ONE + 1)
            dve.sem_inc(consts_ready, 1)

            def head_max(n):
                for k in range(GROUPS):
                    tile, c = divmod(k, S // CH)
                    dve.wait_ge(group_ready, ONE + GROUPS * n + k + 1)
                    dve.reduce_max(gmax[:, tile, c:c + 1], pg[k % GB][:, :], AX).then_inc(group_done, 1)
                dve.wait_ge(group_done, ONE + GROUPS * n + GROUPS)
                dve.reduce_max(qmax[:, :], gmax[:, :, :], AX).then_inc(max_ready, 1)
                dve.wait_ge(maxT_ready, ONE + n + 1)
                dve.wait_ge(max_rows_loaded, ONE + 32 * n)
                dve.tensor_scalar_mul(mhi[:, :], pm[0:JT, 0:P], -1.0).then_inc(max_parts_hi, 1)
                dve.wait_ge(max_parts_hi, ONE + n + 1)
                dve.scalar_tensor_tensor(mlo[:, :], pm[0:JT, 0:P], -1.0, mhi[:, :], op0=ALU.mult, op1=ALU.subtract).then_inc(max_parts_ready, 1)

            head_max(0)
            with dve.Fori(1, NH) as n:
                head_max(n)

        @block.scalar
        def _(act):
            def exps(n, t, half):
                if half == 0:
                    act.wait_ge(summed, ONE + JT * n + t)
                wait_alone(w, act, scores_ready, ONE + 2 * JT * n + 2 * t + half + 1)
                for a, z, kind in segments(t, half):
                    bias = {"left": w.far[:, bass.ds(n, 1), 0:1], "right": w.far[:, bass.ds(n, 1), 1:2], "band": None}[kind]
                    more = {} if bias is None else {"bias": bias.rearrange("p a b -> p (a b)")}
                    last = act.activation(probs[t % NBUF][:, a:z], psc[half][:, a - half * HALF:z - half * HALF], ACT.Exp, **more)
                last.then_inc(probs_ready, 1)

            act.sem_inc(probs_ready, 1)
            for t in range(AHEAD):
                exps(0, t, 0)
                exps(0, t, 1)

            def head(n, last):
                for t in range(AHEAD, JT):
                    exps(n, t, 0)
                    exps(n, t, 1)
                if not last:
                    for t in range(AHEAD):
                        exps(n + 1, t, 0)
                        exps(n + 1, t, 1)
                act.wait_ge(summed, ONE + JT * n + JT + NBUF - 1)
                act.wait_ge(out_stored, ONE + 16 * (S // CH) * n)
                act.activation(osb[:, :], po[:, :], ACT.Copy).then_inc(out_taken, 1)

            with act.Fori(0, NH - 1) as n:
                head(n, False)
            head(NH - 1, True)

        @block.gpsimd
        def _(pool):
            with pool.Fori(0, NH // 2) as g:
                for q in range(2):
                    n = g * 2 + q
                    pool.wait_ge(score_loaded[q], ONE + 224 * g + 224)
                    for t in range(JT):
                        lo = (t - 2) * P
                        for half in range(2):
                            for a, z, kind in segments(t, half):
                                if kind == "band":
                                    pool.wait_ge(probs_ready, ONE + 2 * JT * n + 2 * t + half + 2)
                                    part = probs[t % NBUF][:, a:z]
                                    pool.tensor_tensor(part, part, EB[q][:, a - lo:z - lo], ALU.mult).then_inc(band_ready, 1)


MAP = 1024
BLOCK, SEG, DIL = 64, 64, 4
NK = SEG // DIL
U = MAP // P + 1
UK = 3
TPT = 3

E0, K0, I0, CAP = 64, 4, 128, 256


def stage_project(nc, w):
    with ExitStack() as ctx:
        sem = lambda name: semaphore(nc, ctx, name)
        loaded = [sem(f"d_loaded{q}") for q in range(2)]
        att_ready = sem("d_att_ready")
        sums_loaded = sem("d_sums_loaded")
        inverse_ready = sem("d_inverse_ready")
        inverse_stored = sem("d_inverse_stored")
        sums = sbuf(nc, ctx, "d_sums", [P, CH])
        projected = sem("d_projected")
        gated = sem("d_gated")
        biased = sem("d_biased")
        raw = [sbuf(nc, ctx, f"d_raw{q}", [P, KD, CH]) for q in range(2)]
        inv = [sbuf(nc, ctx, f"d_inv{q}", [P, KD, CH]) for q in range(2)]
        att = [sbuf(nc, ctx, f"d_att{q}", [P, KD, CH]) for q in range(2)]
        gate = [sbuf(nc, ctx, f"d_gate{q}", [P, CT, D]) for q in range(2)]
        pp = [psum(nc, ctx, f"d_pp{q}", [P, CT, D]) for q in range(2)]
        block = start(nc, ctx)
        HB = P // DH
        GBATCH = NC // B // 2

        @block.sync
        def _(sp):
            sp.dma_start(sums[:, :], w.attT_dram[:, DH, :].rearrange("n (c t) -> n c t", t=CH)).then_inc(sums_loaded, 16)
            sp.wait_ge(inverse_ready, ONE + 1)
            sp.dma_start(w.inverse_dram.rearrange("n (c t) -> (n c) t", t=CH), sums[:, :]).then_inc(inverse_stored, 16)
            sp.wait_ge(inverse_stored, ONE + 16)
            with sp.Fori(0, B) as b:
                with sp.Fori(0, GBATCH) as gb:
                    g = b * GBATCH + gb
                    sp.wait_ge(att_ready, ONE + g * 2)
                    for q in range(2):
                        cols = bass.ds(gb * (2 * CH) + q * CH, CH)
                        for k in range(KD):
                            heads = bass.ds(b * H + k * HB, HB)
                            sp.dma_start(raw[q][:, k, :], w.attT_dram[heads, 0:DH, cols]).then_inc(loaded[q], 16)
                            sp.dma_start(inv[q][:, k, :], w.inverse_dram[heads, cols].rearrange("h (o t) -> h o t", o=1).broadcast_to([HB, DH, CH])).then_inc(loaded[q], 16)

        @block.gpsimd
        def _(pool):
            with pool.Fori(0, B) as b:
                with pool.Fori(0, NC // B) as cb:
                    xs = w.x[:, bass.ds(b * TB + cb * CT, CT), :]
                    pool.tensor_tensor(xs, xs, w.gbo0[:, bass.ds(b, 1), :].broadcast_to([P, CT, D]), ALU.add).then_inc(biased, 1)

        @block.vector
        def _(dve):
            dve.wait_ge(sums_loaded, ONE + 16)
            dve.reciprocal(sums[:, :], sums[:, :]).then_inc(inverse_ready, 1)
            with dve.Fori(0, B) as b:
                with dve.Fori(0, GBATCH) as gb:
                    g = b * GBATCH + gb
                    for q in range(2):
                        dve.wait_ge(loaded[q], ONE + 16 * 2 * KD * g + 16 * 2 * KD)
                        dve.wait_ge(projected, ONE + g * 2)
                        dve.tensor_tensor(att[q][:, :, :], raw[q][:, :, :], inv[q][:, :, :], ALU.mult).then_inc(att_ready, 1)
                    for q in range(2):
                        c = g * 2 + q
                        dve.wait_ge(projected, ONE + c + 1)
                        ga = w.modrow[0][:, bass.ds(b, 1), GA * D:(GA + 1) * D].broadcast_to([P, CT, D])
                        dve.tensor_tensor(gate[q][:, :, :], pp[q][:, :, :], ga, ALU.mult).then_inc(gated, 1)
                    for q in range(2):
                        c = g * 2 + q
                        xs = w.x[:, bass.ds(c * CT, CT), :]
                        dve.wait_ge(gated, ONE + c + 1)
                        dve.wait_ge(biased, ONE + c + 1)
                        dve.tensor_tensor(xs, xs, gate[q][:, :, :], ALU.add)

        @block.tensor
        def _(pe):
            with pe.Fori(0, NC // 2) as g:
                for q in range(2):
                    pe.wait_ge(att_ready, ONE + g * 2 + q + 1)
                    pe.wait_ge(gated, ONE + g * 2)
                    for t in range(CT):
                        for k in range(KD):
                            last = pe.matmul(pp[q][:, t, :], att[q][:, k, t * P:(t + 1) * P], w.Wout0[:, k, :], start=k == 0, stop=k == KD - 1)
                    last.then_inc(projected, 1)


def stage_norm(nc, w, x, tiles, mean_var, rstd, name):
    with ExitStack() as ctx:
        sem = lambda n: semaphore(nc, ctx, f"{name}_{n}")
        stats_ready, var_ready, std_ready = sem("stats_ready"), sem("var_ready"), sem("std_ready")
        st = sbuf(nc, ctx, f"{name}_st", [P, tiles, 6])
        block = start(nc, ctx)

        @block.vector
        def _(dve):
            for t in range(tiles):
                dve.bn_stats(st[:, t, :], x[:, t, :]).then_inc(stats_ready, 1)
            for t in range(tiles):
                dve.wait_ge(stats_ready, ONE + t + 1)
                dve.bn_aggr(mean_var[:, t, :], st[:, t, :]).then_inc(var_ready, 1)
            dve.wait_ge(std_ready, ONE + 1)
            dve.reciprocal(rstd[:, 0:tiles], rstd[:, 0:tiles])

        @block.scalar
        def _(act):
            act.wait_ge(var_ready, ONE + tiles)
            act.activation(rstd[:, 0:tiles], mean_var[:, 0:tiles, 1], ACT.Sqrt, bias=w.eps[:, 0:1]).then_inc(std_ready, 1)


def stage_router(nc, w, x, mean_var, rstd, h, hT_all, layer, Wg, logits, name):
    n_experts = logits.shape[2]
    with ExitStack() as ctx:
        sem = lambda n: semaphore(nc, ctx, f"{name}_{n}")
        norm_ready, norm_turned, hT_ready, logits_ready = sem("norm_ready"), sem("norm_turned"), sem("hT_ready"), sem("logits_ready")
        logits_out, scaled, shifted, hT_kept = sem("logits_out"), sem("scaled"), sem("shifted"), sem("hT_kept")
        xn = [sbuf(nc, ctx, f"{name}_xn{q}", [P, CT, D]) for q in range(2)]
        hT = [sbuf(nc, ctx, f"{name}_hT{q}", [P, KD, CH]) for q in range(2)]
        tmp = [sbuf(nc, ctx, f"{name}_tmp{q}", [P, CT, D]) for q in range(2)]
        pT = [psum(nc, ctx, f"{name}_pT{q}", [P, KD, CH]) for q in range(2)]
        pl = [psum(nc, ctx, f"{name}_pl{q}", [P, CT, n_experts]) for q in range(2)]
        block = start(nc, ctx)
        natural = h is not None
        GBATCH = NC // B // 2

        row = lambda part, b: w.modrow[layer][:, bass.ds(b, 1), part * D:(part + 1) * D].broadcast_to([P, CT, D])

        @block.vector
        def _(dve):
            def turn(b, g):
                for q in range(2):
                    c = g * 2 + q
                    dve.wait_ge(norm_turned, ONE + g * 2)
                    if natural:
                        dve.wait_ge(scaled, ONE + g * 2)
                    for t in range(CT):
                        i = c * CT + t
                        last = dve.tensor_scalar(xn[q][:, t:t + 1, :], x[:, bass.ds(i, 1), :], mean_var[:, bass.ds(i, 1), 0:1].rearrange("p a b -> p (a b)"),
                                                 rstd[:, bass.ds(i, 1)], ALU.subtract, ALU.mult)
                    last.then_inc(norm_ready, 1)
                if natural:
                    for q in range(2):
                        dve.wait_ge(norm_ready, ONE + g * 2 + q + 1)
                        dve.wait_ge(shifted, ONE + g * 2)
                        dve.tensor_tensor(tmp[q][:, :, :], xn[q][:, :, :], row(CB, b), ALU.mult).then_inc(scaled, 1)
                for q in range(2):
                    c = g * 2 + q
                    dve.wait_ge(logits_ready, ONE + c + 1)
                    dve.tensor_copy(logits[:, bass.ds(c * CT, CT), :], pl[q][:, :, :]).then_inc(logits_out, 1)

            with dve.Fori(0, B) as b:
                with dve.Fori(0, GBATCH) as gb:
                    turn(b, b * GBATCH + gb)

        @block.tensor
        def _(pe):
            with pe.Fori(0, NC // 2) as g:
                for q in range(2):
                    pe.wait_ge(norm_ready, ONE + g * 2 + q + 1)
                    pe.wait_ge(hT_ready, ONE + KD * 2 * g)
                    if hT_all is not None:
                        pe.wait_ge(hT_kept, ONE + 2 * g)
                    for t in range(CT):
                        for k in range(KD):
                            last = pe.transpose(pT[q][:, k, t * P:(t + 1) * P], xn[q][:, t, k * P:(k + 1) * P], w.ident[:, :])
                    last.then_inc(norm_turned, 1)
                for q in range(2):
                    pe.wait_ge(hT_ready, ONE + KD * 2 * g + KD * q + KD)
                    pe.wait_ge(logits_out, ONE + g * 2)
                    for t in range(CT):
                        for k in range(KD):
                            last = pe.matmul(pl[q][:, t, :], hT[q][:, k, t * P:(t + 1) * P], Wg[:, k, :], start=k == 0, stop=k == KD - 1)
                    last.then_inc(logits_ready, 1)

        @block.scalar
        def _(act):
            with act.Fori(0, B) as b:
                with act.Fori(0, GBATCH) as gb:
                    g = b * GBATCH + gb
                    for q in range(2):
                        wait_alone(w, act, norm_turned, ONE + g * 2 + q + 1)
                        wait_alone(w, act, logits_ready, ONE + g * 2)
                        for k in range(KD):
                            act.activation(hT[q][:, k, :], pT[q][:, k, :], ACT.Identity, scale=w.modcol[:, layer, 2 * CB + k, bass.ds(b, 1)],
                                           bias=w.modcol[:, layer, 2 * SB_ + k, bass.ds(b, 1)]).then_inc(hT_ready, 1)
                        if hT_all is not None:
                            for k in range(KD):
                                last = act.activation(hT_all[:, k, bass.ds((g * 2 + q) * CH, CH)], pT[q][:, k, :], ACT.Identity, scale=w.modcol[:, layer, 2 * CB + k, bass.ds(b, 1)],
                                                      bias=w.modcol[:, layer, 2 * SB_ + k, bass.ds(b, 1)])
                            last.then_inc(hT_kept, 1)

        @block.gpsimd
        def _(pool):
            with pool.Fori(0, B) as b:
                with pool.Fori(0, GBATCH) as gb:
                    for q in range(2):
                        c = (b * GBATCH + gb) * 2 + q
                        if natural:
                            wait_alone(w, pool, scaled, ONE + c + 1)
                            pool.tensor_tensor(h[:, bass.ds(c * CT, CT), :], tmp[q][:, :, :], row(SB_, b), ALU.add).then_inc(shifted, 1)


def softmax_rows(dve, link, logits, top, total, exp_request, exp_done):
    tiles, n = logits.shape[1], logits.shape[2]
    over = lambda v: v[:, :].rearrange("p (t o) -> p t o", o=1).broadcast_to([P, tiles, n])
    link(dve.reduce_max(top[:, :], logits[:, :, :], AX))
    dve.tensor_tensor(logits[:, :, :], logits[:, :, :], over(top), ALU.subtract).then_inc(exp_request, 1)
    dve.wait_ge(exp_done, ONE + 1)
    link(dve.reduce_sum(total[:, :], logits[:, :, :], AX))
    link(dve.reciprocal(total[:, :], total[:, :]))
    link(dve.tensor_tensor(logits[:, :, :], logits[:, :, :], over(total), ALU.mult))


def stage_route(nc, w):
    with ExitStack() as ctx:
        sem = lambda name: semaphore(nc, ctx, name)
        step = sem("r_step")
        exp_request, exp_done = sem("r_exp_request"), sem("r_exp_done")
        made = sem("r_made")
        mask_ready, counted, base_step = sem("r_mask_ready"), sem("r_counted"), sem("r_base_step")
        N = NT * K0
        top = sbuf(nc, ctx, "r_top", [P, NT])
        total = sbuf(nc, ctx, "r_total", [P, NT])
        m8 = sbuf(nc, ctx, "r_m8", [P, NT, 8])
        i8 = sbuf(nc, ctx, "r_i8", [P, NT, 8], U32)
        i4 = sbuf(nc, ctx, "r_i4", [P, N])
        col_i = sbuf(nc, ctx, "r_col_i", [P, E0], I32)
        col = sbuf(nc, ctx, "r_col", [P, E0])
        chosen = sbuf(nc, ctx, "r_chosen", [P, N, E0], BF16)
        mask = sbuf(nc, ctx, "r_mask", [P, NT, E0], BF16)
        before = sbuf(nc, ctx, "r_before", [P, P], BF16)
        ones = sbuf(nc, ctx, "r_ones", [P, P], BF16)
        base = sbuf(nc, ctx, "r_base", [P, NT, E0])
        tot = sbuf(nc, ctx, "r_tot", [P, NT, E0])
        prod = sbuf(nc, ctx, "r_prod", [P, N, E0])
        place = sbuf(nc, ctx, "r_place", [P, N])
        over = sbuf(nc, ctx, "r_over", [P, N])
        slot = sbuf(nc, ctx, "r_slot", [P, N])
        G = CH // E0
        pw = psum(nc, ctx, "r_pw", [P, NT, E0])
        pt = psum(nc, ctx, "r_pt", [P, NT, E0])
        block = start(nc, ctx)
        BIG = float(1 << 22)

        @block.gpsimd
        def _(pool):
            pool.iota(col_i[:, :], [[1, E0]], base=0, channel_multiplier=0).then_inc(made, 1)
            pool.memset(ones[:, :], 1.0).then_inc(made, 1)
            pool.wait_ge(made, ONE + 2)
            pool.affine_select(out=before[:, :], in_=ones[:, :], compare_op=ALU.is_gt, fill=0.0, base=0,
                               pattern=[[1, P]], channel_multiplier=-1).then_inc(made, 1)

        @block.scalar
        def _(act):
            act.wait_ge(exp_request, ONE + 1)
            act.activation(w.logits0[:, :, :], w.logits0[:, :, :], ACT.Exp).then_inc(exp_done, 1)

        @block.tensor
        def _(pe):
            pe.wait_ge(made, ONE + 3)
            pe.wait_ge(mask_ready, ONE + 1)
            for g in range(NT // G):
                pe.matmul(pw[:, g * G:(g + 1) * G, :], before[:, :], mask[:, g * G:(g + 1) * G, :], start=True, stop=True)
                last = pe.matmul(pt[:, g * G:(g + 1) * G, :], ones[:, :], mask[:, g * G:(g + 1) * G, :], start=True, stop=True)
            last.then_inc(counted, 1)

        @block.vector
        def _(dve):
            link = linker(dve, step)
            probs = w.logits0
            softmax_rows(dve, link, probs, top, total, exp_request, exp_done)
            for t in range(NT):
                last = dve.max(m8[:, t, :], probs[:, t, :])
            link(last)
            for t in range(NT):
                last = dve.max_index(i8[:, t, :], m8[:, t, :], probs[:, t, :])
            dve.tensor_copy(w.gate4[:, :, :], m8[:, :, 0:K0])
            link(last)
            link(dve.tensor_copy(i4[:, :].rearrange("p (t k) -> p t k", k=K0), i8[:, :, 0:K0]))
            dve.wait_ge(made, ONE + 1)
            link(dve.tensor_copy(col[:, :], col_i[:, :]))
            link(dve.tensor_tensor(chosen[:, :, :], col[:, :].rearrange("p (o e) -> p o e", o=1).broadcast_to([P, N, E0]),
                                   i4[:, :].rearrange("p (n o) -> p n o", o=1).broadcast_to([P, N, E0]), ALU.is_equal))
            by_k = chosen[:, :, :].rearrange("p (t k) e -> p t k e", k=K0)
            link(dve.tensor_tensor(mask[:, :, :], by_k[:, :, 0, :], by_k[:, :, 1, :], ALU.add))
            link(dve.tensor_tensor(mask[:, :, :], mask[:, :, :], by_k[:, :, 2, :], ALU.add))
            dve.tensor_tensor(mask[:, :, :], mask[:, :, :], by_k[:, :, 3, :], ALU.add).then_inc(mask_ready, 1)
            dve.wait_ge(counted, ONE + 1)
            dve.tensor_copy(tot[:, :, :], pt[:, :, :]).then_inc(base_step, 1)
            dve.memset(base[:, 0:1, :], 0.0).then_inc(base_step, 1)
            dve.wait_ge(base_step, ONE + 2)
            with dve.Fori(0, NT - 1) as t:
                dve.wait_ge(base_step, ONE + t + 2)
                dve.tensor_tensor(base[:, bass.ds(t + 1, 1), :], base[:, bass.ds(t, 1), :], tot[:, bass.ds(t, 1), :], ALU.add).then_inc(base_step, 1)
            dve.wait_ge(base_step, ONE + NT + 1)
            link(dve.tensor_tensor(base[:, :, :], pw[:, :, :], base[:, :, :], ALU.add))
            for k in range(K0):
                last = dve.tensor_tensor(prod[:, :, :].rearrange("p (t k) e -> p t k e", k=K0)[:, :, k, :], by_k[:, :, k, :], base[:, :, :], ALU.mult)
            link(last)
            link(dve.reduce_sum(place[:, :], prod[:, :, :], AX))
            link(dve.tensor_scalar(over[:, :], place[:, :], float(CAP), BIG, ALU.is_ge, ALU.mult))
            link(dve.scalar_tensor_tensor(slot[:, :], i4[:, :], float(CAP), place[:, :], op0=ALU.mult, op1=ALU.add))
            link(dve.tensor_tensor(slot[:, :], slot[:, :], over[:, :], ALU.add))
            link(dve.tensor_copy(w.put_at[:, :, :].rearrange("p t k -> p (t k)"), slot[:, :]))
            link(dve.tensor_scalar_min(place[:, :], place[:, :], float(CAP - 1)))
            link(dve.scalar_tensor_tensor(slot[:, :], i4[:, :], float(CAP), place[:, :], op0=ALU.mult, op1=ALU.add))
            dve.memset(w.get_from[:, NT:NT + 4, :], 0)
            link(dve.tensor_copy(w.get_from[:, 0:NT, :].rearrange("p t k -> p (t k)"), slot[:, :]))


def stage_scatter(nc, w):
    with ExitStack() as ctx:
        sem = lambda name: semaphore(nc, ctx, name)
        staged = sem("s_staged")
        sent = [gpsimd_dma_semaphore(nc, ctx, f"s_sent{q}") for q in range(4)]
        rows = [sbuf(nc, ctx, f"s_rows{q}", [P, D]) for q in range(4)]
        at = [sbuf(nc, ctx, f"s_at{q}", [P, K0], I32) for q in range(4)]
        loaded, step, made, key_at_ready = sem("i_loaded"), sem("i_step"), sem("i_made"), sem("i_key_at_ready")
        first = sbuf(nc, ctx, "i_first", [P, UK], I32)
        offs = sbuf(nc, ctx, "i_offs", [P, 1], I32)
        key_at = sbuf(nc, ctx, "i_key_at", [P, UK], I32)
        keys = sbuf(nc, ctx, "i_keys", [P, UK], I32)
        index = w.index
        m = w.a['L1_attn_mapping']
        by_block = m.rearrange("(n r) -> n r", r=BLOCK)
        last_entry = m[MAP - 1:MAP].rearrange("(n r) -> n r", r=1)
        NBT = P // NK
        block = start(nc, ctx)

        @block.sync
        def _(sp):
            sp.dma_start(index[:, 0, 0:U - 1], m.rearrange("(u p) -> p u", p=P), allow_slow_non_contiguous=True).then_inc(loaded, 16)
            sp.dma_start(index[:, 0, U - 1:U], last_entry.broadcast_to([P, 1])).then_inc(loaded, 16)
            for j in range(UK - 1):
                for i in range(NBT):
                    n = j * NBT + i
                    sp.dma_start(first[i * NK:(i + 1) * NK, j:j + 1], by_block[n:n + 1, 0:1].broadcast_to([NK, 1])).then_inc(loaded, 16)
            sp.dma_start(first[:, UK - 1:UK], last_entry.broadcast_to([P, 1])).then_inc(loaded, 16)

        @block.vector
        def _(dve):
            def stage(t, q):
                dve.tensor_copy(at[q][:, :].rearrange("p (o k) -> p o k", o=1), w.put_at[:, bass.ds(t, 1), :])
                dve.tensor_copy(rows[q][:, :].rearrange("p (o n) -> p o n", o=1), w.h[:, bass.ds(t, 1), :]).then_inc(staged, 1)

            for q in range(4):
                stage(q, q)
            with dve.Fori(1, NT // 4) as g:
                for q in range(4):
                    dve.wait_ge(sent[q], 16 * K0 * g)
                    stage(g * 4 + q, q)
            link = linker(dve, step)
            dve.wait_ge(made, ONE + 1)
            link(dve.tensor_scalar(offs[:, :], offs[:, :], NK - 1, DIL.bit_length() - 1, ALU.bitwise_and, ALU.logical_shift_left))
            dve.wait_ge(loaded, ONE + 16 * (3 + (UK - 1) * NBT))
            link(dve.tensor_scalar(key_at[:, :], first[:, :], -SEG, None, ALU.bitwise_and))
            link(dve.tensor_tensor(key_at[:, :], key_at[:, :], offs[:, :].broadcast_to([P, UK]), ALU.add))
            link(dve.tensor_scalar_min(key_at[:, :], key_at[:, :], float(MAP - 1)))
            dve.sem_inc(key_at_ready, 1)
            dve.wait_ge(w.keys_got, 16 * UK)
            link(dve.tensor_copy(index[:, 0, U:U + UK], keys[:, :]))
            for b in range(1, B):
                link(dve.tensor_scalar_add(index[:, b, :], index[:, 0, :], float(b * S)))

        @block.gpsimd
        def _(pool):
            pool.iota(offs[:, :], [[0, 1]], base=0, channel_multiplier=1).then_inc(made, 1)
            with pool.Fori(0, NT // 4) as g:
                for q in range(4):
                    wait_alone(w, pool, staged, ONE + g * 4 + q + 1)
                    for k in range(K0):
                        pool.indirect_dma_start(out=w.xe_dram[:, :], out_offset=bass.IndirectOffsetOnAxis(ap=at[q][:, k:k + 1], axis=0),
                                                in_=rows[q][:, :], in_offset=None, bounds_check=E0 * CAP - 1, oob_is_err=False).then_inc(sent[q], 16)
            for q in range(4):
                pool.wait_ge(sent[q], 16 * K0 * (NT // 4))
            pool.wait_ge(key_at_ready, ONE + 1)
            for j in range(UK):
                pool.indirect_dma_start(out=keys[:, j:j + 1], out_offset=None, in_=m.rearrange("(n o) -> n o", o=1),
                                        in_offset=bass.IndirectOffsetOnAxis(ap=key_at[:, j:j + 1], axis=0)).then_inc(w.keys_got, 16)
            pool.wait_ge(w.keys_got, 16 * UK)


def stage_experts(nc, w):
    NB = 8
    with ExitStack() as ctx:
        sem = lambda name: semaphore(nc, ctx, name)
        loaded = [sem(f"e_loaded{q}") for q in range(NB)]
        turned, xT_ready = sem("e_turned"), sem("e_xT_ready")
        up_ready, silu_ready, g_ready, down_ready = sem("e_up_ready"), sem("e_silu_ready"), sem("e_g_ready"), sem("e_down_ready")
        y_ready = sem("e_y_ready")
        stored = [sem(f"e_stored{q}") for q in range(2)]
        SC = CAP // P
        X = [sbuf(nc, ctx, f"e_X{q}", [P, SC, D]) for q in range(NB)]
        W1 = [sbuf(nc, ctx, f"e_W1{q}", [P, KD, 2 * I0]) for q in range(NB)]
        W2 = [sbuf(nc, ctx, f"e_W2{q}", [P, D]) for q in range(NB)]
        XT = [sbuf(nc, ctx, f"e_XT{q}", [P, KD, CAP]) for q in range(2)]
        SG = [sbuf(nc, ctx, f"e_SG{q}", [P, CAP]) for q in range(2)]
        G = [sbuf(nc, ctx, f"e_G{q}", [P, CAP]) for q in range(2)]
        Y = [sbuf(nc, ctx, f"e_Y{q}", [P, SC, D]) for q in range(2)]
        px = [psum(nc, ctx, f"e_px{q}", [P, KD, CAP]) for q in range(2)]
        ph = [psum(nc, ctx, f"e_ph{q}", [P, 2, CAP]) for q in range(2)]
        py = [psum(nc, ctx, f"e_py{q}", [P, SC, D]) for q in range(2)]
        block = start(nc, ctx)

        @block.sync
        def _(sp):
            with sp.Fori(0, E0 // NB) as g:
                for q in range(NB):
                    e = g * NB + q
                    if q % 2 == 0:
                        sp.wait_ge(down_ready, ONE + g * NB + q + 2)
                    sp.dma_start(W1[q][:, :, :], w.w1_0[bass.ds(e, 1), :, :].rearrange("o (k p) n -> p (o k) n", p=P)).then_inc(loaded[q], 16)
                    sp.dma_start(W2[q][:, :], w.w2_0[bass.ds(e, 1), :, :].rearrange("o p n -> p (o n)")).then_inc(loaded[q], 16)
                    sp.dma_start(X[q][:, :, :], w.xe_dram[bass.ds(e * CAP, CAP), :].rearrange("(s p) n -> p s n", p=P)).then_inc(loaded[q], 16)

        @block.tensor
        def _(pe):
            def turn_tokens(g, i, n):
                for q in range(2):
                    pe.wait_ge(loaded[i * 2 + q], ONE + 48 * g + 48)
                    pe.wait_ge(xT_ready, ONE + n * 2)
                    for s in range(SC):
                        for k in range(KD):
                            last = pe.transpose(px[q][:, k, s * P:(s + 1) * P], X[i * 2 + q][:, s, k * P:(k + 1) * P], w.ident[:, :])
                    last.then_inc(turned, 1)

            def four(g, last_four):
                for i in range(NB // 2):
                    n = g * (NB // 2) + i
                    for q in range(2):
                        pe.wait_ge(xT_ready, ONE + n * 2 + q + 1)
                        pe.wait_ge(g_ready, ONE + n * 2)
                        for f in range(2):
                            for k in range(KD):
                                last = pe.matmul(ph[q][:, f, :], W1[i * 2 + q][:, k, f * I0:(f + 1) * I0], XT[q][:, k, :], start=k == 0, stop=k == KD - 1)
                        last.then_inc(up_ready, 1)
                    if i + 1 < NB // 2:
                        turn_tokens(g, i + 1, n + 1)
                    elif not last_four:
                        turn_tokens(g + 1, 0, n + 1)
                    for q in range(2):
                        pe.wait_ge(g_ready, ONE + n * 2 + q + 1)
                        pe.wait_ge(y_ready, ONE + n * 2)
                        for s in range(SC):
                            last = pe.matmul(py[q][:, s, :], G[q][:, s * P:(s + 1) * P], W2[i * 2 + q][:, :], start=True, stop=True)
                        last.then_inc(down_ready, 1)

            pe.sem_inc(down_ready, NB)
            turn_tokens(0, 0, 0)
            with pe.Fori(0, E0 // NB - 1) as g:
                four(g, False)
            four(E0 // NB - 1, True)

        @block.scalar
        def _(act):
            with act.Fori(0, E0 // 2) as g:
                for q in range(2):
                    act.wait_ge(up_ready, ONE + g * 2 + q + 1)
                    act.wait_ge(g_ready, ONE + g * 2)
                    act.activation(SG[q][:, :], ph[q][:, 0, :], ACT.Silu).then_inc(silu_ready, 1)
                for q in range(2):
                    act.wait_ge(y_ready, ONE + g * 2 + q + 1)
                    act.dma_start(w.ye_dram[bass.ds((g * 2 + q) * CAP, CAP), :].rearrange("(s p) n -> p s n", p=P), Y[q][:, :, :]).then_inc(stored[q], 16)
            for q in range(2):
                act.wait_ge(stored[q], ONE + 16 * (E0 // 2))

        @block.vector
        def _(dve):
            def keep_tokens(g):
                for q in range(2):
                    dve.wait_ge(turned, ONE + g * 2 + q + 1)
                    dve.wait_ge(up_ready, ONE + g * 2)
                    dve.tensor_copy(XT[q][:, :, :], px[q][:, :, :]).then_inc(xT_ready, 1)

            def pair(g, last_pair):
                for q in range(2):
                    dve.wait_ge(silu_ready, ONE + g * 2 + q + 1)
                    dve.wait_ge(down_ready, ONE + NB + g * 2)
                    dve.tensor_tensor(G[q][:, :], SG[q][:, :], ph[q][:, 1, :], ALU.mult).then_inc(g_ready, 1)
                if not last_pair:
                    keep_tokens(g + 1)
                for q in range(2):
                    dve.wait_ge(down_ready, ONE + NB + g * 2 + q + 1)
                    dve.wait_ge(stored[q], ONE + 16 * g)
                    dve.tensor_copy(Y[q][:, :, :], py[q][:, :, :]).then_inc(y_ready, 1)

            keep_tokens(0)
            with dve.Fori(0, E0 // 2 - 1) as g:
                pair(g, False)
            pair(E0 // 2 - 1, True)


def stage_combine(nc, w):
    with ExitStack() as ctx:
        sem = lambda name: semaphore(nc, ctx, name)
        staged, summed, scaled, added = sem("f_staged"), sem("f_summed"), sem("f_scaled"), sem("f_added")
        got = [gpsimd_dma_semaphore(nc, ctx, f"f_got{q}") for q in range(4)]
        stored = sem("f_stored")
        at = [sbuf(nc, ctx, f"f_at{q}", [P, K0], I32) for q in range(4)]
        y = [sbuf(nc, ctx, f"f_y{q}", [P, K0, D]) for q in range(4)]
        acc = [sbuf(nc, ctx, f"f_acc{q}", [P, 1, D]) for q in range(4)]
        block = start(nc, ctx)

        @block.gpsimd
        def _(pool):
            with pool.Fori(0, NT // 4) as g:
                for q in range(4):
                    wait_alone(w, pool, staged, ONE + g * 4 + q + 1)
                    for k in range(K0):
                        pool.indirect_dma_start(out=y[q][:, k, :], out_offset=None, in_=w.ye_dram[:, :],
                                                in_offset=bass.IndirectOffsetOnAxis(ap=at[q][:, k:k + 1], axis=0)).then_inc(got[q], 16)

        @block.vector
        def _(dve):
            def stage(t, q):
                dve.tensor_copy(at[q][:, :].rearrange("p (o k) -> p o k", o=1), w.get_from[:, bass.ds(t, 1), :]).then_inc(staged, 1)

            for q in range(4):
                stage(q, q)
            with dve.Fori(0, B) as b:
                with dve.Fori(0, TB // 4) as gb:
                    g = b * (TB // 4) + gb
                    for q in range(4):
                        t = g * 4 + q
                        dve.wait_ge(got[q], 16 * K0 * g + 16 * K0)
                        p4 = lambda k: w.gate4[:, bass.ds(t, 1), k:k + 1].rearrange("p a b -> p (a b)")
                        y1 = lambda k: y[q][:, k:k + 1, :]
                        dve.tensor_scalar(acc[q][:, :, :], y1(0), p4(0), None, ALU.mult).then_inc(summed, 1)
                        for k in range(1, K0):
                            dve.wait_ge(summed, ONE + K0 * t + k)
                            dve.scalar_tensor_tensor(acc[q][:, :, :], y1(k), p4(k), acc[q][:, :, :], op0=ALU.mult, op1=ALU.add).then_inc(summed, 1)
                        dve.wait_ge(summed, ONE + K0 * t + K0)
                        stage_t = t + 4
                        dve.tensor_copy(at[q][:, :].rearrange("p (o k) -> p o k", o=1), w.get_from[:, bass.ds(stage_t, 1), :]).then_inc(staged, 1)
                        dve.tensor_tensor(acc[q][:, :, :], acc[q][:, :, :], w.modrow[0][:, bass.ds(b, 1), GB * D:(GB + 1) * D], ALU.mult).then_inc(scaled, 1)
                        dve.wait_ge(scaled, ONE + t + 1)
                        xs = w.x[:, bass.ds(t, 1), :]
                        dve.tensor_tensor(xs, xs, acc[q][:, :, :], ALU.add).then_inc(added, 1)

        @block.sync
        def _(sp):
            with sp.Fori(0, NT // 4) as g:
                sp.wait_ge(added, ONE + g * 4 + 4)
                sp.dma_start(w.x2_dram[bass.ds(g * 4 * P, 4 * P), :].rearrange("(t p) n -> p t n", p=P), w.x[:, bass.ds(g * 4, 4), :]).then_inc(stored, 16)
            sp.wait_ge(stored, ONE + 16 * (NT // 4))


def stage_gather(nc, w):
    with ExitStack() as ctx:
        loaded = semaphore(nc, ctx, "i_loaded")
        got = gpsimd_dma_semaphore(nc, ctx, "i_got")
        block = start(nc, ctx)

        @block.sync
        def _(sp):
            sp.dma_start(w.Wqkv1[:, :, :], w.a['L1_attn_Wqkv'].rearrange("(k p) n -> p k n", p=P)).then_inc(loaded, 16)
            sp.dma_start(w.Wproj1[:, :, :], w.a['L1_attn_Wproj'].rearrange("(k p) n -> p k n", p=P)).then_inc(loaded, 16)
            sp.dma_start(w.bqk1[:, :], w.a['L1_attn_bqkv'][0:2 * D].rearrange("(c p) -> p c", p=P), allow_slow_non_contiguous=True).then_inc(loaded, 16)
            sp.dma_start(w.bv1[:, :], w.a['L1_attn_bqkv'][2 * D:3 * D].rearrange("(o n) -> o n", o=1).broadcast_to([P, D])).then_inc(loaded, 16)
            sp.dma_start(w.bo1[:, :], w.a['L1_attn_bproj'].rearrange("(o n) -> o n", o=1).broadcast_to([P, D])).then_inc(loaded, 16)
            sp.wait_ge(loaded, ONE + 80)

        @block.gpsimd
        def _(pool):
            for b in range(B):
                for u in range(U + UK):
                    pool.indirect_dma_start(out=w.xg[:, b * (U + UK) + u, :], out_offset=None, in_=w.x2_dram[:, :],
                                            in_offset=bass.IndirectOffsetOnAxis(ap=w.index[:, b, u:u + 1], axis=0)).then_inc(got, 16)
            pool.wait_ge(got, 16 * B * (U + UK))


def stage_keys(nc, w):
    with ExitStack() as ctx:
        sem = lambda name: semaphore(nc, ctx, name)
        norm_ready, turned, hk_ready, projected, kT_ready, made, step = (
            sem(f"k_{n}") for n in ("norm_ready", "turned", "hk_ready", "projected", "kT_ready", "made", "step"))
        xn = sbuf(nc, ctx, "k_xn", [P, UK, D])
        pT = psum(nc, ctx, "k_pT", [P, KD, CH])
        pk = psum(nc, ctx, "k_pk", [P, KD, CH])
        block = start(nc, ctx)
        R = U * 2 * NK

        @block.gpsimd
        def _(pool):
            pool.memset(w.own[:, :], 1.0).then_inc(made, 1)
            pool.wait_ge(made, ONE + 1)
            pool.affine_select(out=w.own[:, :], in_=w.own[:, :], compare_op=ALU.is_ge, fill=0.0, base=0,
                               pattern=[[-NK, P // NK]], channel_multiplier=1).then_inc(made, 1)
            pool.wait_ge(made, ONE + 2)
            pool.affine_select(out=w.own[:, :], in_=w.own[:, :], compare_op=ALU.is_ge, fill=0.0, base=NK - 1,
                               pattern=[[NK, P // NK]], channel_multiplier=-1).then_inc(made, 1)
            pool.wait_ge(made, ONE + 3)

        @block.vector
        def _(dve):
            link = linker(dve, step)
            for b in range(B):
                if b:
                    dve.wait_ge(turned, ONE + b)
                for j in range(UK):
                    i = b * (U + UK) + U + j
                    last = dve.tensor_scalar(xn[:, j, :], w.xg[:, i, :], w.mean_var[:, i, 0:1], w.rstd[:, i:i + 1], ALU.subtract, ALU.mult)
                last.then_inc(norm_ready, 1)
            link(dve.tensor_scalar_mul(w.bqk1[:, 0:KD], w.bqk1[:, 0:KD], w.SCALE))
            dve.wait_ge(made, ONE + 3)
            link(dve.tensor_copy(w.own_square[:, :].rearrange("p (h d) -> p h d", d=DH), w.own[:, :].rearrange("p (h o) -> p h o", o=1).broadcast_to([P, P // DH, DH])))
            for b in range(B):
                link(dve.tensor_tensor(w.gbo1[:, b, :], w.modrow[1][:, b, GA * D:(GA + 1) * D], w.bo1[:, :], ALU.mult))

        @block.tensor
        def _(pe):
            for b in range(B):
                pe.wait_ge(norm_ready, ONE + b + 1)
                if b:
                    pe.wait_ge(hk_ready, ONE + KD * b)
                for j in range(UK):
                    for k in range(KD):
                        last = pe.transpose(pT[:, k, j * P:(j + 1) * P], xn[:, j, k * P:(k + 1) * P], w.ident[:, :])
                last.then_inc(turned, 1)
                pe.wait_ge(hk_ready, ONE + KD * b + KD)
                if b:
                    pe.wait_ge(kT_ready, ONE + KD * b)
                for f in range(KD):
                    for k in range(KD):
                        last = pe.matmul(pk[:, f, 0:R], w.Wqkv1[:, k, D + f * P:D + (f + 1) * P], w.hk[:, k, b, 0:R], start=k == 0, stop=k == KD - 1)
                last.then_inc(projected, 1)

        @block.scalar
        def _(act):
            for b in range(B):
                act.wait_ge(turned, ONE + b + 1)
                for k in range(KD):
                    act.activation(w.hk[:, k, b, :], pT[:, k, 0:UK * P], ACT.Identity, scale=w.modcol[:, 1, 2 * CA + k, b:b + 1],
                                   bias=w.modcol[:, 1, 2 * SA + k, b:b + 1]).then_inc(hk_ready, 1)
                act.wait_ge(projected, ONE + b + 1)
                for f in range(KD):
                    act.activation(w.kT[:, f, b, :], pk[:, f, 0:R], ACT.Identity, bias=w.bqk1[:, KD + f:KD + f + 1]).then_inc(kT_ready, 1)


def stage_values(nc, w):
    with ExitStack() as ctx:
        sem = lambda name: semaphore(nc, ctx, name)
        rep_ready, v_ready, vb_ready, vd_ready = (sem(f"v_{n}") for n in ("rep_ready", "v_ready", "vb_ready", "vd_ready"))
        GH = P // NK
        M = 2
        VT = 2 * U // M
        assert VT % 3 == 0
        hr = [sbuf(nc, ctx, f"v_hr{q}", [P, KD, M, GH, NK]) for q in range(3)]
        vb = [sbuf(nc, ctx, f"v_vb{q}", [P, M, D]) for q in range(3)]
        pv = [psum(nc, ctx, f"v_pv{q}", [P, M, D]) for q in range(3)]
        block = start(nc, ctx)

        @block.scalar
        def _(act):
            with act.Fori(0, B) as b:
                with act.Fori(0, VT // 3) as j:
                    for q in range(3):
                        n = (b * (VT // 3) + j) * 3 + q
                        act.wait_ge(v_ready, ONE + n - q)
                        keys = bass.ds(j * (3 * M * NK) + q * (M * NK), M * NK)
                        for k in range(KD):
                            last = act.activation(hr[q][:, k, :, :, :], w.hk[:, k, bass.ds(b, 1), keys].rearrange("p a (n o r) -> p (a n) o r", o=1, r=NK).broadcast_to([P, M, GH, NK]), ACT.Copy)
                        last.then_inc(rep_ready, 1)

        @block.tensor
        def _(pe):
            with pe.Fori(0, B * VT // 3) as g:
                for q in range(3):
                    pe.wait_ge(rep_ready, ONE + g * 3 + q + 1)
                    pe.wait_ge(vb_ready, ONE + g * 3)
                    for m in range(M):
                        for k in range(KD):
                            last = pe.matmul(pv[q][:, m, :], hr[q][:, k, m, :, :], w.Wqkv1[:, k, 2 * D:3 * D], start=k == 0, stop=k == KD - 1)
                    last.then_inc(v_ready, 1)

        @block.vector
        def _(dve):
            with dve.Fori(0, B * VT // 3) as g:
                for q in range(3):
                    dve.wait_ge(v_ready, ONE + g * 3 + q + 1)
                    dve.wait_ge(vd_ready, ONE + g * 3)
                    dve.tensor_tensor(vb[q][:, :, :], pv[q][:, :, :], w.bv1[:, :].rearrange("p (o n) -> p o n", o=1).broadcast_to([P, M, D]), ALU.add).then_inc(vb_ready, 1)

        @block.gpsimd
        def _(pool):
            own = w.own[:, :].rearrange("p (o h q) -> p o h q", o=1, q=1).broadcast_to([P, M, GH, DH])
            with pool.Fori(0, B * VT // 3) as g:
                for q in range(3):
                    n = g * 3 + q
                    wait_alone(w, pool, vb_ready, ONE + n + 1)
                    for k in range(KD):
                        cols = lambda v: v[:, :, k * P:(k + 1) * P].rearrange("p m (h d) -> p m h d", d=DH)
                        last = pool.tensor_tensor(w.vd[:, bass.ds(n * M, M), k * P:(k + 1) * P].rearrange("p m (h d) -> p m h d", d=DH), cols(vb[q]), own, ALU.mult)
                    last.then_inc(vd_ready, 1)


def stage_blocks(nc, w):
    with ExitStack() as ctx:
        sem = lambda name: semaphore(nc, ctx, name)
        s = World()
        s.norm_ready = sem("l_norm_ready")
        s.turned = sem("l_turned")
        s.hT_ready = sem("l_hT_ready")
        s.projected = sem("l_projected")
        s.q_ready = sem("l_q_ready")
        s.kd_ready = sem("l_kd_ready")
        s.scored = sem("l_scored")
        s.top_ready = sem("l_top_ready")
        s.less_ready = sem("l_less_ready")
        s.exp_ready = sem("l_exp_ready")
        s.eps_ready = sem("l_eps_ready")
        s.inverse_ready = sem("l_inverse_ready")
        s.total_ready = sem("l_total_ready")
        s.summed = sem("l_summed")
        s.oT_ready = sem("l_oT_ready")
        s.out_ready = sem("l_out_ready")
        s.gated = sem("l_gated")
        s.kept = sem("l_kept")
        GH = P // NK
        xn = sbuf(nc, ctx, "l_xn", [P, TPT, D])
        hT = sbuf(nc, ctx, "l_hT", [P, KD, TPT * P])
        qT = sbuf(nc, ctx, "l_qT", [P, KD, TPT * P])
        kd = sbuf(nc, ctx, "l_kd", [P, KD, TPT * 2, GH, NK])
        sc = sbuf(nc, ctx, "l_sc", [P, KD, TPT * P])
        top = sbuf(nc, ctx, "l_top", [P, KD, TPT * 2])
        tot = sbuf(nc, ctx, "l_tot", [P, KD, TPT * P])
        oT = sbuf(nc, ctx, "l_oT", [P, KD, TPT * P])
        gate = sbuf(nc, ctx, "l_gate", [P, TPT, D])
        pa = psum(nc, ctx, "l_pa", [P, 2, CH])
        pb = psum(nc, ctx, "l_pb", [P, 2, CH])
        pf = psum(nc, ctx, "l_pf", [P, 2, CH])
        pq = psum(nc, ctx, "l_pq", [P, 2, CH])
        block = start(nc, ctx)
        wide = lambda t: t[:, :, :].rearrange("p a n -> p (a n)")[:, 0:TPT * D]
        TURNS = U // TPT

        @block.vector
        def _(dve):
            def norm(n, i0):
                dve.wait_ge(s.turned, ONE + n)
                for u in range(TPT):
                    i = i0 + u
                    last = dve.tensor_scalar(xn[:, u:u + 1, :], w.xg[:, bass.ds(i, 1), :], w.mean_var[:, bass.ds(i, 1), 0:1].rearrange("p a b -> p (a b)"),
                                             w.rstd[:, bass.ds(i, 1)], ALU.subtract, ALU.mult)
                last.then_inc(s.norm_ready, 1)

            norm(0, 0)
            for b in range(B):
                for j in range(TURNS):
                    n = b * TURNS + j
                    dve.wait_ge(s.scored, ONE + n + 1)
                    by_block = lambda v: v[:, :, 0:TPT * P].rearrange("p k (m q) -> p k m q", q=BLOCK)
                    over = top[:, :, :].rearrange("p k (m o) -> p k m o", o=1).broadcast_to([P, KD, TPT * 2, BLOCK])
                    dve.reduce_max(top[:, :, :], by_block(pb), AX).then_inc(s.top_ready, 1)
                    dve.wait_ge(s.top_ready, ONE + n + 1)
                    dve.tensor_tensor(by_block(sc), by_block(pb), over, ALU.subtract).then_inc(s.less_ready, 1)
                    if n + 1 < B * TURNS:
                        norm(n + 1, (n + 1) // TURNS * (U + UK) + (n + 1) % TURNS * TPT)
                    dve.wait_ge(s.total_ready, ONE + n + 1)
                    dve.tensor_scalar_add(tot[:, :, :], pa[:, :, 0:TPT * P], 1e-6).then_inc(s.eps_ready, 1)
                    dve.wait_ge(s.eps_ready, ONE + n + 1)
                    dve.reciprocal(tot[:, :, :], tot[:, :, :]).then_inc(s.inverse_ready, 1)
                    dve.wait_ge(s.inverse_ready, ONE + n + 1)
                    dve.wait_ge(s.summed, ONE + n + 1)
                    dve.tensor_tensor(oT[:, :, :], pb[:, :, 0:TPT * P], tot[:, :, :], ALU.mult).then_inc(s.oT_ready, 1)
                    dve.wait_ge(s.out_ready, ONE + n + 1)
                    dve.tensor_tensor(gate[:, :, :], wide(pa).rearrange("p (t n) -> p t n", t=TPT),
                                      w.modrow[1][:, bass.ds(b, 1), GA * D:(GA + 1) * D].broadcast_to([P, TPT, D]), ALU.mult).then_inc(s.gated, 1)
                    dve.wait_ge(s.gated, ONE + n + 1)
                    dve.tensor_tensor(w.att1[:, bass.ds(n * TPT, TPT), :], gate[:, :, :], w.gbo1[:, bass.ds(b, 1), :].broadcast_to([P, TPT, D]), ALU.add).then_inc(s.kept, 1)
            for b in range(B):
                if b == 0:
                    dve.wait_ge(s.kept, ONE + B * TURNS)
                t0, a0 = b * TB, b * U
                for x, y in ((w.x[:, t0:t0 + U - 1, :], w.att1[:, a0:a0 + U - 1, :]),
                             (w.x[:, t0 + U - 1:t0 + TB, :], w.att1[:, a0 + U - 1:a0 + U, :].broadcast_to([P, TB - U + 1, D]))):
                    dve.tensor_tensor(x, x, y, ALU.add)

        @block.gpsimd
        def _(pool):
            with pool.Fori(0, B) as b:
                with pool.Fori(0, TURNS) as j:
                    n = b * TURNS + j
                    keys = bass.ds(j * TPT * 2 * NK, TPT * 2 * NK)
                    own = w.own[:, :].rearrange("p (o h q) -> p o h q", o=1, q=1).broadcast_to([P, TPT * 2, GH, NK])
                    spread = lambda v: v.rearrange("p a (n o r) -> p (a n) o r", o=1, r=NK).broadcast_to([P, TPT * 2, GH, NK])
                    pool.wait_ge(s.scored, ONE + n)
                    for k in range(KD):
                        pool.tensor_tensor(kd[:, k, :, :, :], spread(w.kT[:, k, bass.ds(b, 1), keys]), own, ALU.mult).then_inc(s.kd_ready, 1)

        @block.tensor
        def _(pe):
            def front(n):
                pe.wait_ge(s.norm_ready, ONE + n + 1)
                pe.wait_ge(s.hT_ready, ONE + KD * n)
                for u in range(TPT):
                    for k in range(KD):
                        last = pe.transpose(pf[:, k, u * P:(u + 1) * P], xn[:, u, k * P:(k + 1) * P], w.ident[:, :])
                last.then_inc(s.turned, 1)
                pe.wait_ge(s.hT_ready, ONE + KD * n + KD)
                pe.wait_ge(s.q_ready, ONE + KD * n)
                for f in range(KD):
                    for k in range(KD):
                        last = pe.matmul(pq[:, f, 0:TPT * P], w.Wqkv1[:, k, f * P:(f + 1) * P], hT[:, k, :], start=k == 0, stop=k == KD - 1)
                last.then_inc(s.projected, 1)

            front(0)
            for n in range(B * TURNS):
                pe.wait_ge(s.q_ready, ONE + KD * n + KD)
                pe.wait_ge(s.kd_ready, ONE + KD * n + KD)
                pe.wait_ge(s.oT_ready, ONE + n)
                for k in range(KD):
                    for m in range(TPT * 2):
                        at = slice(m * BLOCK, (m + 1) * BLOCK)
                        last = pe.matmul(pb[:, k, at], kd[:, k, m, :, :], qT[:, k, at], start=True, stop=True)
                last.then_inc(s.scored, 1)
                pe.wait_ge(s.exp_ready, ONE + n + 1)
                pe.wait_ge(s.gated, ONE + n)
                for k in range(KD):
                    last = pe.matmul(pa[:, k, 0:TPT * P], w.own_square[:, :], sc[:, k, :], start=True, stop=True)
                last.then_inc(s.total_ready, 1)
                for k in range(KD):
                    for m in range(TPT * 2):
                        at = slice(m * BLOCK, (m + 1) * BLOCK)
                        last = pe.matmul(pb[:, k, at], w.vd[:, n * (TPT * 2) + m, k * P:(k + 1) * P], sc[:, k, at], start=True, stop=True)
                last.then_inc(s.summed, 1)
                if n + 1 < B * TURNS:
                    front(n + 1)
                pe.wait_ge(s.oT_ready, ONE + n + 1)
                for u in range(TPT):
                    for k in range(KD):
                        last = pe.matmul(wide(pa)[:, u * D:(u + 1) * D], oT[:, k, u * P:(u + 1) * P], w.Wproj1[:, k, :], start=k == 0, stop=k == KD - 1)
                last.then_inc(s.out_ready, 1)

        @block.scalar
        def _(act):
            def front(n):
                act.wait_ge(s.turned, ONE + n + 1)
                act.wait_ge(s.projected, ONE + n)
                b = n // TURNS
                for k in range(KD):
                    act.activation(hT[:, k, :], pf[:, k, 0:TPT * P], ACT.Identity, scale=w.modcol[:, 1, 2 * CA + k, b:b + 1],
                                   bias=w.modcol[:, 1, 2 * SA + k, b:b + 1]).then_inc(s.hT_ready, 1)
                act.wait_ge(s.projected, ONE + n + 1)
                act.wait_ge(s.scored, ONE + n)
                for f in range(KD):
                    act.activation(qT[:, f, :], pq[:, f, 0:TPT * P], ACT.Identity, scale=w.SCALE, bias=w.bqk1[:, f:f + 1]).then_inc(s.q_ready, 1)

            front(0)
            for n in range(B * TURNS):
                act.wait_ge(s.less_ready, ONE + n + 1)
                act.activation(sc[:, :, :], sc[:, :, :], ACT.Exp).then_inc(s.exp_ready, 1)
                if n + 1 < B * TURNS:
                    front(n + 1)



E1, K1, I1 = 8, 2, 512
GT = 2 * P
GTURNS = B * S * K1 // GT + E1
PACKED = 3 * KD * D + 3 * KD


def stage_places(nc, w):
    with ExitStack() as ctx:
        sem = lambda name: semaphore(nc, ctx, name)
        step, exp_request, exp_done, made = sem("t_step"), sem("t_exp_request"), sem("t_exp_done"), sem("t_made")
        mask_ready, counted = sem("t_mask_ready"), sem("t_counted")
        loaded = sem("t_loaded")
        N = NT * K1
        top = sbuf(nc, ctx, "t_top", [P, NT])
        total = sbuf(nc, ctx, "t_total", [P, NT])
        m8 = sbuf(nc, ctx, "t_m8", [P, NT, 8])
        i8 = sbuf(nc, ctx, "t_i8", [P, NT, 8], U32)
        i2 = sbuf(nc, ctx, "t_i2", [P, N])
        col_i = sbuf(nc, ctx, "t_col_i", [P, E1], I32)
        col = sbuf(nc, ctx, "t_col", [P, E1])
        turn_i = sbuf(nc, ctx, "t_turn_i", [P, GTURNS], I32)
        turn = sbuf(nc, ctx, "t_turn", [P, GTURNS])
        row_i = sbuf(nc, ctx, "t_row_i", [P, 1], I32)
        row = sbuf(nc, ctx, "t_row", [P, 1])
        chosen = sbuf(nc, ctx, "t_chosen", [P, N, E1], BF16)
        mask = sbuf(nc, ctx, "t_mask", [P, NT, E1], BF16)
        before = sbuf(nc, ctx, "t_before", [P, P], BF16)
        ones = sbuf(nc, ctx, "t_ones", [P, P], BF16)
        run = [sbuf(nc, ctx, f"t_run{q}", [P, NT, E1]) for q in range(2)]
        base = sbuf(nc, ctx, "t_base", [P, NT, E1])
        whole_i = sbuf(nc, ctx, "t_whole_i", [P, E1], I32)
        whole = sbuf(nc, ctx, "t_whole", [P, E1])
        first = sbuf(nc, ctx, "t_first", [P, E1])
        begun = sbuf(nc, ctx, "t_begun", [P, GTURNS, E1])
        prod = sbuf(nc, ctx, "t_prod", [P, N, E1])
        place = sbuf(nc, ctx, "t_place", [P, N])
        pw = psum(nc, ctx, "t_pw", [P, NT, E1])
        pt = psum(nc, ctx, "t_pt", [P, NT, E1])
        block = start(nc, ctx)

        @block.sync
        def _(sp):
            for dst, name in zip(w.shared, ('L1_ffn_sw1', 'L1_ffn_sw2', 'L1_ffn_sw3')):
                sp.dma_start(dst[:, :, :], w.a[name].rearrange("(k p) n -> p k n", p=P)).then_inc(loaded, 16)
            sp.wait_ge(loaded, ONE + 48)

        @block.gpsimd
        def _(pool):
            pool.iota(col_i[:, :], [[1, E1]], base=0, channel_multiplier=0).then_inc(made, 1)
            pool.iota(turn_i[:, :], [[GT, GTURNS]], base=0, channel_multiplier=0).then_inc(made, 1)
            pool.iota(row_i[:, :], [[0, 1]], base=0, channel_multiplier=1).then_inc(made, 1)
            pool.memset(ones[:, :], 1.0).then_inc(made, 1)
            pool.wait_ge(made, ONE + 4)
            pool.affine_select(out=before[:, :], in_=ones[:, :], compare_op=ALU.is_gt, fill=0.0, base=0,
                               pattern=[[1, P]], channel_multiplier=-1).then_inc(made, 1)

        @block.scalar
        def _(act):
            act.wait_ge(exp_request, ONE + 1)
            act.activation(w.logits1[:, :, :], w.logits1[:, :, :], ACT.Exp).then_inc(exp_done, 1)

        @block.tensor
        def _(pe):
            pe.wait_ge(made, ONE + 5)
            pe.wait_ge(mask_ready, ONE + 1)
            pe.matmul(pw[:, :, :], before[:, :], mask[:, :, :], start=True, stop=True)
            pe.matmul(pt[:, :, :], ones[:, :], mask[:, :, :], start=True, stop=True).then_inc(counted, 1)

        @block.vector
        def _(dve):
            link = linker(dve, step)
            probs = w.logits1
            softmax_rows(dve, link, probs, top, total, exp_request, exp_done)
            for t in range(NT):
                last = dve.max(m8[:, t, :], probs[:, t, :])
            link(last)
            for t in range(NT):
                last = dve.max_index(i8[:, t, :], m8[:, t, :], probs[:, t, :])
            dve.tensor_copy(w.gate2[:, :, :], m8[:, :, 0:K1])
            link(last)
            link(dve.tensor_copy(i2[:, :].rearrange("p (t k) -> p t k", k=K1), i8[:, :, 0:K1]))
            dve.wait_ge(made, ONE + 5)
            dve.tensor_copy(turn[:, :], turn_i[:, :])
            dve.tensor_copy(row[:, :], row_i[:, :])
            link(dve.tensor_copy(col[:, :], col_i[:, :]))
            link(dve.tensor_tensor(chosen[:, :, :], col[:, :].rearrange("p (o e) -> p o e", o=1).broadcast_to([P, N, E1]),
                                   i2[:, :].rearrange("p (n o) -> p n o", o=1).broadcast_to([P, N, E1]), ALU.is_equal))
            by_k = chosen[:, :, :].rearrange("p (t k) e -> p t k e", k=K1)
            dve.tensor_tensor(mask[:, :, :], by_k[:, :, 0, :], by_k[:, :, 1, :], ALU.add).then_inc(mask_ready, 1)
            dve.wait_ge(counted, ONE + 1)
            link(dve.tensor_copy(run[0][:, :, :], pt[:, :, :]))
            q, reach = 0, 1
            while reach < NT:
                dve.tensor_copy(run[1 - q][:, 0:reach, :], run[q][:, 0:reach, :])
                link(dve.tensor_tensor(run[1 - q][:, reach:NT, :], run[q][:, reach:NT, :], run[q][:, 0:NT - reach, :], ALU.add))
                q, reach = 1 - q, 2 * reach
            link(dve.tensor_scalar_add(whole_i[:, :], run[q][:, NT - 1, :], float(GT - 1)))
            link(dve.tensor_scalar(whole_i[:, :], whole_i[:, :], -GT, None, ALU.bitwise_and))
            dve.memset(first[:, 0:1], 0.0)
            link(dve.tensor_copy(whole[:, :], whole_i[:, :]))
            for e in range(1, E1):
                link(dve.tensor_tensor(first[:, e:e + 1], first[:, e - 1:e], whole[:, e - 1:e], ALU.add))
            link(dve.tensor_tensor(base[:, :, :], pw[:, :, :], first[:, :].rearrange("p (o e) -> p o e", o=1).broadcast_to([P, NT, E1]), ALU.add))
            link(dve.tensor_tensor(base[:, 1:NT, :], base[:, 1:NT, :], run[q][:, 0:NT - 1, :], ALU.add))
            for k in range(K1):
                last = dve.tensor_tensor(prod[:, :, :].rearrange("p (t k) e -> p t k e", k=K1)[:, :, k, :], by_k[:, :, k, :], base[:, :, :], ALU.mult)
            dve.tensor_tensor(begun[:, :, :], turn[:, :].rearrange("p (r o) -> p r o", o=1).broadcast_to([P, GTURNS, E1]),
                              first[:, :].rearrange("p (o e) -> p o e", o=1).broadcast_to([P, GTURNS, E1]), ALU.is_ge)
            link(last)
            link(dve.reduce_sum(place[:, :], prod[:, :, :], AX))
            link(dve.reduce_sum(turn[:, :], begun[:, :, :], AX))
            dve.tensor_copy(w.slot2[:, :, :].rearrange("p t k -> p (t k)"), place[:, :])
            link(dve.tensor_scalar(turn[:, :], turn[:, :], float(P), float(-P), ALU.mult, ALU.add))
            link(dve.tensor_tensor(w.turn_row[:, :], turn[:, :], row[:, :].broadcast_to([P, GTURNS]), ALU.add))


def stage_shared(nc, w):
    with ExitStack() as ctx:
        sem = lambda name: semaphore(nc, ctx, name)
        a_ready, b_ready, silu_ready, u_ready, z_ready, z_out, added, staged = (
            sem(f"z_{n}") for n in ("a_ready", "b_ready", "silu_ready", "u_ready", "z_ready", "z_out", "added", "staged"))
        sent = gpsimd_dma_semaphore(nc, ctx, "z_sent")
        IB = I1 // P
        W1, W2, W3 = w.shared
        si = sbuf(nc, ctx, "z_si", [P, IB, CH])
        u = sbuf(nc, ctx, "z_u", [P, IB, CH])
        gz = sbuf(nc, ctx, "z_gz", [P, CT, D])
        rows = sbuf(nc, ctx, "z_rows", [P, CT, K1, D])
        at = sbuf(nc, ctx, "z_at", [P, CT, K1], I32)
        pa = psum(nc, ctx, "z_pa", [P, 2, CH])
        pb = psum(nc, ctx, "z_pb", [P, 2, CH])
        pz = psum(nc, ctx, "z_pz", [P, CT, D])
        block = start(nc, ctx)

        @block.tensor
        def _(pe):
            with pe.Fori(0, NC) as c:
                h = lambda k: w.hT1[:, k, bass.ds(c * CH, CH)]
                for i in range(IB):
                    if i < 2:
                        pe.wait_ge(u_ready, ONE + IB * c)
                    else:
                        pe.wait_ge(u_ready, ONE + IB * c + i - 1)
                    for k in range(KD):
                        last = pe.matmul(pa[:, i % 2, :], W1[:, k, i * P:(i + 1) * P], h(k), start=k == 0, stop=k == KD - 1)
                    last.then_inc(a_ready, 1)
                    for k in range(KD):
                        last = pe.matmul(pb[:, i % 2, :], W2[:, k, i * P:(i + 1) * P], h(k), start=k == 0, stop=k == KD - 1)
                    last.then_inc(b_ready, 1)
                pe.wait_ge(u_ready, ONE + IB * c + IB)
                pe.wait_ge(z_out, ONE + c)
                for t in range(CT):
                    for i in range(IB):
                        last = pe.matmul(pz[:, t, :], u[:, i, t * P:(t + 1) * P], W3[:, i, :], start=i == 0, stop=i == IB - 1)
                last.then_inc(z_ready, 1)

        @block.scalar
        def _(act):
            with act.Fori(0, NC) as c:
                act.wait_ge(u_ready, ONE + IB * c)
                for i in range(IB):
                    act.wait_ge(a_ready, ONE + IB * c + i + 1)
                    act.activation(si[:, i, :], pa[:, i % 2, :], ACT.Silu).then_inc(silu_ready, 1)

        @block.vector
        def _(dve):
            with dve.Fori(0, B) as b:
                with dve.Fori(0, NC // B) as cb:
                    c = b * (NC // B) + cb
                    dve.wait_ge(sent, 16 * CT * K1 * c)
                    dve.tensor_copy(at[:, :, :], w.slot2[:, bass.ds(c * CT, CT), :])
                    for t in range(CT):
                        for k in range(K1):
                            last = dve.tensor_scalar(rows[:, t, k:k + 1, :], w.h[:, bass.ds(c * CT + t, 1), :],
                                                     w.gate2[:, bass.ds(c * CT + t, 1), k:k + 1].rearrange("p a b -> p (a b)"), None, ALU.mult)
                    last.then_inc(staged, 1)
                    dve.wait_ge(z_ready, ONE + c)
                    for i in range(IB):
                        dve.wait_ge(silu_ready, ONE + IB * c + i + 1)
                        dve.wait_ge(b_ready, ONE + IB * c + i + 1)
                        dve.tensor_tensor(u[:, i, :], si[:, i, :], pb[:, i % 2, :], ALU.mult).then_inc(u_ready, 1)
                    dve.wait_ge(z_ready, ONE + c + 1)
                    dve.wait_ge(added, ONE + c)
                    dve.tensor_tensor(gz[:, :, :], pz[:, :, :], w.modrow[1][:, bass.ds(b, 1), GB * D:(GB + 1) * D].broadcast_to([P, CT, D]), ALU.mult).then_inc(z_out, 1)

        @block.gpsimd
        def _(pool):
            with pool.Fori(0, NC) as c:
                wait_alone(w, pool, staged, ONE + c + 1)
                for t in range(CT):
                    for k in range(K1):
                        pool.indirect_dma_start(out=w.xe_dram[:, :], out_offset=bass.IndirectOffsetOnAxis(ap=at[:, t, k:k + 1], axis=0),
                                                in_=rows[:, t, k, :], in_offset=None, bounds_check=E0 * CAP - 1, oob_is_err=False).then_inc(sent, 16)
                wait_alone(w, pool, z_out, ONE + c + 1)
                xs = w.x[:, bass.ds(c * CT, CT), :]
                pool.tensor_tensor(xs, xs, gz[:, :, :], ALU.add).then_inc(added, 1)
            pool.wait_ge(sent, 16 * K1 * NT)


def stage_groups(nc, w):
    NB = 8
    SC = GT // P
    with ExitStack() as ctx:
        sem = lambda name: semaphore(nc, ctx, name)
        x_loaded = [sem(f"y_x_loaded{q}") for q in range(NB)]
        w_got = [gpsimd_dma_semaphore(nc, ctx, f"y_w_got{q}") for q in range(NB)]
        staged, turned, xT_ready, up_ready, third_ready, silu_ready, x3_ready, down_ready, t_ready, back_ready, y_ready = (
            sem(f"y_{n}") for n in ("staged", "turned", "xT_ready", "up_ready", "third_ready", "silu_ready", "x3_ready", "down_ready",
                                    "t_ready", "back_ready", "y_ready"))
        stored = [sem(f"y_stored{q}") for q in range(2)]
        X = [sbuf(nc, ctx, f"y_X{q}", [P, SC, D]) for q in range(NB)]
        W = [sbuf(nc, ctx, f"y_W{q}", [P, PACKED]) for q in range(NB)]
        at = [sbuf(nc, ctx, f"y_at{q}", [P, 1], I32) for q in range(NB)]
        XT = [sbuf(nc, ctx, f"y_XT{q}", [P, KD, GT]) for q in range(2)]
        HH = [sbuf(nc, ctx, f"y_HH{q}", [P, KD, GT]) for q in range(2)]
        X3 = [sbuf(nc, ctx, f"y_X3{q}", [P, KD, GT]) for q in range(2)]
        T = [sbuf(nc, ctx, f"y_T{q}", [P, KD, GT]) for q in range(2)]
        Y = [sbuf(nc, ctx, f"y_Y{q}", [P, SC, D]) for q in range(2)]
        px = [psum(nc, ctx, f"y_px{q}", [P, 2, GT]) for q in range(2)]
        p1 = [psum(nc, ctx, f"y_p1{q}", [P, KD, GT]) for q in range(2)]
        p3 = [psum(nc, ctx, f"y_p3{q}", [P, KD, GT]) for q in range(2)]
        p2 = [psum(nc, ctx, f"y_p2{q}", [P, KD, GT]) for q in range(2)]
        block = start(nc, ctx)
        FIRST, THIRD, SECOND = range(3)
        weight = lambda i, which, k, f: W[i][:, (which * KD + k) * D + f * P:(which * KD + k) * D + (f + 1) * P]
        bias = lambda i, which, f: W[i][:, 3 * KD * D + which * KD + f:3 * KD * D + which * KD + f + 1]
        assert GTURNS % NB == 0

        @block.sync
        def _(sp):
            with sp.Fori(0, GTURNS // NB) as g:
                for i in range(NB):
                    n = g * NB + i
                    sp.wait_ge(t_ready, ONE + n + 1)
                    sp.dma_start(X[i][:, :, :], w.xe_dram[bass.ds(n * GT, GT), :].rearrange("(s p) n -> p s n", p=P)).then_inc(x_loaded[i], 16)

        @block.gpsimd
        def _(pool):
            with pool.Fori(0, GTURNS // NB) as g:
                for i in range(NB):
                    n = g * NB + i
                    wait_alone(w, pool, t_ready, ONE + n + 1)
                    pool.tensor_copy(at[i][:, :], w.turn_row[:, bass.ds(n, 1)]).then_inc(staged, 1)
                    wait_alone(w, pool, staged, ONE + n + 1)
                    pool.indirect_dma_start(out=W[i][:, :], out_offset=None, in_=w.packed,
                                            in_offset=bass.IndirectOffsetOnAxis(ap=at[i][:, 0:1], axis=0)).then_inc(w_got[i], 16)

        @block.tensor
        def _(pe):
            pe.sem_inc(t_ready, NB)
            def turn_tokens(g, j, n):
                for q in range(2):
                    i = j * 2 + q
                    pe.wait_ge(x_loaded[i], ONE + 16 * g + 16)
                    pe.wait_ge(xT_ready, ONE + n)
                    for s in range(SC):
                        for k in range(KD):
                            last = pe.transpose(px[q][:, k, s * P:(s + 1) * P], X[i][:, s, k * P:(k + 1) * P], w.ident[:, :])
                    last.then_inc(turned, 1)

            def four(g, last_four):
                for j in range(NB // 2):
                    n = g * NB + j * 2
                    for q in range(2):
                        i = j * 2 + q
                        pe.wait_ge(w_got[i], 16 * g + 16)
                        pe.wait_ge(xT_ready, ONE + n + q + 1)
                        for which, out, ready in ((THIRD, p3, third_ready), (FIRST, p1, up_ready)):
                            if which == FIRST:
                                pe.wait_ge(y_ready, ONE + n)
                            for f in range(KD):
                                for k in range(KD):
                                    last = pe.matmul(out[q][:, f, :], weight(i, which, k, f), XT[q][:, k, :], start=k == 0, stop=k == KD - 1)
                            last.then_inc(ready, 1)
                    for q in range(2):
                        i = j * 2 + q
                        pe.wait_ge(silu_ready, ONE + n + q + 1)
                        for f in range(KD):
                            for k in range(KD):
                                last = pe.matmul(p2[q][:, f, :], weight(i, SECOND, k, f), HH[q][:, k, :], start=k == 0, stop=k == KD - 1)
                        last.then_inc(down_ready, 1)
                    if j + 1 < NB // 2:
                        turn_tokens(g, j + 1, n + 2)
                    elif not last_four:
                        turn_tokens(g + 1, 0, n + 2)
                    for q in range(2):
                        pe.wait_ge(t_ready, ONE + NB + n + q + 1)
                        for s in range(SC):
                            for k in range(KD):
                                last = pe.transpose(p1[q][:, s, k * P:(k + 1) * P], T[q][:, k, s * P:(s + 1) * P], w.ident[:, :])
                        last.then_inc(back_ready, 1)

            turn_tokens(0, 0, 0)
            with pe.Fori(0, GTURNS // NB - 1) as g:
                four(g, False)
            four(GTURNS // NB - 1, True)

        @block.scalar
        def _(act):
            with act.Fori(0, GTURNS // NB) as g:
                for j in range(NB // 2):
                    n = g * NB + j * 2
                    for q in range(2):
                        act.wait_ge(up_ready, ONE + n + q + 1)
                        act.wait_ge(down_ready, ONE + n)
                        for f in range(KD):
                            last = act.activation(HH[q][:, f, :], p1[q][:, f, :], ACT.Silu, bias=bias(j * 2 + q, FIRST, f))
                        last.then_inc(silu_ready, 1)
                    for q in range(2):
                        act.wait_ge(y_ready, ONE + n + q + 1)
                        act.dma_start(w.ye_dram[bass.ds((n + q) * GT, GT), :].rearrange("(s p) n -> p s n", p=P), Y[q][:, :, :]).then_inc(stored[q], 16)
            for q in range(2):
                act.wait_ge(stored[q], ONE + 16 * (GTURNS // 2))

        @block.vector
        def _(dve):
            def keep_tokens(n):
                for q in range(2):
                    dve.wait_ge(turned, ONE + n + q + 1)
                    dve.wait_ge(up_ready, ONE + n)
                    dve.tensor_copy(XT[q][:, :, :], px[q][:, :, :]).then_inc(xT_ready, 1)

            def four(g, last_four):
                for j in range(NB // 2):
                    n = g * NB + j * 2
                    for q in range(2):
                        dve.wait_ge(third_ready, ONE + n + q + 1)
                        for f in range(KD):
                            last = dve.tensor_scalar(X3[q][:, f, :], p3[q][:, f, :], bias(j * 2 + q, THIRD, f), None, ALU.add)
                        last.then_inc(x3_ready, 1)
                    for q in range(2):
                        dve.wait_ge(down_ready, ONE + n + q + 1)
                        dve.wait_ge(x3_ready, ONE + n + q + 1)
                        dve.wait_ge(back_ready, ONE + n)
                        for f in range(KD):
                            last = dve.scalar_tensor_tensor(T[q][:, f, :], p2[q][:, f, :], bias(j * 2 + q, SECOND, f), X3[q][:, f, :], op0=ALU.add, op1=ALU.mult)
                        last.then_inc(t_ready, 1)
                    if j + 1 < NB // 2 or not last_four:
                        keep_tokens(n + 2)
                    for q in range(2):
                        dve.wait_ge(back_ready, ONE + n + q + 1)
                        dve.wait_ge(stored[q], ONE + g * (16 * (NB // 2)) + 16 * j)
                        dve.tensor_copy(Y[q][:, :, :], p1[q][:, :, :]).then_inc(y_ready, 1)

            keep_tokens(0)
            with dve.Fori(0, GTURNS // NB - 1) as g:
                four(g, False)
            four(GTURNS // NB - 1, True)


def stage_output(nc, w):
    with ExitStack() as ctx:
        sem = lambda name: semaphore(nc, ctx, name)
        staged, summed, scaled, added, stored = (sem(f"o_{n}") for n in ("staged", "summed", "scaled", "added", "stored"))
        got = [gpsimd_dma_semaphore(nc, ctx, f"o_got{q}") for q in range(4)]
        at = [sbuf(nc, ctx, f"o_at{q}", [P, 1, K1], I32) for q in range(4)]
        y = [sbuf(nc, ctx, f"o_y{q}", [P, K1, D]) for q in range(4)]
        t1 = [sbuf(nc, ctx, f"o_t{q}", [P, 1, D]) for q in range(4)]
        block = start(nc, ctx)

        @block.gpsimd
        def _(pool):
            with pool.Fori(0, NT // 4) as g:
                for q in range(4):
                    wait_alone(w, pool, staged, ONE + g * 4 + q + 1)
                    for k in range(K1):
                        pool.indirect_dma_start(out=y[q][:, k, :], out_offset=None, in_=w.ye_dram[:, :],
                                                in_offset=bass.IndirectOffsetOnAxis(ap=at[q][:, 0, k:k + 1], axis=0)).then_inc(got[q], 16)

        @block.vector
        def _(dve):
            def stage(t, q):
                dve.tensor_copy(at[q][:, :, :], w.slot2[:, bass.ds(t, 1), :]).then_inc(staged, 1)

            def turn(g, b, last):
                for q in range(4):
                    dve.wait_ge(got[q], 16 * K1 * g + 16 * K1)
                    dve.tensor_tensor(t1[q][:, :, :], y[q][:, 0:1, :], y[q][:, 1:2, :], ALU.add).then_inc(summed, 1)
                    dve.wait_ge(summed, ONE + g * 4 + q + 1)
                    if not last:
                        stage(g * 4 + q + 4, q)
                    dve.tensor_tensor(t1[q][:, :, :], t1[q][:, :, :], w.modrow[1][:, bass.ds(b, 1), GB * D:(GB + 1) * D], ALU.mult).then_inc(scaled, 1)
                    dve.wait_ge(scaled, ONE + g * 4 + q + 1)
                    xs = w.x[:, bass.ds(g * 4 + q, 1), :]
                    dve.tensor_tensor(xs, xs, t1[q][:, :, :], ALU.add).then_inc(added, 1)

            for q in range(4):
                stage(q, q)
            for b in range(B):
                last = b == B - 1
                with dve.Fori(b * (TB // 4), (b + 1) * (TB // 4) - (1 if last else 0)) as g:
                    turn(g, b, False)
            turn(NT // 4 - 1, B - 1, True)

        @block.sync
        def _(sp):
            with sp.Fori(0, NT // 4) as g:
                sp.wait_ge(added, ONE + g * 4 + 4)
                sp.dma_start(w.out[bass.ds(g * 4 * P, 4 * P), :].rearrange("(t p) n -> p t n", p=P), w.x[:, bass.ds(g * 4, 4), :]).then_inc(stored, 16)
            sp.wait_ge(stored, ONE + 16 * (NT // 4))




def clear_semaphores(nc):
    with nc.semaphore("first") as s:
        first = s.num
    numbers = [first]
    while True:
        with nc.semaphore("next") as s:
            if s.num == first:
                break
            numbers.append(s.num)
    nc.all_engine_barrier()
    nc.gpsimd.sem_clear(range(min(numbers), max(numbers) + 1))
    nc.all_engine_barrier()


def build(nc, a, out, stages=99):
    w = World()
    ctx = ExitStack()
    with ctx:
        w.passed = ctx.enter_context(nc.semaphore("passed"))
        w.band_stored = gpsimd_dma_semaphore(nc, ctx, "band_stored")
        w.keys_got = gpsimd_dma_semaphore(nc, ctx, "keys_got")
        w.SCALE = DH ** -0.5
        w.EXT = 2 * REL + 1 + 2 * (P - 1)
        w.c = [a['L0_c'], a['L1_c']]
        w.wmod = [a['L0_wmod'], a['L1_wmod']]
        w.rel_biasT = a['L0_attn_rel_bias']
        w.W_qkv0, w.W_out0, w.router_w = a['L0_attn_W_qkv'], a['L0_attn_W_out'], a['L0_ffn_router_w']
        w.b_qkv0, w.b_out0 = a['L0_attn_b_qkv'], a['L0_attn_b_out']
        w.x_dram = a['L0_attn_x'].rearrange("b s d -> (b s) d")
        w.a, w.out = a, out.rearrange("b s d -> (b s) d")
        dram = lambda name, shape, dt=F32: nc.dram_tensor(name, shape, dt).ap()
        w.ext_dram = dram("ext_dram", [NH, w.EXT])
        w.far_dram = dram("far_dram", [H, 2])
        w.qk_parts = [dram(f"{n}_parts", [3, NH * DH, S], BF16) for n in "qk"]
        w.attT_dram = dram("attT_dram", [NH, DH + 1, S])
        w.inverse_dram = dram("inverse_dram", [NH, S])
        w.BAND = 2 * REL + P
        w.skew_dram = dram("skew_dram", [NH, P * (w.EXT + 1)])
        w.xe_dram = dram("xe_dram", [E0 * CAP, D])
        w.ye_dram = dram("ye_dram", [E0 * CAP, D])
        w.x2_dram = dram("x2_dram", [B * S, D])
        w.w1_0, w.w2_0 = a['L0_ffn_w1'], a['L0_ffn_w2']
        w.packed = a['L1_ffn_packed']
        w.v_dram = dram("v_dram", [NH, S, DH])
        sb = lambda name, shape, dt=F32: sbuf(nc, ctx, name, shape, dt)
        w.index = sb("index", [P, B, U + UK], I32)
        w.ident = sb("ident", [P, P])
        w.zeros = sb("zeros", [P, 2048])
        w.eps = sb("eps", [P, 1])
        w.modrow = [sb(f"modrow{l}", [P, B, 6 * D]) for l in range(2)]
        w.modcol = sb("modcol", [P, 2, 12, B])
        w.far = sb("far", [P, NH, 2])
        w.Wout0 = sb("Wout0", [P, KD, D])
        w.Wr0 = sb("Wr0", [P, KD, 64])
        w.Wg1 = sb("Wg1", [P, KD, E1])
        w.bo0 = sb("bo0", [P, D])
        w.gbo0 = sb("gbo0", [P, B, D])
        w.x = sb("x", [P, NT, D])
        with ExitStack() as qkv:
            w.Wqkv0 = sbuf(nc, qkv, "Wqkv0", [P, KD, 3 * D])
            w.bqk = sbuf(nc, qkv, "bqk", [P, 2 * KD])
            w.bv0 = sbuf(nc, qkv, "bv0", [P, D])
            w.mean_var0 = sbuf(nc, qkv, "mean_var0", [P, NT, 2])
            w.rstd0 = sbuf(nc, qkv, "rstd0", [P, NT])
            stage_constants(nc, w)
            stage_qkv(nc, w)
        stage_attention(nc, w)
        stage_project(nc, w)
        w.mean_var = sb("mean_var", [P, NT, 2])
        w.rstd = sb("rstd", [P, NT])
        with ExitStack() as moe:
            w.gate4 = sbuf(nc, moe, "gate4", [P, NT, K0])
            w.put_at = sbuf(nc, moe, "put_at", [P, NT, K0], I32)
            w.get_from = sbuf(nc, moe, "get_from", [P, NT + 4, K0], I32)
            with ExitStack() as tokens:
                w.h = sbuf(nc, tokens, "h", [P, NT, D])
                w.logits0 = sbuf(nc, tokens, "logits0", [P, NT, E0])
                stage_norm(nc, w, w.x, NT, w.mean_var, w.rstd, "n0")
                stage_router(nc, w, w.x, w.mean_var, w.rstd, w.h, None, 0, w.Wr0, w.logits0, "g0")
                stage_route(nc, w)
                stage_scatter(nc, w)
            stage_experts(nc, w)
            stage_combine(nc, w)
        clear_semaphores(nc)
        with ExitStack() as att:
            w.xg = sbuf(nc, att, "xg", [P, B * (U + UK), D])
            w.att1 = sbuf(nc, att, "att1", [P, B * U, D])
            w.Wqkv1 = sbuf(nc, att, "Wqkv1", [P, KD, 3 * D])
            w.Wproj1 = sbuf(nc, att, "Wproj1", [P, KD, D])
            w.bqk1 = sbuf(nc, att, "bqk1", [P, 2 * KD])
            w.bv1 = sbuf(nc, att, "bv1", [P, D])
            w.bo1 = sbuf(nc, att, "bo1", [P, D])
            w.gbo1 = sbuf(nc, att, "gbo1", [P, B, D])
            w.own_square = sbuf(nc, att, "own_square", [P, P])
            w.own = sbuf(nc, att, "own", [P, P // NK])
            w.hk = sbuf(nc, att, "hk", [P, KD, B, UK * P])
            w.kT = sbuf(nc, att, "kT", [P, KD, B, U * 2 * NK])
            stage_gather(nc, w)
            stage_norm(nc, w, w.xg, B * (U + UK), w.mean_var, w.rstd, "n1")
            stage_keys(nc, w)
            w.vd = sbuf(nc, att, "vd", [P, B * U * 2, D])
            stage_values(nc, w)
            stage_blocks(nc, w)
            if stages == 5:
                return w
        w.hT1 = sb("hT1", [P, KD, B * S])
        w.gate2 = sb("gate2", [P, NT, K1])
        w.slot2 = sb("slot2", [P, NT, K1], I32)
        w.turn_row = sb("turn_row", [P, GTURNS], I32)
        with ExitStack() as tokens:
            w.h = sbuf(nc, tokens, "h1", [P, NT, D])
            w.shared = [sbuf(nc, tokens, "shared_W1", [P, KD, I1]), sbuf(nc, tokens, "shared_W2", [P, KD, I1]),
                        sbuf(nc, tokens, "shared_W3", [P, I1 // P, D])]
            w.logits1 = sbuf(nc, tokens, "logits1", [P, NT, E1])
            stage_norm(nc, w, w.x, NT, w.mean_var, w.rstd, "n2")
            stage_router(nc, w, w.x, w.mean_var, w.rstd, w.h, w.hT1, 1, w.Wg1, w.logits1, "g1")
            stage_places(nc, w)
            stage_shared(nc, w)
        stage_groups(nc, w)
        stage_output(nc, w)
    return w


_PLAIN = ['L0_attn_x', 'L0_attn_W_qkv', 'L0_attn_b_qkv', 'L0_attn_W_out', 'L0_attn_b_out', 'L0_ffn_router_w', 'L0_ffn_w1',
          'L0_ffn_w2', 'L0_wmod', 'L1_attn_Wqkv', 'L1_attn_bqkv', 'L1_attn_Wproj', 'L1_attn_bproj', 'L1_attn_mapping', 'L1_wmod']
_TURNED = ['L0_c', 'L1_c', 'L0_attn_rel_bias', 'L1_ffn_gate_w', 'L1_ffn_sw1', 'L1_ffn_sw2', 'L1_ffn_sw3']


def laid_out(inputs):
    arrays = {name: np.ascontiguousarray(np.asarray(inputs[name])) for name in _PLAIN}
    for name in _TURNED:
        arrays[name] = np.ascontiguousarray(np.swapaxes(np.asarray(inputs[name]), -1, -2))
    parts = []
    for i in (1, 3, 2):
        turned = np.swapaxes(np.asarray(inputs[f'L1_ffn_w{i}']), -1, -2).reshape(E1, KD, P, D)
        parts.append(turned.transpose(0, 2, 1, 3).reshape(E1 * P, KD * D))
    for i in (1, 3, 2):
        parts.append(np.asarray(inputs[f'L1_ffn_b{i}']).reshape(E1, KD, P).transpose(0, 2, 1).reshape(E1 * P, KD))
    arrays['L1_ffn_packed'] = np.ascontiguousarray(np.concatenate(parts, axis=1))
    return arrays


def kernel(**inputs):
    import concourse.bacc as _bacc
    from concourse import mybir as _mybir
    from concourse.bass_utils import run_bass_kernel_spmd as _run

    nc = _bacc.Bacc("TRN2", target_bir_lowering=False, num_devices=1)
    arrays, args = {}, {}
    for name, a in laid_out(inputs).items():
        arrays[f"in_{name}_dram"] = a
        args[name] = nc.dram_tensor(f"in_{name}_dram", a.shape, _mybir.dt.from_np(a.dtype), kind="ExternalInput").ap()
    out = nc.dram_tensor("out_dram", (B, S, D), _mybir.dt.from_np(np.dtype("float32")), kind="ExternalOutput").ap()
    build(nc, args, out)
    r = _run(nc, [arrays], core_ids=[0])
    return r.results[0]["out_dram"]
```
